# Optimizing a Trainium2 kernel written in Bass

```python
import numpy as np
import jax
import jax.numpy as jnp

def _softmax(x, axis=-1):
    return jax.nn.softmax(x, axis=axis)

def _gelu(x):
    return jax.nn.gelu(x, approximate=True)

def _silu(x):
    return jax.nn.silu(x)

def _sigmoid(x):
    return jax.nn.sigmoid(x)

def _layernorm(x, axis=-1, eps=1e-05):
    m = jnp.mean(x, axis=axis, keepdims=True)
    v = jnp.var(x, axis=axis, keepdims=True)
    return (x - m) / jnp.sqrt(v + eps)

def _scatter_add(tgt, idx, src, axis=0):
    return tgt.at[idx].add(src)

def _segment_sum(src, seg, n):
    return jax.ops.segment_sum(src, seg, n)
kernel_name = 'mk_audio_tower_d1_tok_audfeat768_r4_e9f6dd'

def setup_inputs(seed: int=0):
    np.random.seed(seed)
    _w = jnp.asarray

    def _rec_inputs():
        import jax
        import jax.numpy as jnp
        _rk = jax.random.key(seed)
        x = -0.000183583 + 0.999963 * jax.random.normal(jax.random.fold_in(_rk, 1), (8, 1024, 192), jnp.float32)
        return x
    x = _rec_inputs()

    def _L0_tok_setup():
        import jax, jax.numpy as jnp
        import numpy as np
        KEEP_RATIO = 0.7
        key = jax.random.key(seed)
        kx, kw = jax.random.split(key)
        B, N, D = (32, 1024, 192)
        x = jax.random.normal(kx, (B, N, D), dtype=jnp.float32)
        w = jax.random.normal(kw, (D, 1), dtype=jnp.float32) * (1.0 / np.sqrt(D))
        b = jnp.zeros((1,), dtype=jnp.float32)
        return {'x': x, 'w': w, 'b': b}
    _L0_tok_all = _L0_tok_setup()
    _L0_tok_in = {k: v for k, v in _L0_tok_all.items() if k in ('w', 'b')}
    del _L0_tok_all

    def _L0_attn_setup():
        import jax, jax.numpy as jnp
        import numpy as np
        H = 12
        BETA = 0.5
        LN_EPS = 1e-12

        def layer_norm(x, g, b):
            mu = x.mean(-1, keepdims=True)
            var = ((x - mu) ** 2).mean(-1, keepdims=True)
            return (x - mu) * jax.lax.rsqrt(var + LN_EPS) * g + b
        key = jax.random.key(seed)
        B, S, D, F, L = (16, 128, 192, 768, 4)
        ks = jax.random.split(key, 9)
        w = lambda k, shape: jax.random.normal(k, shape, jnp.float32) * 0.02
        return {'hidden_states': jax.random.normal(ks[0], (B, S, D), jnp.float32), 'Wq': w(ks[1], (L, D, D)), 'bq': jnp.zeros((L, D), jnp.float32), 'Wk': w(ks[2], (L, D, D)), 'bk': jnp.zeros((L, D), jnp.float32), 'Wv': w(ks[3], (L, D, D)), 'bv': jnp.zeros((L, D), jnp.float32), 'Wc': w(ks[4], (L, D, D)), 'bc': jnp.zeros((L, D), jnp.float32), 'Wo': w(ks[5], (L, D, D)), 'bo': jnp.zeros((L, D), jnp.float32), 'g1': jnp.ones((L, D), jnp.float32), 'b1': jnp.zeros((L, D), jnp.float32), 'Wi': w(ks[6], (L, D, F)), 'bi': jnp.zeros((L, F), jnp.float32), 'Wo2': w(ks[7], (L, F, D)), 'bo2': jnp.zeros((L, D), jnp.float32), 'g2': jnp.ones((L, D), jnp.float32), 'b2': jnp.zeros((L, D), jnp.float32)}
    _L0_attn_all = _L0_attn_setup()
    _L0_attn_in = {k: v for k, v in _L0_attn_all.items() if k in ('Wq', 'bq', 'Wk', 'bk', 'Wv', 'bv', 'Wc', 'bc', 'Wo', 'bo', 'g1', 'b1', 'Wi', 'bi', 'Wo2', 'bo2', 'g2', 'b2')}
    del _L0_attn_all

    def _L0_ffn_setup():
        import jax, jax.numpy as jnp
        import numpy as np
        H = 192
        R = 64
        E = 8
        B, S = (8, 512)
        key = jax.random.key(seed)
        ks = jax.random.split(key, 10)
        s_in = 1.0 / np.sqrt(H)
        s_r = 1.0 / np.sqrt(R)
        return {'x': jax.random.normal(ks[0], (B, S, H), dtype=jnp.float32), 'enc_w': jax.random.uniform(ks[1], (H, R), jnp.float32, -s_in, s_in), 'enc_b': jax.random.uniform(ks[2], (R,), jnp.float32, -s_in, s_in), 'sw_w': jax.random.uniform(ks[3], (R, E), jnp.float32, -s_r, s_r), 'sw_b': jax.random.uniform(ks[4], (E,), jnp.float32, -s_r, s_r), 'w1': jax.random.uniform(ks[5], (E, H, R), jnp.float32, -s_in, s_in), 'b1': jax.random.uniform(ks[6], (E, R), jnp.float32, -s_in, s_in), 'w2': jax.random.uniform(ks[7], (E, R, H), jnp.float32, -s_r, s_r), 'b2': jax.random.uniform(ks[8], (E, H), jnp.float32, -s_r, s_r)}
    _L0_ffn_all = _L0_ffn_setup()
    _L0_ffn_in = {k: v for k, v in _L0_ffn_all.items() if k in ('enc_w', 'enc_b', 'sw_w', 'sw_b', 'w1', 'b1', 'w2', 'b2')}
    del _L0_ffn_all
    return {'x': x, 'L0_tok_w': _L0_tok_in['w'], 'L0_tok_b': _L0_tok_in['b'], 'L0_attn_Wq': _L0_attn_in['Wq'], 'L0_attn_bq': _L0_attn_in['bq'], 'L0_attn_Wk': _L0_attn_in['Wk'], 'L0_attn_bk': _L0_attn_in['bk'], 'L0_attn_Wv': _L0_attn_in['Wv'], 'L0_attn_bv': _L0_attn_in['bv'], 'L0_attn_Wc': _L0_attn_in['Wc'], 'L0_attn_bc': _L0_attn_in['bc'], 'L0_attn_Wo': _L0_attn_in['Wo'], 'L0_attn_bo': _L0_attn_in['bo'], 'L0_attn_g1': _L0_attn_in['g1'], 'L0_attn_b1': _L0_attn_in['b1'], 'L0_attn_Wi': _L0_attn_in['Wi'], 'L0_attn_bi': _L0_attn_in['bi'], 'L0_attn_Wo2': _L0_attn_in['Wo2'], 'L0_attn_bo2': _L0_attn_in['bo2'], 'L0_attn_g2': _L0_attn_in['g2'], 'L0_attn_b2': _L0_attn_in['b2'], 'L0_ffn_enc_w': _L0_ffn_in['enc_w'], 'L0_ffn_enc_b': _L0_ffn_in['enc_b'], 'L0_ffn_sw_w': _L0_ffn_in['sw_w'], 'L0_ffn_sw_b': _L0_ffn_in['sw_b'], 'L0_ffn_w1': _L0_ffn_in['w1'], 'L0_ffn_b1': _L0_ffn_in['b1'], 'L0_ffn_w2': _L0_ffn_in['w2'], 'L0_ffn_b2': _L0_ffn_in['b2']}

def reference(x, L0_tok_w, L0_tok_b, L0_attn_Wq, L0_attn_bq, L0_attn_Wk, L0_attn_bk, L0_attn_Wv, L0_attn_bv, L0_attn_Wc, L0_attn_bc, L0_attn_Wo, L0_attn_bo, L0_attn_g1, L0_attn_b1, L0_attn_Wi, L0_attn_bi, L0_attn_Wo2, L0_attn_bo2, L0_attn_g2, L0_attn_b2, L0_ffn_enc_w, L0_ffn_enc_b, L0_ffn_sw_w, L0_ffn_sw_b, L0_ffn_w1, L0_ffn_b1, L0_ffn_w2, L0_ffn_b2):
    import jax
    import jax.numpy as jnp

    def _L0_tok_ref(x, w, b):
        import jax, jax.numpy as jnp
        import numpy as np
        KEEP_RATIO = 0.7
        scores = jnp.einsum('bnd,do->bn', x, w) + b[0]
        N = x.shape[1]
        k = int(round(N * KEEP_RATIO))
        _, idx = jax.lax.top_k(scores, k)
        return jnp.take_along_axis(x, idx[:, :, None], axis=1)

    def _L0_attn_ref(hidden_states, Wq, bq, Wk, bk, Wv, bv, Wc, bc, Wo, bo, g1, b1, Wi, bi, Wo2, bo2, g2, b2):
        import jax, jax.numpy as jnp
        import numpy as np
        H = 12
        BETA = 0.5
        LN_EPS = 1e-12

        def layer_norm(x, g, b):
            mu = x.mean(-1, keepdims=True)
            var = ((x - mu) ** 2).mean(-1, keepdims=True)
            return (x - mu) * jax.lax.rsqrt(var + LN_EPS) * g + b
        B, S, D = hidden_states.shape
        Dh = D // H
        L = Wq.shape[0]
        eye = jnp.eye(S, dtype=hidden_states.dtype)
        scale = 1.0 / np.sqrt(Dh).astype(np.float32)

        def heads(t):
            return t.reshape(B, S, H, Dh).transpose(0, 2, 1, 3)
        x = hidden_states
        for i in range(L):
            q = heads(x @ Wq[i] + bq[i])
            k = heads(x @ Wk[i] + bk[i])
            v = heads(x @ Wv[i] + bv[i])
            c = heads(x @ Wc[i] + bc[i])
            cn = jnp.linalg.norm(c, axis=-1, keepdims=True)
            denom = cn * jnp.swapaxes(cn, -1, -2)
            s1 = 1.0 - jnp.einsum('bhld,bhrd->bhlr', c, c) / denom + eye
            p1 = jax.nn.softmax(s1, axis=-1)
            s2 = jnp.einsum('bhld,bhrd->bhlr', q, k) * scale
            p2 = jax.nn.softmax(s2, axis=-1)
            p = BETA * p1 + (1.0 - BETA) * p2
            ctx = jnp.einsum('bhlr,bhrd->bhld', p, v)
            ctx = ctx.transpose(0, 2, 1, 3).reshape(B, S, D)
            attn_out = layer_norm(ctx @ Wo[i] + bo[i] + x, g1[i], b1[i])
            h = jax.nn.gelu(attn_out @ Wi[i] + bi[i], approximate=False)
            x = layer_norm(h @ Wo2[i] + bo2[i] + attn_out, g2[i], b2[i])
        return x

    def _L0_ffn_ref(x, enc_w, enc_b, sw_w, sw_b, w1, b1, w2, b2):
        import jax, jax.numpy as jnp
        import numpy as np
        H = 192
        R = 64
        E = 8
        B, S = (8, 512)
        b, s, d = x.shape
        xt = x.reshape(-1, d)
        x_enc = xt @ enc_w + enc_b
        route_prob = jax.nn.softmax(x_enc @ sw_w + sw_b, axis=-1)
        route_prob_max = jnp.max(route_prob, axis=-1)
        routes = jnp.argmax(route_prob, axis=-1)
        onehot = jax.nn.one_hot(routes, E, dtype=xt.dtype)
        h = jnp.einsum('td,edr->ter', xt, w1) + b1[None]
        h = jax.nn.gelu(h, approximate=False)
        h = h * onehot[..., None]
        out = jnp.einsum('ter,erd->td', h, w2) + onehot @ b2
        out = out * route_prob_max[:, None]
        return out.reshape(b, s, d)
    h = _L0_tok_ref(x, L0_tok_w, L0_tok_b)
    h = h + _L0_attn_ref(_layernorm(h, axis=-1), L0_attn_Wq, L0_attn_bq, L0_attn_Wk, L0_attn_bk, L0_attn_Wv, L0_attn_bv, L0_attn_Wc, L0_attn_bc, L0_attn_Wo, L0_attn_bo, L0_attn_g1, L0_attn_b1, L0_attn_Wi, L0_attn_bi, L0_attn_Wo2, L0_attn_bo2, L0_attn_g2, L0_attn_b2)
    h = h + _L0_ffn_ref(_layernorm(h, axis=-1), L0_ffn_enc_w, L0_ffn_enc_b, L0_ffn_sw_w, L0_ffn_sw_b, L0_ffn_w1, L0_ffn_b1, L0_ffn_w2, L0_ffn_b2)
    return h

_drawn_inputs = setup_inputs


def setup_inputs(seed=0):
    import zlib

    import numpy as np

    out = dict(_drawn_inputs(seed))
    spreads = {'L0_attn_bq': (0.0, 0.8),
     'L0_attn_bk': (0.0, 2.0),
     'L0_attn_bv': (0.0, 0.273),
     'L0_attn_bc': (0.0, 2.0),
     'L0_attn_bo': (0.0, 0.1),
     'L0_attn_g1': (1.0, 0.2),
     'L0_attn_b1': (0.0, 0.1),
     'L0_attn_bi': (0.0, 0.1),
     'L0_attn_bo2': (0.0, 0.1),
     'L0_attn_g2': (1.0, 0.2),
     'L0_attn_b2': (0.0, 0.1)}
    factors = {'L0_attn_Wq': 8.0,
     'L0_attn_Wk': 8.0,
     'L0_attn_Wv': 3.049,
     'L0_attn_Wc': 63.456,
     'L0_ffn_enc_w': 2.84,
     'L0_ffn_enc_b': 8.0,
     'L0_ffn_sw_w': 2.857,
     'L0_ffn_sw_b': 4.923,
     'L0_ffn_w1': 3.06,
     'L0_ffn_b1': 8.0,
     'L0_ffn_w2': 2.866,
     'L0_ffn_b2': 7.991}
    for name, (base, spread) in spreads.items():
        noise = np.random.default_rng([zlib.crc32(name.encode()), seed]).standard_normal(out[name].shape)
        drawn = base * np.exp(spread * noise) if base else spread * noise
        out[name] = jnp.asarray(drawn.astype(out[name].dtype))
    for name, factor in factors.items():
        out[name] = (out[name] * factor).astype(out[name].dtype)
    return out
```

```python
from contextlib import ExitStack

import concourse.bass as bass
from concourse import mybir

ALU = mybir.AluOpType
ACT = mybir.ActivationFunctionType
F32 = mybir.dt.float32
BF16 = mybir.dt.bfloat16
I32 = mybir.dt.int32
AX = mybir.AxisListType

B, N, D = 8, 1024, 192
KEEP = int(round(N * 0.7))
L, H, DH = 4, 12, 16
F = 768
R, E = 64, 8
LN_EPS, BLOCK_EPS = 1e-5, 1e-12

T = 6
P = 120
S = T * P
HALF = S // 2
MT = 2
DM = D // MT
FM = F // 128
XT = N // 128
GROUPS, GH = 3, 4
SPANS = GROUPS * 2
STEPS = L * B
SLOTS = STEPS + B + 1
Q_PARTS = (0, 0, 0, 1, 1, 2)
K_PARTS = (0, 1, 2, 0, 1, 0)
KQ = len(Q_PARTS) * DH
ROWS = KQ + 3
MAX_TILES = H * T * 2
MAX_PER_TILE = 5
HIDDEN_AT = (0, 3, 5)
LAST = (KEEP - 1) // T
FULL = KEEP - LAST * T


def kept(t):
    return P if t < FULL else LAST


class Tally:

    def __init__(self, sem, before=0):
        self.sem, self.before, self.count = sem, before, 0

    def add(self, instruction, by=1):
        instruction.then_inc(self.sem, by)
        self.count += by
        return self.before + self.count

    def now(self):
        return self.before + self.count


def max_tile_at(gh, kt, i):
    n = ((gh - 1) * T + kt) * MAX_PER_TILE + i
    return n if gh and n < MAX_TILES else None


def hidden_at(gh, kt):
    return ((gh - 2) * len(HIDDEN_AT) + HIDDEN_AT.index(kt)) if gh >= 2 and kt in HIDDEN_AT else None


class Ring:

    def __init__(self, before=0):
        self.before, self.count = before, 0

    def take(self):
        k = self.count
        self.count += 1
        return k % 2, self.before + k + 1


def combine_stats(nc, dve, done, stats, mean_var, spread, width):
    def link(instruction):
        dve.wait_ge(done.sem, done.add(instruction))

    link(nc.vector.tensor_tensor(spread[:], stats[:, :, 1], stats[:, :, 4], ALU.subtract))
    link(nc.vector.tensor_tensor(spread[:], spread[:], spread[:], ALU.mult))
    link(nc.vector.tensor_tensor(mean_var[:, :, 0], stats[:, :, 1], stats[:, :, 4], ALU.add))
    link(nc.vector.tensor_scalar(mean_var[:, :, 0], mean_var[:, :, 0], 0.5, None, ALU.mult))
    link(nc.vector.tensor_tensor(mean_var[:, :, 1], stats[:, :, 2], stats[:, :, 5], ALU.add))
    link(nc.vector.tensor_scalar(mean_var[:, :, 1], mean_var[:, :, 1], 1.0 / width, None, ALU.mult))
    return nc.vector.scalar_tensor_tensor(out=mean_var[:, :, 1], in0=spread[:], scalar=0.25,
                                          in1=mean_var[:, :, 1], op0=ALU.mult, op1=ALU.add)


def sort_tokens(nc, x, tok_w, tok_b, scores_d, sorted_d, state_d):
    with ExitStack() as ctx:
        sb = lambda name, shape, dt=F32: ctx.enter_context(nc.sbuf_tensor("so_" + name, shape, dt))
        sem = lambda name: ctx.enter_context(nc.semaphore("so_" + name))
        x_all = sb("x", [128, B * XT, D])
        prod = sb("prod", [128, B * XT, D])
        w_bc = sb("w", [128, D])
        b_bc = sb("b", [128, 1])
        score = sb("score", [128, B * XT])
        score_row = sb("score_row", [128, B * N])
        scoreT = sb("scoreT", [B * XT, 128])
        junk = sb("junk", [128, N])
        before = sb("before", [128, 128])
        counts = sb("counts", [128, XT, 3])
        rank = sb("rank", [128, XT])
        first_row = sb("first_row", [128, B * XT])
        place = sb("place", [128, B * XT], I32)
        ident = sb("ident", [128, 128])
        kept_x = sb("kept", [P, B, T * D])
        stats = sb("stats", [P, T, 6])
        mean_var = sb("mean_var", [P, T, 2])
        mean_gap = sb("mean_gap", [P, T])
        eps = sb("eps", [P, T])
        rstd = sb("rstd", [P, T])
        minus_half = sb("minus_half", [P, T])
        turned = ctx.enter_context(nc.psum_tensor("so_turned", [128, 128], F32))

        consts = sem("consts")
        x_loaded = sem("x_loaded")
        scored = sem("scored")
        turned_done = sem("turned")
        row_ready = sem("row_ready")
        row_stored = sem("row_stored")
        row_loaded = sem("row_loaded")
        vec = sem("vec")
        ranked = sem("ranked")
        scattered = [sem(f"scattered{b}") for b in range(B)]
        kept_loaded = [sem(f"kept{b}") for b in range(2)]
        moments = sem("moments")
        rstd_ready = sem("rstd_ready")
        pool = sem("pool")
        normed = sem("normed")
        stored = sem("stored")

        block = ctx.enter_context(nc.Block())
        RANK_OPS = 3 * XT
        NORM_OPS = T + 6

        @block.sync
        def _(sp):
            sp.dma_start(w_bc[:], tok_w.rearrange("d o -> (o d)").partition_broadcast(128)).then_inc(x_loaded, 16)
            sp.dma_start(b_bc[:], tok_b.partition_broadcast(128)).then_inc(x_loaded, 16)
            for b in range(B):
                sp.dma_start(x_all[:, b * XT:(b + 1) * XT, :],
                             x[b].rearrange("(t p) d -> p t d", p=128)).then_inc(x_loaded, 16)
            sp.wait_ge(row_ready, 1)
            sp.dma_start(scores_d, scoreT[:]).then_inc(row_stored, 16)
            sp.wait_ge(row_stored, 16)
            sp.dma_start(score_row[:], scores_d.rearrange("a b -> (a b)").partition_broadcast(128)).then_inc(row_loaded, 16)
            for b in range(B):
                sp.wait_ge(scattered[b], 16 * XT)
                if b >= 2:
                    sp.wait_ge(kept_loaded[b % 2], 16 * (b // 2))
                sp.dma_start(kept_x[:, b, :], sorted_d[b * N:b * N + S].rearrange("(p t) d -> p (t d)", t=T)
                             ).then_inc(kept_loaded[b % 2], 16)
            for b in range(B):
                sp.wait_ge(normed, T * (b + 1))
                sp.dma_start(state_d[STEPS + b].rearrange("(p t) d -> p (t d)", t=T), kept_x[:, b, :]).then_inc(stored, 16)
            sp.wait_ge(stored, 16 * B)

        @block.gpsimd
        def _(pool_e):
            nc.gpsimd.memset(ident[:], 0.0).then_inc(pool, 1)
            nc.gpsimd.memset(before[:], 1.0).then_inc(pool, 1)
            nc.gpsimd.memset(minus_half[:], -0.5).then_inc(consts, 1)
            nc.gpsimd.memset(eps[:], LN_EPS).then_inc(pool, 1)
            for b in range(B):
                nc.gpsimd.memset(first_row[:, b * XT:(b + 1) * XT], float(b * N)).then_inc(consts, 1)
            pool_e.wait_ge(pool, 3)
            nc.gpsimd.affine_select(out=ident[:], in_=ident[:], compare_op=ALU.not_equal, fill=1.0, base=0,
                                    pattern=[[-1, 128]], channel_multiplier=1).then_inc(consts, 1)
            nc.gpsimd.affine_select(out=before[:], in_=before[:], compare_op=ALU.is_gt, fill=0.0, base=0,
                                    pattern=[[-1, 128]], channel_multiplier=1).then_inc(consts, 1)
            for b in range(B):
                pool_e.wait_ge(ranked, b + 1)
                for t in range(XT):
                    k = b * XT + t
                    nc.gpsimd.indirect_dma_start(
                        out=sorted_d, out_offset=bass.IndirectOffsetOnAxis(ap=place[:, k:k + 1], axis=0),
                        in_=x_all[:, k, :], in_offset=None).then_inc(scattered[b], 16)
            for b in range(B):
                pool_e.wait_ge(moments, b + 1)
                nc.gpsimd.tensor_tensor(rstd[:], mean_var[:, :, 1], eps[:], ALU.add).then_inc(pool, 1)
                pool_e.wait_ge(pool, 4 + b)
                nc.gpsimd.tensor_tensor(rstd[:], rstd[:], minus_half[:], ALU.pow).then_inc(rstd_ready, 1)

        @block.tensor
        def _(pe):
            pe.wait_ge(scored, 1)
            pe.wait_ge(consts, B + 3)
            nc.tensor.transpose(turned[0:B * XT, :], score[:], ident[:]).then_inc(turned_done, 1)

        @block.vector
        def _(dve):
            dve.wait_ge(x_loaded, 16 * (B + 2))
            nc.vector.memset(counts[:], 0.0).then_inc(vec, 1)
            nc.vector.tensor_tensor(prod[:], x_all[:], w_bc[:, None, :].broadcast_to([128, B * XT, D]),
                                    ALU.mult).then_inc(vec, 1)
            dve.wait_ge(vec, 2)
            nc.vector.tensor_reduce(score[:], prod[:], AX.X, ALU.add).then_inc(vec, 1)
            dve.wait_ge(vec, 3)
            nc.vector.tensor_scalar(score[:], score[:], b_bc[:, 0:1], None, ALU.add).then_inc(scored, 1)
            dve.wait_ge(turned_done, 1)
            nc.vector.tensor_copy(scoreT[:], turned[0:B * XT, :]).then_inc(row_ready, 1)
            dve.wait_ge(row_loaded, 16)
            dve.wait_ge(consts, B + 3)
            dve.wait_ge(scored, 1)
            with dve.Fori(0, B) as b:
                done = Tally(vec, b * RANK_OPS + 3)
                row = b * N
                for t in range(XT):
                    s = score[:, bass.ds(b * XT + t, 1)]
                    if t:
                        done.add(nc.vector.tensor_scalar(junk[:, 0:128 * t], score_row[:, bass.ds(row, 128 * t)], s, 0.0,
                                                         ALU.is_ge, ALU.add, accum_out=counts[:, t, 0:1]))
                        dve.wait_ge(vec, done.now())
                    done.add(nc.vector.tensor_scalar(junk[:, 0:N - 128 * t],
                                                     score_row[:, bass.ds(row + 128 * t, N - 128 * t)], s, 0.0,
                                                     ALU.is_gt, ALU.add, accum_out=counts[:, t, 1:2]))
                    dve.wait_ge(vec, done.now())
                    done.add(nc.vector.scalar_tensor_tensor(
                        out=junk[:, 0:128], in0=score_row[:, bass.ds(row + 128 * t, 128)], scalar=s, in1=before[:],
                        op0=ALU.is_equal, op1=ALU.mult, accum_out=counts[:, t, 2:3]))
                    dve.wait_ge(vec, done.now())
                done.add(nc.vector.tensor_reduce(rank[:], counts[:], AX.X, ALU.add))
                dve.wait_ge(vec, done.now())
                nc.vector.tensor_tensor(place[:, bass.ds(b * XT, XT)], rank[:], first_row[:, bass.ds(b * XT, XT)],
                                        ALU.add).then_inc(ranked, 1)
                dve.wait_ge(ranked, b + 1)
                assert done.count == RANK_OPS
            ranks_done = 3 + B * RANK_OPS
            for b in range(B):
                dve.wait_ge(kept_loaded[b % 2], 16 * (b // 2 + 1))
                done = Tally(vec, ranks_done + NORM_OPS * b)
                for t in range(T):
                    done.add(nc.vector.bn_stats(stats[:, t, :], kept_x[:, b, t * D:(t + 1) * D]))
                dve.wait_ge(vec, done.now())
                combine_stats(nc, dve, done, stats, mean_var, mean_gap, D).then_inc(moments, 1)
                dve.wait_ge(moments, b + 1)
                dve.wait_ge(rstd_ready, b + 1)
                for t in range(T):
                    xt = kept_x[:, b, t * D:(t + 1) * D]
                    nc.vector.tensor_scalar(xt, xt, mean_var[:, t, 0:1], rstd[:, t:t + 1],
                                            ALU.subtract, ALU.mult).then_inc(normed, 1)
                dve.wait_ge(normed, T * (b + 1))


COS, DOT = 0, 1
SPAN_UNITS = T * 2
STEP_UNITS = 2 * SPANS * SPAN_UNITS
STEP_TILES = 2 * SPANS * T
STEP_SPANS = 2 * SPANS
PRO_JOBS = 4 + T + 4 + 4 + 4
TAIL_JOBS = 4 + 3 + 4 + FM * 2 + 3
STEP_JOBS = PRO_JOBS + TAIL_JOBS + STEP_SPANS + MAX_TILES + 2
COS_JOBS = 4 + 3 + 4 + 2 * FM + SPANS + MAX_TILES
TURNED_MAX_JOBS = COS_JOBS + 2
DOT_JOBS = TURNED_MAX_JOBS + 4 + T + 1 + 3
UNIT_CREDIT, TILE_CREDIT, BANK_CREDIT = 2, 3, 2
VEC_PRO, VEC_STEP = 18, 57
N_PROJ, N_FFN = 9, 13
assert STEP_JOBS % 2 == 0 and PRO_JOBS % 2 == 0


def layers(nc, w, parts_d, state_d):
    with ExitStack() as ctx:
        sb = lambda name, shape, dt=F32: ctx.enter_context(nc.sbuf_tensor("la_" + name, shape, dt))
        sem = lambda name: ctx.enter_context(nc.semaphore("la_" + name))
        q_stack = sb("q_stack", [ROWS, H, S], BF16)
        k_stack = sb("k_stack", [ROWS, H, S], BF16)
        c_stack = sb("c_stack", [KQ, H, S], BF16)
        d_stack = sb("d_stack", [KQ, H, S], BF16)
        prob = sb("prob", [P, 3, GH, HALF])
        x_in = sb("x_in", [P, T, D])
        resid = sb("resid", [P, T, D])
        x1 = sb("x1", [P, T, D])
        xT = sb("xT", [DM, MT, S])
        featT = sb("featT", [DM, MT, S])
        ctxt = sb("ctx", [P, T, D])
        partial = sb("partial", [P, 3, GH * DH])
        hid = sb("hid", [128, FM, S])
        c_tok = sb("c_tok", [P, T, D])
        v_next = sb("v_next", [P, T, D])
        v_aug = sb("v_aug", [P, T, H, 32])
        o_sb = sb("o_sb", [128, HALF])
        opT = sb("opT", [128, MT * S])
        part = [sb(f"part{i}", [DM, MT, S], BF16) for i in range(3)]
        wq, wk, wo = (sb(n, [DM, MT, D]) for n in ("wq", "wk", "wo"))
        wcv = sb("wcv", [DM, MT, 2 * D])
        wi = sb("wi", [DM, MT, F])
        wo2 = sb("wo2", [128, FM, D])
        bcv = sb("bcv", [P, 2 * D])
        bq_col, bk_col, g1_col, b1_col = (sb(n, [DM, MT]) for n in ("bq_col", "bk_col", "g1_col", "b1_col"))
        bi_col = sb("bi_col", [128, FM])
        bo, g1, b1, bo2, g2, b2 = (sb(n, [P, D]) for n in ("bo", "g1", "b1", "bo2", "g2", "b2"))
        ident = sb("ident", [128, 128])
        ident16 = sb("ident16", [128, 128], BF16)
        minus_ident = sb("minus_ident", [128, 128], BF16)
        minus_half = sb("minus_half", [P, T * H])
        neg_max = sb("neg_max", [P, 2, T * H])
        max_part = sb("max_part", [P, T + 1, 3, H], BF16)
        maxT = sb("maxT", [3 * H, S], BF16)
        recip = sb("recip", [P, 3, GH])
        stats = sb("stats", [P, T, 6])
        mean_var = sb("mean_var", [P, T, 2])
        mean_gap = sb("mean_gap", [P, T])
        eps = sb("eps", [P, T])
        rstd = sb("rstd", [P, T])
        c_norm = sb("c_norm", [P, T * H])

        score_ps = ctx.enter_context(nc.psum_tensor("la_score", [128, GH, 512], F32))
        out_ps = ctx.enter_context(nc.psum_tensor("la_out", [128, 2, 512], F32))
        job_ps = ctx.enter_context(nc.psum_tensor("la_job", [128, 2, 512], F32))
        job16 = job_ps[:, :, :].bitcast(BF16)

        consts = sem("consts")
        proj_loaded = sem("proj_loaded")
        ffn_loaded = sem("ffn_loaded")
        qk_loaded = sem("qk_loaded")
        c_loaded = sem("c_loaded")
        m_loaded = sem("m_loaded")
        parts_stored = sem("parts_stored")
        x_stored = sem("x_stored")
        scores_ready = sem("scores_ready")
        exp_done = sem("exp_done")
        pv_done = sem("pv_done")
        o_copied = sem("o_copied")
        bank_full = sem("bank_full")
        bank_free = sem("bank_free")
        vec = sem("vec")
        v_ready = sem("v_ready")
        parts_ready = sem("parts_ready")
        max_ready = sem("max_ready")
        moments1 = sem("moments1")
        moments2 = sem("moments2")
        rstd1 = sem("rstd1")
        rstd2 = sem("rstd2")
        normed1 = sem("normed1")
        normed2 = sem("normed2")
        resid_in = sem("resid_in")
        resid_mid = sem("resid_mid")
        x_out = sem("x_out")
        ctx_ready = sem("ctx_ready")
        squares = sem("squares")
        c_norm_ready = sem("c_norm_ready")
        c_unit = sem("c_unit")
        gelu_done = sem("gelu_done")
        pool = sem("pool")

        block = ctx.enter_context(nc.Block())

        def slot_of_input(n):
            return (n + STEPS) % (STEPS + B)

        def slot_of_output(n):
            return (n + SLOTS - 1) % SLOTS

        def job_base(n):
            return n * STEP_JOBS + PRO_JOBS

        @block.sync
        def _(sp):
            def load_projection(layer, slot):
                y = layer
                for dst, src in (
                        (wq[:], w["Wq"][y].rearrange("a (k p) n -> p (a k) n", p=DM)),
                        (wk[:], w["Wk"][y].rearrange("a (k p) n -> p (a k) n", p=DM)),
                        (wcv[:, :, 0:D], w["Wc"][y].rearrange("a (k p) n -> p (a k) n", p=DM)),
                        (wcv[:, :, D:2 * D], w["Wv"][y].rearrange("a (k p) n -> p (a k) n", p=DM)),
                        (bcv[:, 0:D], w["bc"][y].rearrange("a d -> (a d)").partition_broadcast(P)),
                        (bcv[:, D:2 * D], w["bv"][y].rearrange("a d -> (a d)").partition_broadcast(P)),
                        (bq_col[:], w["bq"][y].rearrange("a (k p) -> p (a k)", p=DM)),
                        (bk_col[:], w["bk"][y].rearrange("a (k p) -> p (a k)", p=DM)),
                        (x_in[:], state_d[slot].rearrange("a (p t) d -> p (a t) d", t=T))):
                    sp.dma_start(dst, src, allow_slow_non_contiguous=True).then_inc(proj_loaded, 16)

            def load_mlp(layer, slot):
                y = layer
                for dst, src in (
                        (wo[:], w["Wo"][y].rearrange("a (k p) n -> p (a k) n", p=DM)),
                        (wi[:], w["Wi"][y].rearrange("a (k p) n -> p (a k) n", p=DM)),
                        (wo2[:], w["Wo2"][y].rearrange("a (k p) n -> p (a k) n", p=128)),
                        *((tile[:], w[name][y].rearrange("a d -> (a d)").partition_broadcast(P))
                          for tile, name in ((bo, "bo"), (g1, "g1"), (b1, "b1"), (bo2, "bo2"), (g2, "g2"), (b2, "b2"))),
                        (g1_col[:], w["g1"][y].rearrange("a (k p) -> p (a k)", p=DM)),
                        (b1_col[:], w["b1"][y].rearrange("a (k p) -> p (a k)", p=DM)),
                        (bi_col[:], w["bi"][y].rearrange("a (k p) -> p (a k)", p=128)),
                        (resid[:], state_d[slot].rearrange("a (p t) d -> p (a t) d", t=T))):
                    sp.dma_start(dst, src, allow_slow_non_contiguous=True).then_inc(ffn_loaded, 16)

            def store_parts(operand, count):
                sp.wait_ge(parts_ready, count)
                for i in range(3):
                    sp.dma_start(parts_d[operand, i].rearrange("(m p) s -> p m s", p=DM),
                                 part[i][:]).then_inc(parts_stored, 16)

            def load_stack(stack, operand, order, loaded):
                for i, p in enumerate(order):
                    sp.dma_start(stack[i * DH:(i + 1) * DH, :, :],
                                 parts_d[operand, p].rearrange("(h d) s -> d h s", d=DH)).then_inc(loaded, 16)

            load_projection(bass.ds(0, 1), bass.ds(STEPS, 1))
            load_mlp(bass.ds(0, 1), bass.ds(STEPS, 1))
            store_parts(0, 1)
            store_parts(1, 2)
            sp.wait_ge(parts_stored, 16 * 6)
            load_stack(c_stack, 1, Q_PARTS, c_loaded)
            load_stack(d_stack, 1, K_PARTS, c_loaded)
            store_parts(2, 3)
            with sp.Fori(0, STEPS) as n:
                sp.wait_ge(pv_done, n * STEP_TILES + TILE_CREDIT)
                sp.wait_ge(parts_stored, 16 * 9 * (n + 1))
                load_stack(q_stack, 0, Q_PARTS, qk_loaded)
                load_stack(k_stack, 2, K_PARTS, qk_loaded)
                sp.wait_ge(x_stored, 16 * n + 1)
                sp.wait_ge(bank_free, job_base(n) + BANK_CREDIT)
                load_projection(bass.ds(((n + 1) // B) % L, 1), bass.ds(slot_of_input(n + 1), 1))
                sp.wait_ge(bank_free, job_base(n) + TURNED_MAX_JOBS + BANK_CREDIT)
                for i in range(3):
                    sp.dma_start(q_stack[KQ + i:KQ + i + 1, :, :], maxT[i * H:(i + 1) * H, :]).then_inc(m_loaded, 16)
                store_parts(0, 3 * n + 4)
                store_parts(1, 3 * n + 5)
                sp.wait_ge(scores_ready, n * STEP_UNITS + STEP_UNITS // 2)
                sp.wait_ge(parts_stored, 16 * (9 * n + 15))
                load_stack(c_stack, 1, Q_PARTS, c_loaded)
                load_stack(d_stack, 1, K_PARTS, c_loaded)
                sp.wait_ge(x_out, n + 1)
                sp.dma_start(state_d[bass.ds(slot_of_output(n), 1)].rearrange("a (p t) d -> p (a t) d", t=T),
                             x1[:]).then_inc(x_stored, 16)
                sp.wait_ge(bank_free, job_base(n) + DOT_JOBS + BANK_CREDIT)
                load_mlp(bass.ds(n // B, 1), bass.ds(slot_of_input(n), 1))
                store_parts(2, 3 * n + 6)
            sp.wait_ge(x_out, STEPS + 1)
            sp.dma_start(state_d[STEPS - 1].rearrange("(p t) d -> p t d", t=T), x1[:]).then_inc(x_stored, 16)
            sp.wait_ge(x_stored, 16 * (STEPS + 1) + 1)
            sp.wait_ge(parts_stored, 16 * 9 * (STEPS + 1))
            sp.wait_ge(c_loaded, 16 * 12 * (STEPS + 1))
            sp.wait_ge(proj_loaded, 16 * N_PROJ * (STEPS + 1))

        @block.tensor
        def _(pe):
            def mm(out, a, b, start=True, stop=True):
                return nc.tensor.matmul(out, a, b, start=start, stop=stop)

            def take(ring):
                bank, use = ring.take()
                pe.wait_ge(bank_free, use - 2 + BANK_CREDIT)
                return bank

            def turn_features(ring, src):
                for m in range(MT):
                    for half in range(2):
                        bank = take(ring)
                        for t in range(3):
                            last = nc.tensor.transpose(job_ps[0:DM, bank, t * P:(t + 1) * P],
                                                       src[:, half * 3 + t, m * DM:(m + 1) * DM], ident[0:P, 0:P])
                        last.then_inc(bank_full, 1)

            def project_cv(ring, n):
                for t in range(T):
                    bank = take(ring)
                    if t == 0:
                        pe.wait_ge(bank_free, ring.before + ring.count - 1 + BANK_CREDIT)
                    for k in range(MT):
                        last = mm(job_ps[0:P, bank, 0:2 * D], xT[:, k, t * P:(t + 1) * P], wcv[:, k, :], k == 0, k == 1)
                    last.then_inc(bank_full, 1)

            def project_t(ring, weights, m):
                for half in range(2):
                    bank = take(ring)
                    for k in range(MT):
                        last = mm(job_ps[0:DM, bank, 0:HALF], weights[:, k, m * DM:(m + 1) * DM],
                                  xT[:, k, half * HALF:(half + 1) * HALF], k == 0, k == 1)
                    last.then_inc(bank_full, 1)

            def scores(kind, tile, unit, gh, kt, pair):
                g, half = divmod(gh, 2)
                pe.wait_ge(exp_done, unit - 1 + UNIT_CREDIT)
                ks, qs, rows = (d_stack, c_stack, KQ) if kind == COS else (k_stack, q_stack, ROWS)
                for j in (2 * pair, 2 * pair + 1):
                    h = g * GH + j
                    diagonal = kind == COS and kt // 3 == half
                    last = mm(score_ps[0:P, j, 0:HALF], ks[0:rows, h, kt * P:(kt + 1) * P],
                              qs[0:rows, h, half * HALF:(half + 1) * HALF], True, not diagonal)
                    if diagonal:
                        at = (kt % 3) * P
                        last = mm(score_ps[0:P, j, at:at + P], ident16[0:P, 0:P], minus_ident[0:P, 0:P], False, True)
                last.then_inc(scores_ready, 1)

            def values(tile, span, gh, kt):
                g = gh // 2
                pe.wait_ge(exp_done, 2 * tile + 2 + UNIT_CREDIT)
                if kt == 0:
                    pe.wait_ge(o_copied, span - 1 + BANK_CREDIT)
                rows = kept(kt)
                for j in range(GH):
                    last = mm(out_ps[32 * j:32 * j + 32, gh % 2, 0:HALF], v_aug[0:rows, kt, g * GH + j, :],
                              prob[0:rows, kt % 3, j, :], kt == 0, kt == T - 1)
                last.then_inc(pv_done, 1)

            def turn_out(ring, copies):
                bank = take(ring)
                pe.wait_ge(o_copied, copies)
                for t in range(3):
                    last = nc.tensor.transpose(job_ps[0:P, bank, t * 128:(t + 1) * 128], o_sb[:, t * P:(t + 1) * P], ident[:])
                last.then_inc(bank_full, 1)

            def max_tile(ring, i):
                if i is None:
                    return
                h, qt, half = i // (2 * T), (i // 2) % T, i % 2
                bank = take(ring)
                if half == 0:
                    out, keys = job_ps[0:P, bank, 0:HALF], k_stack[0:KQ, h, 0:HALF]
                else:
                    out = job_ps[0:P, bank, 0:3 * LAST]
                    keys = k_stack[0:KQ, h, HALF:S].rearrange("p (t k) -> p t k", t=3)[:, :, 0:LAST]
                mm(out, q_stack[0:KQ, h, qt * P:(qt + 1) * P], keys).then_inc(bank_full, 1)

            def turn_max(ring):
                for half in range(2):
                    bank = take(ring)
                    for t in range(3):
                        q = half * 3 + t
                        last = nc.tensor.transpose(job16[0:6 * H, bank, t * P:(t + 1) * P],
                                                   max_part[:, q:q + 2, :, :].rearrange("p t a h -> p (t a h)"),
                                                   ident16[0:P, 0:P])
                    last.then_inc(bank_full, 1)

            def output_projection(ring):
                for i in range(3):
                    bank = take(ring)
                    if i == 0:
                        pe.wait_ge(bank_free, ring.before + ring.count - 1 + BANK_CREDIT)
                    for t in (2 * i, 2 * i + 1):
                        for k in range(MT):
                            last = mm(job_ps[0:P, bank, (t % 2) * D:(t % 2 + 1) * D], featT[:, k, t * P:(t + 1) * P],
                                      wo[:, k, :], k == 0, k == 1)
                    last.then_inc(bank_full, 1)

            def mlp_in(ring, i):
                m, half = divmod(i, 2)
                bank = take(ring)
                if i == 0:
                    pe.wait_ge(bank_free, ring.before + ring.count - 1 + BANK_CREDIT)
                for k in range(MT):
                    last = mm(job_ps[:, bank, 0:HALF], wi[:, k, m * 128:(m + 1) * 128],
                              featT[:, k, half * HALF:(half + 1) * HALF], k == 0, k == 1)
                last.then_inc(bank_full, 1)

            def mlp_out(ring, i, n):
                pe.wait_ge(gelu_done, n + 1)
                bank = take(ring)
                for t in (2 * i, 2 * i + 1):
                    for k in range(FM):
                        last = mm(job_ps[0:P, bank, (t % 2) * D:(t % 2 + 1) * D], hid[:, k, t * P:(t + 1) * P],
                                  wo2[:, k, :], k == 0, k == FM - 1)
                last.then_inc(bank_full, 1)

            ring = Ring(0)
            pe.wait_ge(consts, 1)
            pe.wait_ge(proj_loaded, 16 * N_PROJ)
            turn_features(ring, x_in)
            project_cv(ring, 0)
            for m in range(MT):
                project_t(ring, wq, m)
            pe.wait_ge(c_unit, 1)
            turn_features(ring, c_tok)
            for m in range(MT):
                project_t(ring, wk, m)
            assert ring.count == PRO_JOBS

            with pe.Fori(0, STEPS) as n:
                ring = Ring(job_base(n))
                for kind in (COS, DOT):
                    if kind == COS:
                        pe.wait_ge(c_loaded, 16 * 12 * (n + 1))
                        pe.wait_ge(v_ready, n + 1)
                    else:
                        pe.wait_ge(max_ready, n + 1)
                        turn_max(ring)
                        pe.wait_ge(proj_loaded, 16 * N_PROJ * (n + 2))
                        turn_features(ring, x_in)
                        project_cv(ring, n)
                        pe.wait_ge(m_loaded, 16 * 3 * (n + 1))
                    for gh in range(SPANS):
                        span = n * STEP_SPANS + kind * SPANS + gh
                        for kt in range(T):
                            tile = n * STEP_TILES + (kind * SPANS + gh) * T + kt
                            unit = n * STEP_UNITS + ((kind * SPANS + gh) * T + kt) * 2
                            if kind == COS and gh == 1 and kt == 0:
                                pe.wait_ge(qk_loaded, 16 * 12 * (n + 1))
                            scores(kind, tile, unit, gh, kt, 0)
                            if kind == COS:
                                max_tile(ring, max_tile_at(gh, kt, 0))
                            scores(kind, tile, unit + 1, gh, kt, 1)
                            if kind == COS:
                                max_tile(ring, max_tile_at(gh, kt, 1))
                            if kt:
                                values(tile - 1, span, gh, kt - 1)
                            elif gh:
                                values(tile - 1, span - 1, gh - 1, T - 1)
                            if kind == COS:
                                max_tile(ring, max_tile_at(gh, kt, 2))
                            if kt == 2:
                                turn_out(ring, span + BANK_CREDIT)
                            if kind == COS:
                                if gh == 0 and kt == 3:
                                    pe.wait_ge(ctx_ready, SPANS * n + 1)
                                    turn_features(ring, ctxt)
                                if gh == 0 and kt == 5:
                                    pe.wait_ge(ffn_loaded, 16 * N_FFN * (n + 1))
                                    output_projection(ring)
                                if hidden_at(gh, kt) is not None:
                                    mlp_in(ring, hidden_at(gh, kt))
                                max_tile(ring, max_tile_at(gh, kt, 3))
                                max_tile(ring, max_tile_at(gh, kt, 4))
                                if gh == 1 and kt == 5:
                                    pe.wait_ge(normed1, T * (n + 1))
                                    turn_features(ring, x1)
                            else:
                                if gh == 0 and kt >= 3:
                                    mlp_out(ring, kt - 3, n)
                                if gh == 1 and kt in (2, 3):
                                    project_t(ring, wq, kt - 2)
                                if gh == 2 and kt == 1:
                                    pe.wait_ge(c_unit, n + 2)
                                    turn_features(ring, c_tok)
                                if gh == 3 and kt in (3, 4):
                                    project_t(ring, wk, kt - 3)
                    last_tile = n * STEP_TILES + (kind + 1) * SPANS * T - 1
                    values(last_tile, n * STEP_SPANS + (kind + 1) * SPANS - 1, SPANS - 1, T - 1)
                assert ring.count == STEP_JOBS

            ring = Ring(job_base(STEPS))
            turn_out(ring, STEP_SPANS * STEPS + BANK_CREDIT)
            pe.wait_ge(ctx_ready, SPANS * STEPS + 1)
            turn_features(ring, ctxt)
            pe.wait_ge(ffn_loaded, 16 * N_FFN * (STEPS + 1))
            output_projection(ring)
            pe.wait_ge(normed1, T * (STEPS + 1))
            turn_features(ring, x1)
            for i in range(2 * FM):
                mlp_in(ring, i)
            for i in range(3):
                mlp_out(ring, i, STEPS)

        @block.scalar
        def _(act):
            with act.Fori(0, STEPS) as n:
                for kind in (COS, DOT):
                    if kind == DOT:
                        act.wait_ge(bank_free, job_base(n) + COS_JOBS + BANK_CREDIT)
                        nc.scalar.activation(hid[:], hid[:], ACT.Gelu).then_inc(gelu_done, 1)
                    for gh in range(SPANS):
                        for kt in range(T):
                            tile = n * STEP_TILES + (kind * SPANS + gh) * T + kt
                            unit = n * STEP_UNITS + ((kind * SPANS + gh) * T + kt) * 2
                            for pair in range(2):
                                act.wait_ge(scores_ready, unit + pair + 1)
                                if pair == 0:
                                    act.wait_ge(pv_done, tile - 2 + TILE_CREDIT)
                                nc.scalar.activation(prob[:, kt % 3, 2 * pair:2 * pair + 2, :],
                                                     score_ps[0:P, 2 * pair:2 * pair + 2, 0:HALF], ACT.Exp,
                                                     scale=-1.0 if kind == COS else 1.0).then_inc(exp_done, 1)
            act.wait_ge(bank_free, job_base(STEPS) + 1 + 4 + 3 + 4 + 2 * FM + BANK_CREDIT)
            nc.scalar.activation(hid[:], hid[:], ACT.Gelu).then_inc(gelu_done, 1)

        @block.vector
        def _(dve):
            def full(ring):
                bank, use = ring.take()
                dve.wait_ge(bank_full, use)
                return bank

            def copy_turned(ring, dst, scale=None, bias=None):
                for m in range(MT):
                    for half in range(2):
                        bank = full(ring)
                        out, src = dst[0:DM, m, half * HALF:(half + 1) * HALF], job_ps[0:DM, bank, 0:HALF]
                        if scale is None:
                            nc.vector.tensor_copy(out, src).then_inc(bank_free, 1)
                        else:
                            nc.vector.tensor_scalar(out, src, scale[:, m:m + 1], bias[:, m:m + 1],
                                                    ALU.mult, ALU.add).then_inc(bank_free, 1)

            opT_view = opT[0:DM, :].rearrange("p (m s) -> p m s", m=MT)
            squares_view = opT[0:P, 0:T * D]

            def take_cv(ring):
                for t in range(T):
                    bank = full(ring)
                    done.add(nc.vector.tensor_tensor(c_tok[:, t, :], job_ps[0:P, bank, 0:D], bcv[:, 0:D], ALU.add))
                    nc.vector.tensor_tensor(v_next[:, t, :], job_ps[0:P, bank, D:2 * D], bcv[:, D:2 * D],
                                            ALU.add).then_inc(bank_free, 1)
                dve.wait_ge(vec, done.now())
                c_flat = c_tok[:, :, :].rearrange("p t d -> p (t d)")
                done.add(nc.vector.tensor_tensor(squares_view, c_flat, c_flat, ALU.mult))
                dve.wait_ge(vec, done.now())
                nc.vector.tensor_reduce(c_norm[:], squares_view.rearrange("p (h d) -> p h d", d=DH), AX.X,
                                        ALU.add).then_inc(squares, 1)

            def take_operand(ring, m, bias, factor):
                for half in range(2):
                    bank = full(ring)
                    nc.vector.tensor_scalar(opT_view[:, m, half * HALF:(half + 1) * HALF], job_ps[0:DM, bank, 0:HALF],
                                            bias[:, m:m + 1], factor, ALU.add, ALU.mult).then_inc(bank_free, 1)

            def split(free_before, copied):
                dve.wait_ge(bank_free, copied)
                dve.wait_ge(parts_stored, free_before)
                hi, mid, lo = (p[:, :, :] for p in part)
                done.add(nc.vector.tensor_copy(hi, opT_view))
                dve.wait_ge(vec, done.now())
                done.add(nc.vector.tensor_tensor(opT_view, opT_view, hi, ALU.subtract))
                dve.wait_ge(vec, done.now())
                done.add(nc.vector.tensor_copy(mid, opT_view))
                dve.wait_ge(vec, done.now())
                nc.vector.tensor_tensor(lo, opT_view, mid, ALU.subtract).then_inc(parts_ready, 1)

            def unit_c(count):
                dve.wait_ge(c_norm_ready, count)
                view = c_tok[:, :, :].rearrange("p t (h d) -> p (t h) d", d=DH)
                nc.vector.tensor_tensor(view, view, c_norm[:, :, None].broadcast_to([P, T * H, DH]),
                                        ALU.mult).then_inc(c_unit, 1)

            def place_v(count):
                dve.wait_ge(pv_done, count)
                nc.vector.tensor_copy(v_aug[:, :, :, 0:DH].rearrange("p t h d -> p (t h) d"),
                                      v_next[:, :, :].rearrange("p t (h d) -> p (t h) d", d=DH)).then_inc(v_ready, 1)

            def copy_out(span, gh):
                dve.wait_ge(pv_done, (span + 1) * T + TILE_CREDIT)
                nc.vector.tensor_copy(o_sb[:], out_ps[:, gh % 2, 0:HALF]).then_inc(o_copied, 1)

            def add_out(ring, kind, gh, count):
                g, half = divmod(gh, 2)
                bank = full(ring)
                sums = job_ps[0:P, bank, 0:3 * 128].rearrange("p (t j c) -> p t j c", t=3, j=GH)
                done.add(nc.vector.reciprocal(recip[:], sums[:, :, :, DH]))
                dve.wait_ge(vec, done.now())
                target = ctxt[:, half * 3:half * 3 + 3, g * GH * DH:(g + 1) * GH * DH]
                out = (target if kind == COS else partial[:, :, :]).rearrange("p t (j d) -> p t j d", d=DH)
                nc.vector.tensor_tensor(out, sums[:, :, :, 0:DH], recip[:, :, :, None].broadcast_to([P, 3, GH, DH]),
                                        ALU.mult).then_inc(bank_free, 1)
                dve.wait_ge(bank_free, ring.before + ring.count + BANK_CREDIT)
                if kind == DOT:
                    nc.vector.tensor_tensor(target, target, partial[:, :, :], ALU.add).then_inc(ctx_ready, 1)

            def take_rows(ring, moments):
                for i in range(3):
                    bank = full(ring)
                    nc.vector.tensor_tensor(x1[:, 2 * i:2 * i + 2, :],
                                            job_ps[0:P, bank, 0:2 * D].rearrange("p (t d) -> p t d", t=2),
                                            resid[:, 2 * i:2 * i + 2, :], ALU.add).then_inc(bank_free, 1)
                dve.wait_ge(bank_free, ring.before + ring.count + BANK_CREDIT)
                for t in range(T):
                    done.add(nc.vector.bn_stats(stats[:, t, :], x1[:, t, :]))
                dve.wait_ge(vec, done.now())
                combine_stats(nc, dve, done, stats, mean_var, mean_gap, D).then_inc(moments, 1)

            def norm_rows(moments, rstd_ready, normed, n):
                dve.wait_ge(moments, n + 1)
                dve.wait_ge(rstd_ready, n + 1)
                for t in range(T):
                    nc.vector.tensor_scalar(x1[:, t, :], x1[:, t, :], mean_var[:, t, 0:1], rstd[:, t:t + 1],
                                            ALU.subtract, ALU.mult).then_inc(normed, 1)

            def take_max(ring, i):
                if i is None:
                    return
                h, qt, half = i // (2 * T), (i // 2) % T, i % 2
                bank = full(ring)
                at = qt * H + h
                nc.vector.tensor_reduce(neg_max[:, half, at:at + 1], job_ps[0:P, bank, 0:HALF if half == 0 else 3 * LAST],
                                        AX.X, ALU.max, negate=True).then_inc(bank_free, 1)

            def split_max():
                view = lambda i: neg_max[:, i, :].rearrange("p (t h) -> p t h", h=H)
                dve.wait_ge(bank_free, ring.before + ring.count + BANK_CREDIT)
                done.add(nc.vector.tensor_tensor(view(0), view(0), view(1), ALU.min))
                for i in range(2):
                    dve.wait_ge(vec, done.now())
                    done.add(nc.vector.tensor_copy(max_part[:, 0:T, i, :], view(0)))
                    dve.wait_ge(vec, done.now())
                    done.add(nc.vector.tensor_tensor(view(0), view(0), max_part[:, 0:T, i, :], ALU.subtract))
                dve.wait_ge(vec, done.now())
                nc.vector.tensor_copy(max_part[:, 0:T, 2, :], view(0)).then_inc(max_ready, 1)

            def take_turned_max(ring):
                for half in range(2):
                    bank = full(ring)
                    nc.vector.tensor_copy(maxT[:, half * HALF:(half + 1) * HALF],
                                          job16[0:3 * H, bank, 0:HALF]).then_inc(bank_free, 1)

            def take_hidden(ring, i):
                m, half = divmod(i, 2)
                bank = full(ring)
                nc.vector.tensor_scalar(hid[:, m, half * HALF:(half + 1) * HALF], job_ps[:, bank, 0:HALF],
                                        bi_col[:, m:m + 1], None, ALU.add).then_inc(bank_free, 1)

            done = Tally(vec)
            done.add(nc.vector.memset(v_aug[:], 0.0))
            dve.wait_ge(vec, done.now())
            nc.vector.memset(v_aug[:, :, :, DH:DH + 1], 2.0).then_inc(bank_free, BANK_CREDIT)
            nc.vector.memset(k_stack[KQ:ROWS, :, :], 1.0).then_inc(pv_done, TILE_CREDIT)
            nc.vector.memset(o_sb[:], 1.0).then_inc(o_copied, BANK_CREDIT)
            nc.vector.memset(ctxt[:], 0.0).then_inc(exp_done, UNIT_CREDIT)
            dve.wait_ge(exp_done, UNIT_CREDIT)
            done.add(nc.vector.memset(recip[:], 1.0))
            nc.vector.memset(max_part[:], 0.0).then_inc(x_stored, 1)
            dve.wait_ge(x_stored, 1)
            dve.wait_ge(consts, 1)
            dve.wait_ge(proj_loaded, 16 * N_PROJ)
            ring = Ring(0)
            copy_turned(ring, xT)
            take_cv(ring)
            dve.wait_ge(squares, 1)
            for m in range(MT):
                take_operand(ring, m, bq_col, DH ** -0.5)
            split(0, ring.count + BANK_CREDIT)
            unit_c(1)
            dve.wait_ge(parts_ready, 1)
            copy_turned(ring, opT_view)
            split(16 * 3, ring.count + BANK_CREDIT)
            dve.wait_ge(parts_ready, 2)
            for m in range(MT):
                take_operand(ring, m, bk_col, 1.0)
            split(16 * 6, ring.count + BANK_CREDIT)
            place_v(TILE_CREDIT)
            assert ring.count == PRO_JOBS and done.count == VEC_PRO, done.count

            with dve.Fori(0, STEPS) as n:
                ring = Ring(job_base(n))
                done = Tally(vec, n * VEC_STEP + VEC_PRO)
                for kind in (COS, DOT):
                    if kind == DOT:
                        split_max()
                        take_turned_max(ring)
                        copy_turned(ring, xT)
                        dve.wait_ge(parts_ready, 3 * n + 3)
                        take_cv(ring)
                    for gh in range(SPANS):
                        span = n * STEP_SPANS + kind * SPANS + gh
                        for kt in range(T):
                            if kind == COS:
                                take_max(ring, max_tile_at(gh, kt, 0))
                                take_max(ring, max_tile_at(gh, kt, 1))
                            if kt == 0 and gh:
                                copy_out(span - 1, gh - 1)
                            if kind == COS:
                                take_max(ring, max_tile_at(gh, kt, 2))
                            if kt == 2:
                                before_kind, before_gh = (kind, gh - 1) if gh else (1 - kind, SPANS - 1)
                                add_out(ring, before_kind, before_gh, span)
                            if kind == COS:
                                if gh == 0 and kt == 3:
                                    dve.wait_ge(ctx_ready, SPANS * n + 1)
                                    copy_turned(ring, featT)
                                if gh == 0 and kt == 5:
                                    dve.wait_ge(resid_in, n + 1)
                                    dve.wait_ge(x_stored, 16 * n + 1)
                                    take_rows(ring, moments1)
                                if hidden_at(gh, kt) is not None:
                                    take_hidden(ring, hidden_at(gh, kt))
                                take_max(ring, max_tile_at(gh, kt, 3))
                                take_max(ring, max_tile_at(gh, kt, 4))
                                if gh == 1 and kt == 3:
                                    norm_rows(moments1, rstd1, normed1, n)
                                if gh == 1 and kt == 5:
                                    copy_turned(ring, featT, g1_col, b1_col)
                            else:
                                if gh == 0 and kt == 3:
                                    dve.wait_ge(resid_mid, n + 1)
                                    take_rows(ring, moments2)
                                if gh == 1 and kt in (2, 3):
                                    if kt == 2:
                                        dve.wait_ge(squares, n + 2)
                                    take_operand(ring, kt - 2, bq_col, DH ** -0.5)
                                    if kt == 3:
                                        split(16 * 9 * (n + 1), ring.before + ring.count + BANK_CREDIT)
                                        unit_c(n + 2)
                                if gh == 2 and kt == 1:
                                    dve.wait_ge(parts_ready, 3 * n + 4)
                                    copy_turned(ring, opT_view)
                                    split(16 * (9 * n + 12), ring.before + ring.count + BANK_CREDIT)
                                    norm_rows(moments2, rstd2, normed2, n)
                                if gh == 3 and kt in (3, 4):
                                    dve.wait_ge(parts_ready, 3 * n + 5)
                                    take_operand(ring, kt - 3, bk_col, 1.0)
                                    if kt == 4:
                                        split(16 * (9 * n + 15), ring.before + ring.count + BANK_CREDIT)
                    copy_out(n * STEP_SPANS + (kind + 1) * SPANS - 1, SPANS - 1)
                place_v((n + 1) * STEP_TILES + TILE_CREDIT)
                assert ring.count == STEP_JOBS and done.count == VEC_STEP, done.count

            ring = Ring(job_base(STEPS))
            done = Tally(vec, STEPS * VEC_STEP + VEC_PRO)
            add_out(ring, DOT, SPANS - 1, 0)
            dve.wait_ge(ctx_ready, SPANS * STEPS + 1)
            copy_turned(ring, featT)
            dve.wait_ge(resid_in, STEPS + 1)
            dve.wait_ge(x_stored, 16 * STEPS + 1)
            take_rows(ring, moments1)
            norm_rows(moments1, rstd1, normed1, STEPS)
            copy_turned(ring, featT, g1_col, b1_col)
            for i in range(2 * FM):
                take_hidden(ring, i)
            dve.wait_ge(resid_mid, STEPS + 1)
            take_rows(ring, moments2)
            norm_rows(moments2, rstd2, normed2, STEPS)

        @block.gpsimd
        def _(gp):
            order = Tally(pool)

            def after(instruction):
                gp.wait_ge(pool, order.add(instruction))

            def input_residual(n):
                gp.wait_ge(ffn_loaded, 16 * N_FFN * (n + 1))
                nc.gpsimd.tensor_tensor(resid[:], resid[:], bo[:, None, :].broadcast_to([P, T, D]),
                                        ALU.add).then_inc(resid_in, 1)

            def root(moments, ready, n):
                gp.wait_ge(moments, n + 1)
                after(nc.gpsimd.tensor_tensor(rstd[:], mean_var[:, :, 1], eps[:], ALU.add))
                nc.gpsimd.tensor_tensor(rstd[:], rstd[:], minus_half[:, 0:T], ALU.pow).then_inc(ready, 1)

            def middle_residual(n):
                gp.wait_ge(normed1, T * (n + 1))
                gp.wait_ge(resid_in, n + 1)
                after(nc.gpsimd.tensor_tensor(resid[:], x1[:], g1[:, None, :].broadcast_to([P, T, D]), ALU.mult))
                after(nc.gpsimd.tensor_tensor(resid[:], resid[:], b1[:, None, :].broadcast_to([P, T, D]), ALU.add))
                nc.gpsimd.tensor_tensor(resid[:], resid[:], bo2[:, None, :].broadcast_to([P, T, D]),
                                        ALU.add).then_inc(resid_mid, 1)

            def c_root(n):
                gp.wait_ge(squares, n + 1)
                nc.gpsimd.tensor_tensor(c_norm[:], c_norm[:], minus_half[:], ALU.pow).then_inc(c_norm_ready, 1)

            def result(n):
                gp.wait_ge(normed2, T * (n + 1))
                after(nc.gpsimd.tensor_tensor(x1[:], x1[:], g2[:, None, :].broadcast_to([P, T, D]), ALU.mult))
                nc.gpsimd.tensor_tensor(x1[:], x1[:], b2[:, None, :].broadcast_to([P, T, D]), ALU.add).then_inc(x_out, 1)

            after(nc.gpsimd.memset(ident[:], 0.0))
            after(nc.gpsimd.memset(minus_half[:], -0.5))
            after(nc.gpsimd.memset(eps[:], BLOCK_EPS))
            after(nc.gpsimd.affine_select(out=ident[:], in_=ident[:], compare_op=ALU.not_equal, fill=1.0, base=0,
                                          pattern=[[-1, 128]], channel_multiplier=1))
            after(nc.gpsimd.tensor_copy(ident16[:], ident[:]))
            nc.gpsimd.tensor_scalar(minus_ident[:], ident[:], -1.0, None, ALU.mult).then_inc(consts, 1)
            c_root(0)
            start = order.count
            with gp.Fori(0, STEPS) as n:
                order = Tally(pool, start + 5 * n)
                input_residual(n)
                root(moments1, rstd1, n)
                middle_residual(n)
                c_root(n + 1)
                root(moments2, rstd2, n)
                result(n)
                assert order.count == 5
            order = Tally(pool, start + 5 * STEPS)
            input_residual(STEPS)
            root(moments1, rstd1, STEPS)
            middle_residual(STEPS)
            root(moments2, rstd2, STEPS)
            result(STEPS)


EC = E * R // 128
EX_JOBS = 4 + 2 + 1 + 2 + 2 * EC + 2 * EC + 3
EX_VEC = 24
assert EX_JOBS % 2 == 0


def experts(nc, w, sorted_d, state_d, out):
    with ExitStack() as ctx:
        sb = lambda name, shape, dt=F32: ctx.enter_context(nc.sbuf_tensor("ex_" + name, shape, dt))
        sem = lambda name: ctx.enter_context(nc.semaphore("ex_" + name))
        h = sb("h", [P, T, D])
        attn = sb("attn", [P, T, D])
        y = sb("y", [P, T, D])
        yT = sb("yT", [DM, MT, S])
        result = sb("result", [P, T, D])
        enc_w = sb("enc_w", [DM, MT, R])
        enc_b = sb("enc_b", [R, 1])
        sw_w = sb("sw_w", [R, E])
        sw_b = sb("sw_b", [P, E])
        w1 = sb("w1", [DM, MT, E, R])
        b1 = sb("b1", [128, EC])
        w2 = sb("w2", [128, EC, D])
        b2 = sb("b2", [E, D])
        encT = sb("encT", [R, S])
        logit = sb("logit", [P, T, E])
        top = sb("top", [P, T])
        total = sb("total", [P, T])
        prob = sb("prob", [P, T, E])
        prob_max = sb("prob_max", [P, T])
        first = sb("first", [P, E])
        onehot = sb("onehot", [P, T, E])
        onehotT = sb("onehotT", [E, S])
        spread = sb("spread", [E, E * R])
        hid = sb("hid", [128, EC, S])
        ident = sb("ident", [128, 128])
        stats = sb("stats", [P, T, 6])
        mean_var = sb("mean_var", [P, T, 2])
        mean_gap = sb("mean_gap", [P, T])
        eps = sb("eps", [P, T])
        rstd = sb("rstd", [P, T])
        minus_half = sb("minus_half", [P, T])
        job_ps = ctx.enter_context(nc.psum_tensor("ex_job", [128, 2, 512], F32))

        consts = sem("consts")
        w_loaded = sem("w_loaded")
        x_loaded = sem("x_loaded")
        bank_full = sem("bank_full")
        bank_free = sem("bank_free")
        vec = sem("vec")
        moments = sem("moments")
        rstd_ready = sem("rstd_ready")
        normed = sem("normed")
        logits_ready = sem("logits_ready")
        exp_done = sem("exp_done")
        onehot_ready = sem("onehot_ready")
        gelu_done = sem("gelu_done")
        out_stored = sem("out_stored")
        pool = sem("pool")
        block = ctx.enter_context(nc.Block())
        LOADS = 8

        @block.sync
        def _(sp):
            for dst, src in (
                    (enc_w[:], w["enc_w"].rearrange("(k p) n -> p k n", p=DM)),
                    (enc_b[:], w["enc_b"].rearrange("(r o) -> r o", o=1)),
                    (sw_w[:], w["sw_w"]),
                    (sw_b[:], w["sw_b"].partition_broadcast(P)),
                    (b1[:], w["eb1"].rearrange("(c a) r -> (a r) c", c=EC)),
                    (w2[:], w["ew2"].rearrange("(c a) r d -> (a r) c d", c=EC)),
                    (b2[:], w["eb2"])):
                sp.dma_start(dst, src, allow_slow_non_contiguous=True).then_inc(w_loaded, 16)
            for k in range(MT):
                sp.dma_start(w1[:, k, :, :], w["ew1"][:, k * DM:(k + 1) * DM, :].rearrange("e p r -> p e r")
                             ).then_inc(w_loaded, 16)
            with sp.Fori(0, B) as b:
                sp.wait_ge(bank_free, EX_JOBS * b + BANK_CREDIT)
                sp.dma_start(h[:], sorted_d.rearrange("(b n) d -> b n d", n=N)[bass.ds(b, 1), 0:S, :]
                             .rearrange("a (p t) d -> p (a t) d", t=T)).then_inc(x_loaded, 16)
                sp.dma_start(attn[:], state_d[bass.ds(b + STEPS - B, 1)].rearrange("a (p t) d -> p (a t) d", t=T)
                             ).then_inc(x_loaded, 16)
                sp.wait_ge(bank_free, EX_JOBS * (b + 1) + BANK_CREDIT)
                sp.dma_start(out[bass.ds(b, 1), 0:LAST * T, :].rearrange("a (p t) d -> p (a t) d", t=T),
                             result[0:LAST, :, :]).then_inc(out_stored, 16)
                sp.dma_start(out[bass.ds(b, 1), LAST * T:KEEP, :], result[LAST:LAST + 1, 0:FULL, :]
                             ).then_inc(out_stored, 16)
            sp.wait_ge(out_stored, 32 * B + 1)

        @block.gpsimd
        def _(gp):
            nc.gpsimd.memset(ident[:], 0.0).then_inc(pool, 1)
            nc.gpsimd.memset(spread[:], 1.0).then_inc(pool, 1)
            for e in range(E):
                nc.gpsimd.memset(first[:, e:e + 1], float(E - e)).then_inc(consts, 1)
            nc.gpsimd.memset(minus_half[:], -0.5).then_inc(consts, 1)
            nc.gpsimd.memset(eps[:], LN_EPS).then_inc(pool, 1)
            gp.wait_ge(pool, 3)
            nc.gpsimd.affine_select(out=ident[:], in_=ident[:], compare_op=ALU.not_equal, fill=1.0, base=0,
                                    pattern=[[-1, 128]], channel_multiplier=1).then_inc(consts, 1)
            nc.gpsimd.affine_select(out=spread[:], in_=spread[:], compare_op=ALU.is_ge, fill=0.0, base=0,
                                    pattern=[[1, E * R]], channel_multiplier=-R).then_inc(pool, 1)
            gp.wait_ge(pool, 4)
            nc.gpsimd.affine_select(out=spread[:], in_=spread[:], compare_op=ALU.is_ge, fill=0.0, base=R - 1,
                                    pattern=[[-1, E * R]], channel_multiplier=R).then_inc(consts, 1)
            with gp.Fori(0, B) as b:
                gp.wait_ge(moments, b + 1)
                nc.gpsimd.tensor_tensor(rstd[:], mean_var[:, :, 1], eps[:], ALU.add).then_inc(pool, 1)
                gp.wait_ge(pool, b + 5)
                nc.gpsimd.tensor_tensor(rstd[:], rstd[:], minus_half[:], ALU.pow).then_inc(rstd_ready, 1)

        @block.tensor
        def _(pe):
            def mm(out_, a, b_, start=True, stop=True):
                return nc.tensor.matmul(out_, a, b_, start=start, stop=stop)

            pe.wait_ge(w_loaded, 16 * (7 + MT))
            pe.wait_ge(consts, E + 3)
            with pe.Fori(0, B) as b:
                ring = Ring(b * EX_JOBS)

                def take():
                    bank, use = ring.take()
                    pe.wait_ge(bank_free, use - 2 + BANK_CREDIT)
                    return bank

                def copied():
                    pe.wait_ge(bank_free, ring.before + ring.count + BANK_CREDIT)

                pe.wait_ge(normed, T * (b + 1))
                for m in range(MT):
                    for half in range(2):
                        bank = take()
                        for t in range(3):
                            last = nc.tensor.transpose(job_ps[0:DM, bank, t * P:(t + 1) * P],
                                                       y[:, half * 3 + t, m * DM:(m + 1) * DM], ident[0:P, 0:P])
                        last.then_inc(bank_full, 1)
                copied()
                for half in range(2):
                    bank = take()
                    for k in range(MT):
                        last = mm(job_ps[0:R, bank, 0:HALF], enc_w[:, k, :], yT[:, k, half * HALF:(half + 1) * HALF],
                                  k == 0, k == 1)
                    last.then_inc(bank_full, 1)
                copied()
                bank = take()
                for t in range(T):
                    last = mm(job_ps[0:P, bank, t * E:(t + 1) * E], encT[:, t * P:(t + 1) * P], sw_w[:])
                last.then_inc(bank_full, 1)
                for c in range(EC):
                    for half in range(2):
                        bank = take()
                        for k in range(MT):
                            last = mm(job_ps[:, bank, 0:HALF],
                                      w1[:, k, 2 * c:2 * c + 2, :].rearrange("p a r -> p (a r)"),
                                      yT[:, k, half * HALF:(half + 1) * HALF], k == 0, k == 1)
                        last.then_inc(bank_full, 1)
                pe.wait_ge(onehot_ready, b + 1)
                for half in range(2):
                    bank = take()
                    for t in range(3):
                        last = nc.tensor.transpose(job_ps[0:E, bank, t * P:(t + 1) * P], onehot[:, half * 3 + t, :],
                                                   ident[0:P, 0:P])
                    last.then_inc(bank_full, 1)
                copied()
                for c in range(EC):
                    for half in range(2):
                        bank = take()
                        mm(job_ps[:, bank, 0:HALF], spread[:, c * 128:(c + 1) * 128],
                           onehotT[:, half * HALF:(half + 1) * HALF]).then_inc(bank_full, 1)
                copied()
                for i in range(3):
                    bank = take()
                    for t in (2 * i, 2 * i + 1):
                        to = job_ps[0:P, bank, (t % 2) * D:(t % 2 + 1) * D]
                        for c in range(EC):
                            mm(to, hid[:, c, t * P:(t + 1) * P], w2[:, c, :], c == 0, False)
                        last = mm(to, onehotT[:, t * P:(t + 1) * P], b2[:], False, True)
                    last.then_inc(bank_full, 1)
                assert ring.count == EX_JOBS

        @block.scalar
        def _(act):
            with act.Fori(0, B) as b:
                act.wait_ge(logits_ready, b + 1)
                nc.scalar.activation(prob[:], logit[:], ACT.Exp).then_inc(exp_done, 1)
                act.wait_ge(bank_free, b * EX_JOBS + 7 + 2 * EC + BANK_CREDIT)
                nc.scalar.activation(hid[:], hid[:], ACT.Gelu).then_inc(gelu_done, 1)

        @block.vector
        def _(dve):
            nc.vector.memset(total[:], 0.0).then_inc(bank_free, BANK_CREDIT)
            nc.vector.memset(top[:], 0.0).then_inc(out_stored, 1)
            dve.wait_ge(out_stored, 1)
            dve.wait_ge(bank_free, BANK_CREDIT)
            dve.wait_ge(w_loaded, 16 * (7 + MT))
            dve.wait_ge(consts, E + 3)
            with dve.Fori(0, B) as b:
                ring = Ring(b * EX_JOBS)
                done = Tally(vec, b * EX_VEC)

                def link(instruction):
                    dve.wait_ge(vec, done.add(instruction))

                def full():
                    bank, use = ring.take()
                    dve.wait_ge(bank_full, use)
                    return bank

                def by_expert(v):
                    return v[:, :, None].broadcast_to([P, T, E])

                dve.wait_ge(x_loaded, 32 * (b + 1))
                link(nc.vector.tensor_tensor(h[:], h[:], attn[:], ALU.add))
                for t in range(T):
                    done.add(nc.vector.bn_stats(stats[:, t, :], h[:, t, :]))
                dve.wait_ge(vec, done.now())
                combine_stats(nc, dve, done, stats, mean_var, mean_gap, D).then_inc(moments, 1)
                dve.wait_ge(moments, b + 1)
                dve.wait_ge(rstd_ready, b + 1)
                for t in range(T):
                    nc.vector.tensor_scalar(y[:, t, :], h[:, t, :], mean_var[:, t, 0:1], rstd[:, t:t + 1],
                                            ALU.subtract, ALU.mult).then_inc(normed, 1)
                for m in range(MT):
                    for half in range(2):
                        bank = full()
                        nc.vector.tensor_copy(yT[:, m, half * HALF:(half + 1) * HALF],
                                              job_ps[0:DM, bank, 0:HALF]).then_inc(bank_free, 1)
                for half in range(2):
                    bank = full()
                    nc.vector.tensor_scalar(encT[:, half * HALF:(half + 1) * HALF], job_ps[0:R, bank, 0:HALF],
                                            enc_b[:, 0:1], None, ALU.add).then_inc(bank_free, 1)
                bank = full()
                nc.vector.tensor_tensor(logit[:], job_ps[0:P, bank, 0:T * E].rearrange("p (t e) -> p t e", e=E),
                                        sw_b[:, None, :].broadcast_to([P, T, E]), ALU.add).then_inc(bank_free, 1)
                dve.wait_ge(bank_free, ring.before + ring.count + BANK_CREDIT)
                link(nc.vector.tensor_reduce(top[:], logit[:], AX.X, ALU.max))
                nc.vector.tensor_tensor(logit[:], logit[:], by_expert(top), ALU.subtract).then_inc(logits_ready, 1)
                for c in range(EC):
                    for half in range(2):
                        bank = full()
                        nc.vector.tensor_scalar(hid[:, c, half * HALF:(half + 1) * HALF], job_ps[:, bank, 0:HALF],
                                                b1[:, c:c + 1], None, ALU.add).then_inc(bank_free, 1)
                dve.wait_ge(exp_done, b + 1)
                link(nc.vector.tensor_reduce(total[:], prob[:], AX.X, ALU.add))
                link(nc.vector.reciprocal(total[:], total[:]))
                link(nc.vector.tensor_tensor(prob[:], prob[:], by_expert(total), ALU.mult))
                link(nc.vector.tensor_reduce(prob_max[:], prob[:], AX.X, ALU.max))
                link(nc.vector.tensor_tensor(onehot[:], prob[:], by_expert(prob_max), ALU.is_equal))
                link(nc.vector.tensor_tensor(onehot[:], onehot[:], first[:, None, :].broadcast_to([P, T, E]), ALU.mult))
                link(nc.vector.tensor_reduce(top[:], onehot[:], AX.X, ALU.max))
                nc.vector.tensor_tensor(onehot[:], onehot[:], by_expert(top), ALU.is_equal).then_inc(onehot_ready, 1)
                for half in range(2):
                    bank = full()
                    nc.vector.tensor_copy(onehotT[:, half * HALF:(half + 1) * HALF],
                                          job_ps[0:E, bank, 0:HALF]).then_inc(bank_free, 1)
                dve.wait_ge(gelu_done, b + 1)
                for c in range(EC):
                    for half in range(2):
                        bank = full()
                        part = hid[:, c, half * HALF:(half + 1) * HALF]
                        nc.vector.tensor_tensor(part, part, job_ps[:, bank, 0:HALF], ALU.mult).then_inc(bank_free, 1)
                dve.wait_ge(out_stored, 32 * b + 1)
                for i in range(3):
                    bank = full()
                    for t in (2 * i, 2 * i + 1):
                        row = nc.vector.scalar_tensor_tensor(
                            out=result[:, t, :], in0=job_ps[0:P, bank, (t % 2) * D:(t % 2 + 1) * D],
                            scalar=prob_max[:, t:t + 1], in1=h[:, t, :], op0=ALU.mult, op1=ALU.add)
                        if t % 2:
                            row.then_inc(bank_free, 1)
                        else:
                            done.add(row)
                dve.wait_ge(bank_free, ring.before + ring.count + BANK_CREDIT)
                assert ring.count == EX_JOBS and done.count == EX_VEC, done.count


def audio_tower(nc, w, out):
    scores_d = nc.dram_tensor("scores_scratch", (B * XT, 128), F32, kind="Internal").ap()
    sorted_d = nc.dram_tensor("sorted_scratch", (B * N, D), F32, kind="Internal").ap()
    state_d = nc.dram_tensor("state_scratch", (SLOTS, S, D), F32, kind="Internal").ap()
    parts_d = nc.dram_tensor("parts_scratch", (3, 3, D, S), BF16, kind="Internal").ap()
    sort_tokens(nc, w["x"], w["tok_w"], w["tok_b"], scores_d, sorted_d, state_d)
    layers(nc, w, parts_d, state_d)
    experts(nc, w, sorted_d, state_d, out)


_INS = {
    "x": "x", "L0_tok_w": "tok_w", "L0_tok_b": "tok_b",
    "L0_attn_Wq": "Wq", "L0_attn_bq": "bq", "L0_attn_Wk": "Wk", "L0_attn_bk": "bk", "L0_attn_Wv": "Wv",
    "L0_attn_bv": "bv", "L0_attn_Wc": "Wc", "L0_attn_bc": "bc", "L0_attn_Wo": "Wo", "L0_attn_bo": "bo",
    "L0_attn_g1": "g1", "L0_attn_b1": "b1", "L0_attn_Wi": "Wi", "L0_attn_bi": "bi", "L0_attn_Wo2": "Wo2",
    "L0_attn_bo2": "bo2", "L0_attn_g2": "g2", "L0_attn_b2": "b2",
    "L0_ffn_enc_w": "enc_w", "L0_ffn_enc_b": "enc_b", "L0_ffn_sw_w": "sw_w", "L0_ffn_sw_b": "sw_b",
    "L0_ffn_w1": "ew1", "L0_ffn_b1": "eb1", "L0_ffn_w2": "ew2", "L0_ffn_b2": "eb2",
}
_OUTS = [((B, KEEP, D), "float32")]


def kernel(**inputs):
    import numpy as _np
    import concourse.bacc as _bacc
    from concourse import mybir as _mybir
    from concourse.bass_utils import run_bass_kernel_spmd as _run

    nc = _bacc.Bacc("TRN2", target_bir_lowering=False, num_devices=1)
    arrays, args = {}, {}
    for name, short in _INS.items():
        a = _np.ascontiguousarray(inputs[name])
        arrays[f"in_{name}_dram"] = a
        args[short] = nc.dram_tensor(f"in_{name}_dram", a.shape, _mybir.dt.from_np(a.dtype), kind="ExternalInput").ap()
    shape, dtype = _OUTS[0]
    out = nc.dram_tensor("out_0_dram", shape, _mybir.dt.from_np(_np.dtype(dtype)), kind="ExternalOutput").ap()
    audio_tower(nc, args, out)
    r = _run(nc, [arrays], core_ids=[0])
    return r.results[0]["out_0_dram"]
```

```python
from contextlib import ExitStack

import concourse.bass as bass
from concourse import mybir

ALU = mybir.AluOpType
ACT = mybir.ActivationFunctionType
F32 = mybir.dt.float32
BF16 = mybir.dt.bfloat16
I32 = mybir.dt.int32
AX = mybir.AxisListType

B, N, D = 8, 1024, 192
KEEP = int(round(N * 0.7))
L, H, DH = 4, 12, 16
F = 768
R, E = 64, 8
LN_EPS, BLOCK_EPS = 1e-5, 1e-12

T = 6
P = 120
S = T * P
HALF = S // 2
MT = 2
DM = D // MT
FM = F // 128
XT = N // 128
COS, DOT = 0, 1
GROUPS, GH = 3, 4
SPANS = GROUPS * 2
STEPS = L * B
SLOTS = STEPS + B + 1
Q_PARTS = (0, 0, 0, 1, 1, 2)
K_PARTS = (0, 1, 2, 0, 1, 0)
KQ = len(Q_PARTS) * DH
ROWS = KQ + 3
MAX_TILES = H * T * 2
GROUP_TILES = GH * T * 2
HIDDEN_AT = (0, 3, 5)
LAST = (KEEP - 1) // T
FULL = KEEP - LAST * T


def kept(t):
    return P if t < FULL else LAST


class Tally:

    def __init__(self, sem, before=0):
        self.sem, self.before, self.count = sem, before, 0

    def add(self, instruction, by=1):
        instruction.then_inc(self.sem, by)
        self.count += by
        return self.before + self.count

    def now(self):
        return self.before + self.count


def max_tile_at(kind, gh, kt, i):
    if kind == COS:
        n = ((gh - 2) * T + kt) * 4 + i
        return n if gh >= 2 and i < 4 else None
    n = 2 * GROUP_TILES + (gh * T + kt) * 3 + i
    return n if n < 3 * GROUP_TILES and i < 3 else None


def hidden_at(gh, kt):
    return ((gh - 2) * len(HIDDEN_AT) + HIDDEN_AT.index(kt)) if gh >= 2 and kt in HIDDEN_AT else None


class Ring:

    def __init__(self, depth, before=0, bank=0):
        self.depth, self.before, self.bank, self.count = depth, before, bank, 0

    def take(self):
        k = self.count
        self.count += 1
        return (self.bank + k) % self.depth, self.before + k + 1


def combine_stats(nc, dve, done, stats, mean_var, spread, width):
    def link(instruction):
        dve.wait_ge(done.sem, done.add(instruction))

    link(nc.vector.tensor_tensor(spread[:], stats[:, :, 1], stats[:, :, 4], ALU.subtract))
    link(nc.vector.tensor_tensor(spread[:], spread[:], spread[:], ALU.mult))
    link(nc.vector.tensor_tensor(mean_var[:, :, 0], stats[:, :, 1], stats[:, :, 4], ALU.add))
    link(nc.vector.tensor_scalar(mean_var[:, :, 0], mean_var[:, :, 0], 0.5, None, ALU.mult))
    link(nc.vector.tensor_tensor(mean_var[:, :, 1], stats[:, :, 2], stats[:, :, 5], ALU.add))
    link(nc.vector.tensor_scalar(mean_var[:, :, 1], mean_var[:, :, 1], 1.0 / width, None, ALU.mult))
    return nc.vector.scalar_tensor_tensor(out=mean_var[:, :, 1], in0=spread[:], scalar=0.25,
                                          in1=mean_var[:, :, 1], op0=ALU.mult, op1=ALU.add)


def sort_tokens(nc, x, tok_w, tok_b, scores_d, sorted_d, state_d):
    with ExitStack() as ctx:
        sb = lambda name, shape, dt=F32: ctx.enter_context(nc.sbuf_tensor("so_" + name, shape, dt))
        sem = lambda name: ctx.enter_context(nc.semaphore("so_" + name))
        x_all = sb("x", [128, B * XT, D])
        prod = sb("prod", [128, B * XT, D])
        w_bc = sb("w", [128, D])
        b_bc = sb("b", [128, 1])
        score = sb("score", [128, B * XT])
        score_row = sb("score_row", [128, B * N])
        scoreT = sb("scoreT", [B * XT, 128])
        junk = sb("junk", [128, N])
        before = sb("before", [128, 128])
        counts = sb("counts", [128, XT, 3])
        rank = sb("rank", [128, XT])
        first_row = sb("first_row", [128, B * XT])
        place = sb("place", [128, B * XT], I32)
        ident = sb("ident", [128, 128])
        kept_x = sb("kept", [P, B, T * D])
        stats = sb("stats", [P, T, 6])
        mean_var = sb("mean_var", [P, T, 2])
        mean_gap = sb("mean_gap", [P, T])
        eps = sb("eps", [P, T])
        rstd = sb("rstd", [P, T])
        minus_half = sb("minus_half", [P, T])
        turned = ctx.enter_context(nc.psum_tensor("so_turned", [128, 128], F32))

        consts = sem("consts")
        x_loaded = sem("x_loaded")
        scored = sem("scored")
        turned_done = sem("turned")
        row_ready = sem("row_ready")
        row_stored = sem("row_stored")
        row_loaded = sem("row_loaded")
        vec = sem("vec")
        ranked = sem("ranked")
        scattered = [sem(f"scattered{b}") for b in range(B)]
        kept_loaded = [sem(f"kept{b}") for b in range(2)]
        moments = sem("moments")
        rstd_ready = sem("rstd_ready")
        pool = sem("pool")
        normed = sem("normed")
        stored = sem("stored")

        block = ctx.enter_context(nc.Block())
        RANK_OPS = 3 * XT
        NORM_OPS = T + 6

        @block.sync
        def _(sp):
            sp.dma_start(w_bc[:], tok_w.rearrange("d o -> (o d)").partition_broadcast(128)).then_inc(x_loaded, 16)
            sp.dma_start(b_bc[:], tok_b.partition_broadcast(128)).then_inc(x_loaded, 16)
            for b in range(B):
                sp.dma_start(x_all[:, b * XT:(b + 1) * XT, :],
                             x[b].rearrange("(t p) d -> p t d", p=128)).then_inc(x_loaded, 16)
            sp.wait_ge(row_ready, 1)
            sp.dma_start(scores_d, scoreT[:]).then_inc(row_stored, 16)
            sp.wait_ge(row_stored, 16)
            sp.dma_start(score_row[:], scores_d.rearrange("a b -> (a b)").partition_broadcast(128)).then_inc(row_loaded, 16)
            for b in range(B):
                sp.wait_ge(scattered[b], 16 * XT)
                if b >= 2:
                    sp.wait_ge(kept_loaded[b % 2], 16 * (b // 2))
                sp.dma_start(kept_x[:, b, :], sorted_d[b * N:b * N + S].rearrange("(p t) d -> p (t d)", t=T)
                             ).then_inc(kept_loaded[b % 2], 16)
            for b in range(B):
                sp.wait_ge(normed, T * (b + 1))
                sp.dma_start(state_d[STEPS + b].rearrange("(p t) d -> p (t d)", t=T), kept_x[:, b, :]).then_inc(stored, 16)
            sp.wait_ge(stored, 16 * B)

        @block.gpsimd
        def _(pool_e):
            nc.gpsimd.memset(ident[:], 0.0).then_inc(pool, 1)
            nc.gpsimd.memset(before[:], 1.0).then_inc(pool, 1)
            nc.gpsimd.memset(minus_half[:], -0.5).then_inc(consts, 1)
            nc.gpsimd.memset(eps[:], LN_EPS).then_inc(pool, 1)
            for b in range(B):
                nc.gpsimd.memset(first_row[:, b * XT:(b + 1) * XT], float(b * N)).then_inc(consts, 1)
            pool_e.wait_ge(pool, 3)
            nc.gpsimd.affine_select(out=ident[:], in_=ident[:], compare_op=ALU.not_equal, fill=1.0, base=0,
                                    pattern=[[-1, 128]], channel_multiplier=1).then_inc(consts, 1)
            nc.gpsimd.affine_select(out=before[:], in_=before[:], compare_op=ALU.is_gt, fill=0.0, base=0,
                                    pattern=[[-1, 128]], channel_multiplier=1).then_inc(consts, 1)
            for b in range(B):
                pool_e.wait_ge(ranked, b + 1)
                for t in range(XT):
                    k = b * XT + t
                    nc.gpsimd.indirect_dma_start(
                        out=sorted_d, out_offset=bass.IndirectOffsetOnAxis(ap=place[:, k:k + 1], axis=0),
                        in_=x_all[:, k, :], in_offset=None).then_inc(scattered[b], 16)
            for b in range(B):
                pool_e.wait_ge(moments, b + 1)
                nc.gpsimd.tensor_tensor(rstd[:], mean_var[:, :, 1], eps[:], ALU.add).then_inc(pool, 1)
                pool_e.wait_ge(pool, 4 + b)
                nc.gpsimd.tensor_tensor(rstd[:], rstd[:], minus_half[:], ALU.pow).then_inc(rstd_ready, 1)

        @block.tensor
        def _(pe):
            pe.wait_ge(scored, 1)
            pe.wait_ge(consts, B + 3)
            nc.tensor.transpose(turned[0:B * XT, :], score[:], ident[:]).then_inc(turned_done, 1)

        @block.vector
        def _(dve):
            dve.wait_ge(x_loaded, 16 * (B + 2))
            nc.vector.memset(counts[:], 0.0).then_inc(vec, 1)
            nc.vector.tensor_tensor(prod[:], x_all[:], w_bc[:, None, :].broadcast_to([128, B * XT, D]),
                                    ALU.mult).then_inc(vec, 1)
            dve.wait_ge(vec, 2)
            nc.vector.tensor_reduce(score[:], prod[:], AX.X, ALU.add).then_inc(vec, 1)
            dve.wait_ge(vec, 3)
            nc.vector.tensor_scalar(score[:], score[:], b_bc[:, 0:1], None, ALU.add).then_inc(scored, 1)
            dve.wait_ge(turned_done, 1)
            nc.vector.tensor_copy(scoreT[:], turned[0:B * XT, :]).then_inc(row_ready, 1)
            dve.wait_ge(row_loaded, 16)
            dve.wait_ge(consts, B + 3)
            dve.wait_ge(scored, 1)
            with dve.Fori(0, B) as b:
                done = Tally(vec, b * RANK_OPS + 3)
                row = b * N
                for t in range(XT):
                    s = score[:, bass.ds(b * XT + t, 1)]
                    if t:
                        done.add(nc.vector.tensor_scalar(junk[:, 0:128 * t], score_row[:, bass.ds(row, 128 * t)], s, 0.0,
                                                         ALU.is_ge, ALU.add, accum_out=counts[:, t, 0:1]))
                        dve.wait_ge(vec, done.now())
                    done.add(nc.vector.tensor_scalar(junk[:, 0:N - 128 * t],
                                                     score_row[:, bass.ds(row + 128 * t, N - 128 * t)], s, 0.0,
                                                     ALU.is_gt, ALU.add, accum_out=counts[:, t, 1:2]))
                    dve.wait_ge(vec, done.now())
                    done.add(nc.vector.scalar_tensor_tensor(
                        out=junk[:, 0:128], in0=score_row[:, bass.ds(row + 128 * t, 128)], scalar=s, in1=before[:],
                        op0=ALU.is_equal, op1=ALU.mult, accum_out=counts[:, t, 2:3]))
                    dve.wait_ge(vec, done.now())
                done.add(nc.vector.tensor_reduce(rank[:], counts[:], AX.X, ALU.add))
                dve.wait_ge(vec, done.now())
                nc.vector.tensor_tensor(place[:, bass.ds(b * XT, XT)], rank[:], first_row[:, bass.ds(b * XT, XT)],
                                        ALU.add).then_inc(ranked, 1)
                dve.wait_ge(ranked, b + 1)
                assert done.count == RANK_OPS
            ranks_done = 3 + B * RANK_OPS
            for b in range(B):
                dve.wait_ge(kept_loaded[b % 2], 16 * (b // 2 + 1))
                done = Tally(vec, ranks_done + NORM_OPS * b)
                for t in range(T):
                    done.add(nc.vector.bn_stats(stats[:, t, :], kept_x[:, b, t * D:(t + 1) * D]))
                dve.wait_ge(vec, done.now())
                combine_stats(nc, dve, done, stats, mean_var, mean_gap, D).then_inc(moments, 1)
                dve.wait_ge(moments, b + 1)
                dve.wait_ge(rstd_ready, b + 1)
                for t in range(T):
                    xt = kept_x[:, b, t * D:(t + 1) * D]
                    nc.vector.tensor_scalar(xt, xt, mean_var[:, t, 0:1], rstd[:, t:t + 1],
                                            ALU.subtract, ALU.mult).then_inc(normed, 1)
                dve.wait_ge(normed, T * (b + 1))


SPAN_UNITS = T * 2
STEP_UNITS = 2 * SPANS * SPAN_UNITS
STEP_TILES = 2 * SPANS * T
STEP_SPANS = 2 * SPANS
PRO_JOBS = 4 + T + 4 + 4 + 4
TAIL_JOBS = 4 + 3 + 4 + FM * 2 + 3
STEP_JOBS = PRO_JOBS + TAIL_JOBS + STEP_SPANS + MAX_TILES + GROUPS
MAX_DONE_AT = ((COS, 4, 0), (DOT, 0, 0), (DOT, 2, 4))
MAX_TURNED_AT = ((COS, 4, 1), (DOT, 0, 1), (DOT, 2, 5))


def jobs_at(kind, gh, kt):
    n = sum(max_tile_at(kind, gh, kt, i) is not None for i in range(4)) + (kt == 2) + ((kind, gh, kt) in MAX_TURNED_AT)
    if kind == COS:
        n += {(0, 3): 4, (0, 4): 2, (0, 5): 1, (1, 4): 4}.get((gh, kt), 0) + (hidden_at(gh, kt) is not None)
    else:
        n += {(0, 3): 1, (0, 4): 1, (0, 5): 1, (1, 1): 2, (1, 3): 2, (2, 3): 4, (4, 1): 2, (4, 3): 2}.get((gh, kt), 0)
    return n


def jobs_through(kind, gh, kt):
    order = [(s, g, t) for s in (COS, DOT) for g in range(SPANS) for t in range(T)]
    n = sum(jobs_at(*at) for at in order[:order.index((kind, gh, kt)) + 1])
    return n + (4 + T if kind == DOT else 0)


UNIT_CREDIT, TILE_CREDIT, OUT_CREDIT = 2, 3, 1
BANKS = BANK_CREDIT = 3
VEC_PRO, VEC_STEP = 18, 67
N_PROJ, N_FFN = 9, 13
assert STEP_JOBS % BANKS == 0 and jobs_through(DOT, SPANS - 1, T - 1) == STEP_JOBS


def layers(nc, w, parts_d, state_d):
    with ExitStack() as ctx:
        sb = lambda name, shape, dt=F32: ctx.enter_context(nc.sbuf_tensor("la_" + name, shape, dt))
        sem = lambda name: ctx.enter_context(nc.semaphore("la_" + name))
        q_stack = sb("q_stack", [ROWS, H, S], BF16)
        k_stack = sb("k_stack", [ROWS, H, S], BF16)
        c_stack = sb("c_stack", [KQ, H, S], BF16)
        d_stack = sb("d_stack", [KQ, H, S], BF16)
        prob = sb("prob", [P, 3, GH, HALF])
        x_in = sb("x_in", [P, T, D])
        resid = sb("resid", [P, T, D])
        x1 = sb("x1", [P, T, D])
        xT = sb("xT", [DM, MT, S])
        featT = sb("featT", [DM, MT, S])
        ctxt = sb("ctx", [P, T, D])
        partial = sb("partial", [P, 3, GH * DH])
        hid = sb("hid", [128, FM, S])
        c_tok = sb("c_tok", [P, T, D])
        v_next = sb("v_next", [P, T, D])
        v_aug = sb("v_aug", [P, T, H, 32])
        o_sb = sb("o_sb", [128, HALF])
        opT = sb("opT", [128, MT * S])
        part = [sb(f"part{i}", [DM, MT, S], BF16) for i in range(3)]
        wq, wk, wo = (sb(n, [DM, MT, D]) for n in ("wq", "wk", "wo"))
        wcv = sb("wcv", [DM, MT, 2 * D])
        wi = sb("wi", [DM, MT, F])
        wo2 = sb("wo2", [128, FM, D])
        bcv = sb("bcv", [P, 2 * D])
        bq_col, bk_col, g1_col, b1_col = (sb(n, [DM, MT]) for n in ("bq_col", "bk_col", "g1_col", "b1_col"))
        bi_col = sb("bi_col", [128, FM])
        bo, g1, b1, bo2, g2, b2 = (sb(n, [P, D]) for n in ("bo", "g1", "b1", "bo2", "g2", "b2"))
        ident = sb("ident", [128, 128])
        ident16 = sb("ident16", [128, 128], BF16)
        minus_ident = sb("minus_ident", [128, 128], BF16)
        minus_half = sb("minus_half", [P, T * H])
        neg_max = sb("neg_max", [P, GROUPS, 2, T * GH])
        max_part = sb("max_part", [P, 2 * T - 1, 3, GH], BF16)
        maxT = sb("maxT", [3 * GH, GROUPS, S], BF16)
        recip = sb("recip", [P, 3, GH])
        stats = sb("stats", [P, T, 6])
        mean_var = sb("mean_var", [P, T, 2])
        mean_gap = sb("mean_gap", [P, T])
        eps = sb("eps", [P, T])
        rstd = sb("rstd", [P, T])
        c_norm = sb("c_norm", [P, T * H])

        score_ps = ctx.enter_context(nc.psum_tensor("la_score", [128, GH, 512], F32))
        out_ps = ctx.enter_context(nc.psum_tensor("la_out", [128, 512], F32))
        job_ps = ctx.enter_context(nc.psum_tensor("la_job", [128, BANKS, 512], F32))
        job16 = job_ps[:, :, :].bitcast(BF16)

        consts = sem("consts")
        proj_loaded = sem("proj_loaded")
        ffn_loaded = sem("ffn_loaded")
        qk_loaded = sem("qk_loaded")
        c_loaded = sem("c_loaded")
        m_loaded = sem("m_loaded")
        parts_stored = sem("parts_stored")
        x_stored = sem("x_stored")
        scores_ready = sem("scores_ready")
        exp_done = sem("exp_done")
        pv_done = sem("pv_done")
        o_copied = sem("o_copied")
        bank_full = sem("bank_full")
        bank_free = sem("bank_free")
        vec = sem("vec")
        v_ready = sem("v_ready")
        parts_ready = sem("parts_ready")
        max_ready = sem("max_ready")
        moments1 = sem("moments1")
        moments2 = sem("moments2")
        rstd1 = sem("rstd1")
        rstd2 = sem("rstd2")
        normed1 = sem("normed1")
        normed2 = sem("normed2")
        resid_in = sem("resid_in")
        resid_mid = sem("resid_mid")
        x_out = sem("x_out")
        ctx_ready = sem("ctx_ready")
        squares = sem("squares")
        c_norm_ready = sem("c_norm_ready")
        c_unit = sem("c_unit")
        gelu_done = sem("gelu_done")
        pool = sem("pool")

        block = ctx.enter_context(nc.Block())

        def slot_of_input(n):
            return (n + STEPS) % (STEPS + B)

        def slot_of_output(n):
            return (n + SLOTS - 1) % SLOTS

        def job_base(n):
            return n * STEP_JOBS + PRO_JOBS

        @block.sync
        def _(sp):
            def load_projection(layer, slot):
                y = layer
                for dst, src in (
                        (wq[:], w["Wq"][y].rearrange("a (k p) n -> p (a k) n", p=DM)),
                        (wk[:], w["Wk"][y].rearrange("a (k p) n -> p (a k) n", p=DM)),
                        (wcv[:, :, 0:D], w["Wc"][y].rearrange("a (k p) n -> p (a k) n", p=DM)),
                        (wcv[:, :, D:2 * D], w["Wv"][y].rearrange("a (k p) n -> p (a k) n", p=DM)),
                        (bcv[:, 0:D], w["bc"][y].rearrange("a d -> (a d)").partition_broadcast(P)),
                        (bcv[:, D:2 * D], w["bv"][y].rearrange("a d -> (a d)").partition_broadcast(P)),
                        (bq_col[:], w["bq"][y].rearrange("a (k p) -> p (a k)", p=DM)),
                        (bk_col[:], w["bk"][y].rearrange("a (k p) -> p (a k)", p=DM)),
                        (x_in[:], state_d[slot].rearrange("a (p t) d -> p (a t) d", t=T))):
                    sp.dma_start(dst, src, allow_slow_non_contiguous=True).then_inc(proj_loaded, 16)

            def load_mlp(layer, slot):
                y = layer
                for dst, src in (
                        (wo[:], w["Wo"][y].rearrange("a (k p) n -> p (a k) n", p=DM)),
                        (wi[:], w["Wi"][y].rearrange("a (k p) n -> p (a k) n", p=DM)),
                        (wo2[:], w["Wo2"][y].rearrange("a (k p) n -> p (a k) n", p=128)),
                        *((tile[:], w[name][y].rearrange("a d -> (a d)").partition_broadcast(P))
                          for tile, name in ((bo, "bo"), (g1, "g1"), (b1, "b1"), (bo2, "bo2"), (g2, "g2"), (b2, "b2"))),
                        (g1_col[:], w["g1"][y].rearrange("a (k p) -> p (a k)", p=DM)),
                        (b1_col[:], w["b1"][y].rearrange("a (k p) -> p (a k)", p=DM)),
                        (bi_col[:], w["bi"][y].rearrange("a (k p) -> p (a k)", p=128)),
                        (resid[:], state_d[slot].rearrange("a (p t) d -> p (a t) d", t=T))):
                    sp.dma_start(dst, src, allow_slow_non_contiguous=True).then_inc(ffn_loaded, 16)

            def store_parts(operand, count):
                sp.wait_ge(parts_ready, count)
                for i in range(3):
                    sp.dma_start(parts_d[operand, i].rearrange("(m p) s -> p m s", p=DM),
                                 part[i][:]).then_inc(parts_stored, 16)

            def load_stack(stack, operand, order, loaded):
                for i, p in enumerate(order):
                    sp.dma_start(stack[i * DH:(i + 1) * DH, :, :],
                                 parts_d[operand, p].rearrange("(h d) s -> d h s", d=DH)).then_inc(loaded, 16)

            def load_max(n, g):
                sp.wait_ge(bank_free, job_base(n) + jobs_through(*MAX_TURNED_AT[g]) + BANK_CREDIT)
                for i in range(3):
                    sp.dma_start(q_stack[KQ + i:KQ + i + 1, g * GH:(g + 1) * GH, :],
                                 maxT[i * GH:(i + 1) * GH, g, :]).then_inc(m_loaded, 16)

            load_projection(bass.ds(0, 1), bass.ds(STEPS, 1))
            load_mlp(bass.ds(0, 1), bass.ds(STEPS, 1))
            store_parts(0, 1)
            store_parts(1, 2)
            sp.wait_ge(parts_stored, 16 * 6)
            load_stack(c_stack, 1, Q_PARTS, c_loaded)
            load_stack(d_stack, 1, K_PARTS, c_loaded)
            store_parts(2, 3)
            with sp.Fori(0, STEPS) as n:
                sp.wait_ge(pv_done, n * STEP_TILES + TILE_CREDIT)
                sp.wait_ge(parts_stored, 16 * 9 * (n + 1))
                load_stack(q_stack, 0, Q_PARTS, qk_loaded)
                load_stack(k_stack, 2, K_PARTS, qk_loaded)
                sp.wait_ge(x_stored, 16 * n + 1)
                sp.wait_ge(bank_free, job_base(n) + BANK_CREDIT)
                load_projection(bass.ds(((n + 1) // B) % L, 1), bass.ds(slot_of_input(n + 1), 1))
                load_max(n, 0)
                load_max(n, 1)
                store_parts(0, 3 * n + 4)
                load_max(n, 2)
                store_parts(1, 3 * n + 5)
                sp.wait_ge(scores_ready, n * STEP_UNITS + STEP_UNITS // 2)
                sp.wait_ge(parts_stored, 16 * (9 * n + 15))
                load_stack(c_stack, 1, Q_PARTS, c_loaded)
                load_stack(d_stack, 1, K_PARTS, c_loaded)
                sp.wait_ge(x_out, n + 1)
                sp.dma_start(state_d[bass.ds(slot_of_output(n), 1)].rearrange("a (p t) d -> p (a t) d", t=T),
                             x1[:]).then_inc(x_stored, 16)
                sp.wait_ge(bank_free, job_base(n) + jobs_through(DOT, 0, 5) + BANK_CREDIT)
                load_mlp(bass.ds(n // B, 1), bass.ds(slot_of_input(n), 1))
                store_parts(2, 3 * n + 6)
            sp.wait_ge(x_out, STEPS + 1)
            sp.dma_start(state_d[STEPS - 1].rearrange("(p t) d -> p t d", t=T), x1[:]).then_inc(x_stored, 16)
            sp.wait_ge(x_stored, 16 * (STEPS + 1) + 1)
            sp.wait_ge(parts_stored, 16 * 9 * (STEPS + 1))
            sp.wait_ge(c_loaded, 16 * 12 * (STEPS + 1))
            sp.wait_ge(proj_loaded, 16 * N_PROJ * (STEPS + 1))

        @block.tensor
        def _(pe):
            def mm(out, a, b, start=True, stop=True):
                return nc.tensor.matmul(out, a, b, start=start, stop=stop)

            def take(ring):
                bank, use = ring.take()
                pe.wait_ge(bank_free, use)
                return bank

            def turn_features(ring, src):
                for m in range(MT):
                    for half in range(2):
                        bank = take(ring)
                        for t in range(3):
                            last = nc.tensor.transpose(job_ps[0:DM, bank, t * P:(t + 1) * P],
                                                       src[:, half * 3 + t, m * DM:(m + 1) * DM], ident[0:P, 0:P])
                        last.then_inc(bank_full, 1)

            def project_cv(ring, n):
                for t in range(T):
                    bank = take(ring)
                    if t == 0:
                        pe.wait_ge(bank_free, ring.before + ring.count - 1 + BANK_CREDIT)
                    for k in range(MT):
                        last = mm(job_ps[0:P, bank, 0:2 * D], xT[:, k, t * P:(t + 1) * P], wcv[:, k, :], k == 0, k == 1)
                    last.then_inc(bank_full, 1)

            def project_t(ring, weights, m):
                for half in range(2):
                    bank = take(ring)
                    for k in range(MT):
                        last = mm(job_ps[0:DM, bank, 0:HALF], weights[:, k, m * DM:(m + 1) * DM],
                                  xT[:, k, half * HALF:(half + 1) * HALF], k == 0, k == 1)
                    last.then_inc(bank_full, 1)

            def scores(kind, tile, unit, gh, kt, pair):
                g, half = divmod(gh, 2)
                pe.wait_ge(exp_done, unit - 1 + UNIT_CREDIT)
                ks, qs, rows = (d_stack, c_stack, KQ) if kind == COS else (k_stack, q_stack, ROWS)
                for j in (2 * pair, 2 * pair + 1):
                    h = g * GH + j
                    diagonal = kind == COS and kt // 3 == half
                    last = mm(score_ps[0:P, j, 0:HALF], ks[0:rows, h, kt * P:(kt + 1) * P],
                              qs[0:rows, h, half * HALF:(half + 1) * HALF], True, not diagonal)
                    if diagonal:
                        at = (kt % 3) * P
                        last = mm(score_ps[0:P, j, at:at + P], ident16[0:P, 0:P], minus_ident[0:P, 0:P], False, True)
                last.then_inc(scores_ready, 1)

            def values(tile, span, gh, kt):
                g = gh // 2
                pe.wait_ge(exp_done, 2 * tile + 2 + UNIT_CREDIT)
                if kt == 0:
                    pe.wait_ge(o_copied, span + OUT_CREDIT)
                rows = kept(kt)
                for j in range(GH):
                    last = mm(out_ps[32 * j:32 * j + 32, 0:HALF], v_aug[0:rows, kt, g * GH + j, :],
                              prob[0:rows, kt % 3, j, :], kt == 0, kt == T - 1)
                last.then_inc(pv_done, 1)

            def turn_out(ring, copies):
                bank = take(ring)
                pe.wait_ge(o_copied, copies)
                for t in range(3):
                    last = nc.tensor.transpose(job_ps[0:P, bank, t * 128:(t + 1) * 128], o_sb[:, t * P:(t + 1) * P], ident[:])
                last.then_inc(bank_full, 1)

            def max_tile(ring, i):
                if i is None:
                    return
                h, qt, half = i // (2 * T), (i // 2) % T, i % 2
                bank = take(ring)
                if half == 0:
                    out, keys = job_ps[0:P, bank, 0:HALF], k_stack[0:KQ, h, 0:HALF]
                else:
                    out = job_ps[0:P, bank, 0:3 * LAST]
                    keys = k_stack[0:KQ, h, HALF:S].rearrange("p (t k) -> p t k", t=3)[:, :, 0:LAST]
                mm(out, q_stack[0:KQ, h, qt * P:(qt + 1) * P], keys).then_inc(bank_full, 1)

            def turn_max(ring, count):
                bank = take(ring)
                pe.wait_ge(max_ready, count)
                for t in range(T):
                    last = nc.tensor.transpose(job16[0:3 * GH * T, bank, t * P:(t + 1) * P],
                                               max_part[:, t:t + T, :, :].rearrange("p t a h -> p (t a h)"),
                                               ident16[0:P, 0:P])
                last.then_inc(bank_full, 1)

            def output_projection(ring, i):
                bank = take(ring)
                if i == 0:
                    pe.wait_ge(bank_free, ring.before + ring.count - 1 + BANK_CREDIT)
                for t in (2 * i, 2 * i + 1):
                    for k in range(MT):
                        last = mm(job_ps[0:P, bank, (t % 2) * D:(t % 2 + 1) * D], featT[:, k, t * P:(t + 1) * P],
                                  wo[:, k, :], k == 0, k == 1)
                last.then_inc(bank_full, 1)

            def mlp_in(ring, i):
                m, half = divmod(i, 2)
                bank = take(ring)
                if i == 0:
                    pe.wait_ge(bank_free, ring.before + ring.count - 1 + BANK_CREDIT)
                for k in range(MT):
                    last = mm(job_ps[:, bank, 0:HALF], wi[:, k, m * 128:(m + 1) * 128],
                              featT[:, k, half * HALF:(half + 1) * HALF], k == 0, k == 1)
                last.then_inc(bank_full, 1)

            def mlp_out(ring, i, n):
                pe.wait_ge(gelu_done, n + 1)
                bank = take(ring)
                for t in (2 * i, 2 * i + 1):
                    for k in range(FM):
                        last = mm(job_ps[0:P, bank, (t % 2) * D:(t % 2 + 1) * D], hid[:, k, t * P:(t + 1) * P],
                                  wo2[:, k, :], k == 0, k == FM - 1)
                last.then_inc(bank_full, 1)

            ring = Ring(BANKS)
            pe.wait_ge(consts, 1)
            pe.wait_ge(proj_loaded, 16 * N_PROJ)
            turn_features(ring, x_in)
            project_cv(ring, 0)
            for m in range(MT):
                project_t(ring, wq, m)
            pe.wait_ge(c_unit, 1)
            turn_features(ring, c_tok)
            for m in range(MT):
                project_t(ring, wk, m)
            assert ring.count == PRO_JOBS
            pe.wait_ge(c_loaded, 16 * 12)
            for pair in range(2):
                scores(COS, 0, pair, 0, 0, pair)

            with pe.Fori(0, STEPS) as n:
                ring = Ring(BANKS, job_base(n), PRO_JOBS % BANKS)
                for kind in (COS, DOT):
                    if kind == COS:
                        pe.wait_ge(v_ready, n + 1)
                    else:
                        pe.wait_ge(proj_loaded, 16 * N_PROJ * (n + 2))
                        turn_features(ring, x_in)
                        project_cv(ring, n)
                    for gh in range(SPANS):
                        span = n * STEP_SPANS + kind * SPANS + gh
                        for kt in range(T):
                            tile = n * STEP_TILES + (kind * SPANS + gh) * T + kt
                            unit = n * STEP_UNITS + ((kind * SPANS + gh) * T + kt) * 2
                            if kind == DOT and gh % 2 == 0 and kt == 0:
                                pe.wait_ge(m_loaded, 16 * 3 * (GROUPS * n + gh // 2 + 1))
                            if kind == COS and gh == 2 and kt == 0:
                                pe.wait_ge(qk_loaded, 16 * 12 * (n + 1))
                            first = kind == COS and gh == 0 and kt == 0
                            if not first:
                                scores(kind, tile, unit, gh, kt, 0)
                            max_tile(ring, max_tile_at(kind, gh, kt, 0))
                            if not first:
                                scores(kind, tile, unit + 1, gh, kt, 1)
                            max_tile(ring, max_tile_at(kind, gh, kt, 1))
                            if kt:
                                values(tile - 1, span, gh, kt - 1)
                            elif gh:
                                values(tile - 1, span - 1, gh - 1, T - 1)
                            max_tile(ring, max_tile_at(kind, gh, kt, 2))
                            if (kind, gh, kt) in MAX_TURNED_AT:
                                turn_max(ring, GROUPS * n + MAX_TURNED_AT.index((kind, gh, kt)) + 1)
                            if kt == 2:
                                turn_out(ring, span + OUT_CREDIT)
                            if kind == COS:
                                if gh == 0 and kt == 3:
                                    pe.wait_ge(ctx_ready, SPANS * n + 1)
                                    turn_features(ring, ctxt)
                                if gh == 0 and kt == 4:
                                    pe.wait_ge(ffn_loaded, 16 * N_FFN * (n + 1))
                                    output_projection(ring, 0)
                                    output_projection(ring, 1)
                                if gh == 0 and kt == 5:
                                    output_projection(ring, 2)
                                if hidden_at(gh, kt) is not None:
                                    mlp_in(ring, hidden_at(gh, kt))
                                max_tile(ring, max_tile_at(kind, gh, kt, 3))
                                if gh == 1 and kt == 4:
                                    pe.wait_ge(normed1, T * (n + 1))
                                    turn_features(ring, x1)
                            else:
                                if gh == 0 and kt >= 3:
                                    mlp_out(ring, kt - 3, n)
                                if gh == 1 and kt in (1, 3):
                                    project_t(ring, wq, kt // 2)
                                if gh == 2 and kt == 3:
                                    pe.wait_ge(c_unit, n + 2)
                                    turn_features(ring, c_tok)
                                if gh == 4 and kt in (1, 3):
                                    project_t(ring, wk, kt // 2)
                            assert ring.count == jobs_through(kind, gh, kt), (kind, gh, kt, ring.count)
                    if kind == DOT:
                        pe.wait_ge(c_loaded, 16 * 12 * (n + 2))
                        for pair in range(2):
                            scores(COS, 0, (n + 1) * STEP_UNITS + pair, 0, 0, pair)
                    last_tile = n * STEP_TILES + (kind + 1) * SPANS * T - 1
                    values(last_tile, n * STEP_SPANS + (kind + 1) * SPANS - 1, SPANS - 1, T - 1)
                assert ring.count == STEP_JOBS

            ring = Ring(BANKS, job_base(STEPS), PRO_JOBS % BANKS)
            turn_out(ring, STEP_SPANS * STEPS + OUT_CREDIT)
            pe.wait_ge(ctx_ready, SPANS * STEPS + 1)
            turn_features(ring, ctxt)
            pe.wait_ge(ffn_loaded, 16 * N_FFN * (STEPS + 1))
            for i in range(3):
                output_projection(ring, i)
            pe.wait_ge(normed1, T * (STEPS + 1))
            turn_features(ring, x1)
            for i in range(2 * FM):
                mlp_in(ring, i)
            for i in range(3):
                mlp_out(ring, i, STEPS)

        @block.scalar
        def _(act):
            with act.Fori(0, STEPS) as n:
                for kind in (COS, DOT):
                    if kind == DOT:
                        act.wait_ge(bank_free, job_base(n) + jobs_through(COS, SPANS - 1, T - 1) + BANK_CREDIT)
                        nc.scalar.activation(hid[:], hid[:], ACT.Gelu).then_inc(gelu_done, 1)
                    for gh in range(SPANS):
                        for kt in range(T):
                            tile = n * STEP_TILES + (kind * SPANS + gh) * T + kt
                            unit = n * STEP_UNITS + ((kind * SPANS + gh) * T + kt) * 2
                            for pair in range(2):
                                act.wait_ge(scores_ready, unit + pair + 1)
                                if pair == 0:
                                    act.wait_ge(pv_done, tile - 2 + TILE_CREDIT)
                                nc.scalar.activation(prob[:, kt % 3, 2 * pair:2 * pair + 2, :],
                                                     score_ps[0:P, 2 * pair:2 * pair + 2, 0:HALF], ACT.Exp,
                                                     scale=-1.0 if kind == COS else 1.0).then_inc(exp_done, 1)
            act.wait_ge(bank_free, job_base(STEPS) + 1 + 4 + 3 + 4 + 2 * FM + BANK_CREDIT)
            nc.scalar.activation(hid[:], hid[:], ACT.Gelu).then_inc(gelu_done, 1)

        @block.vector
        def _(dve):
            def full(ring):
                bank, use = ring.take()
                dve.wait_ge(bank_full, use)
                return bank

            def copy_turned(ring, dst, scale=None, bias=None):
                for m in range(MT):
                    for half in range(2):
                        bank = full(ring)
                        out, src = dst[0:DM, m, half * HALF:(half + 1) * HALF], job_ps[0:DM, bank, 0:HALF]
                        if scale is None:
                            nc.vector.tensor_copy(out, src).then_inc(bank_free, 1)
                        else:
                            nc.vector.tensor_scalar(out, src, scale[:, m:m + 1], bias[:, m:m + 1],
                                                    ALU.mult, ALU.add).then_inc(bank_free, 1)

            opT_view = opT[0:DM, :].rearrange("p (m s) -> p m s", m=MT)
            squares_view = opT[0:P, 0:T * D]

            def take_cv(ring):
                for t in range(T):
                    bank = full(ring)
                    done.add(nc.vector.tensor_tensor(c_tok[:, t, :], job_ps[0:P, bank, 0:D], bcv[:, 0:D], ALU.add))
                    nc.vector.tensor_tensor(v_next[:, t, :], job_ps[0:P, bank, D:2 * D], bcv[:, D:2 * D],
                                            ALU.add).then_inc(bank_free, 1)

            def square_c():
                dve.wait_ge(vec, done.now())
                c_flat = c_tok[:, :, :].rearrange("p t d -> p (t d)")
                done.add(nc.vector.tensor_tensor(squares_view, c_flat, c_flat, ALU.mult))

            def sum_squares():
                dve.wait_ge(vec, done.now())
                nc.vector.tensor_reduce(c_norm[:], squares_view.rearrange("p (h d) -> p h d", d=DH), AX.X,
                                        ALU.add).then_inc(squares, 1)

            def take_operand(ring, m, bias, factor):
                for half in range(2):
                    bank = full(ring)
                    nc.vector.tensor_scalar(opT_view[:, m, half * HALF:(half + 1) * HALF], job_ps[0:DM, bank, 0:HALF],
                                            bias[:, m:m + 1], factor, ALU.add, ALU.mult).then_inc(bank_free, 1)

            def split_high(free_before, copied):
                dve.wait_ge(bank_free, copied)
                dve.wait_ge(parts_stored, free_before)
                done.add(nc.vector.tensor_copy(part[0][:, :, :], opT_view))
                dve.wait_ge(vec, done.now())
                done.add(nc.vector.tensor_tensor(opT_view, opT_view, part[0][:, :, :], ALU.subtract))

            def split_low():
                mid, lo = part[1][:, :, :], part[2][:, :, :]
                dve.wait_ge(vec, done.now())
                done.add(nc.vector.tensor_copy(mid, opT_view))
                dve.wait_ge(vec, done.now())
                nc.vector.tensor_tensor(lo, opT_view, mid, ALU.subtract).then_inc(parts_ready, 1)

            def unit_c(count):
                dve.wait_ge(c_norm_ready, count)
                view = c_tok[:, :, :].rearrange("p t (h d) -> p (t h) d", d=DH)
                nc.vector.tensor_tensor(view, view, c_norm[:, :, None].broadcast_to([P, T * H, DH]),
                                        ALU.mult).then_inc(c_unit, 1)

            def place_v(count):
                dve.wait_ge(pv_done, count)
                nc.vector.tensor_copy(v_aug[:, :, :, 0:DH].rearrange("p t h d -> p (t h) d"),
                                      v_next[:, :, :].rearrange("p t (h d) -> p (t h) d", d=DH)).then_inc(v_ready, 1)

            def copy_out(span, gh):
                dve.wait_ge(pv_done, (span + 1) * T + TILE_CREDIT)
                nc.vector.tensor_copy(o_sb[:], out_ps[:, 0:HALF]).then_inc(o_copied, 1)

            def add_out(ring, kind, gh, count):
                g, half = divmod(gh, 2)
                bank = full(ring)
                sums = job_ps[0:P, bank, 0:3 * 128].rearrange("p (t j c) -> p t j c", t=3, j=GH)
                done.add(nc.vector.reciprocal(recip[:], sums[:, :, :, DH]))
                dve.wait_ge(vec, done.now())
                target = ctxt[:, half * 3:half * 3 + 3, g * GH * DH:(g + 1) * GH * DH]
                out = (target if kind == COS else partial[:, :, :]).rearrange("p t (j d) -> p t j d", d=DH)
                nc.vector.tensor_tensor(out, sums[:, :, :, 0:DH], recip[:, :, :, None].broadcast_to([P, 3, GH, DH]),
                                        ALU.mult).then_inc(bank_free, 1)
                dve.wait_ge(bank_free, ring.before + ring.count + BANK_CREDIT)
                if kind == DOT:
                    nc.vector.tensor_tensor(target, target, partial[:, :, :], ALU.add).then_inc(ctx_ready, 1)

            def take_rows(ring, i):
                bank = full(ring)
                nc.vector.tensor_tensor(x1[:, 2 * i:2 * i + 2, :],
                                        job_ps[0:P, bank, 0:2 * D].rearrange("p (t d) -> p t d", t=2),
                                        resid[:, 2 * i:2 * i + 2, :], ALU.add).then_inc(bank_free, 1)

                dve.wait_ge(bank_free, ring.before + ring.count + BANK_CREDIT)
                for t in (2 * i, 2 * i + 1):
                    done.add(nc.vector.bn_stats(stats[:, t, :], x1[:, t, :]))

            def row_moments(moments):
                dve.wait_ge(vec, done.now())
                combine_stats(nc, dve, done, stats, mean_var, mean_gap, D).then_inc(moments, 1)

            def norm_rows(moments, rstd_ready, normed, n):
                dve.wait_ge(moments, n + 1)
                dve.wait_ge(rstd_ready, n + 1)
                for t in range(T):
                    nc.vector.tensor_scalar(x1[:, t, :], x1[:, t, :], mean_var[:, t, 0:1], rstd[:, t:t + 1],
                                            ALU.subtract, ALU.mult).then_inc(normed, 1)

            def take_max(ring, i):
                if i is None:
                    return
                h, qt, half = i // (2 * T), (i // 2) % T, i % 2
                bank = full(ring)
                g, at = h // GH, qt * GH + h % GH
                nc.vector.tensor_reduce(neg_max[:, g, half, at:at + 1], job_ps[0:P, bank, 0:HALF if half == 0 else 3 * LAST],
                                        AX.X, ALU.max, negate=True).then_inc(bank_free, 1)

            def split_max(g):
                view = lambda i: neg_max[:, g, i, :].rearrange("p (t h) -> p t h", h=GH)
                dve.wait_ge(bank_free, ring.before + ring.count + BANK_CREDIT)
                done.add(nc.vector.tensor_tensor(view(0), view(0), view(1), ALU.min))
                for i in range(2):
                    dve.wait_ge(vec, done.now())
                    done.add(nc.vector.tensor_copy(max_part[:, 0:T, i, :], view(0)))
                    dve.wait_ge(vec, done.now())
                    done.add(nc.vector.tensor_tensor(view(0), view(0), max_part[:, 0:T, i, :], ALU.subtract))
                dve.wait_ge(vec, done.now())
                nc.vector.tensor_copy(max_part[:, 0:T, 2, :], view(0)).then_inc(max_ready, 1)

            def take_turned_max(ring, g):
                bank = full(ring)
                nc.vector.tensor_copy(maxT[:, g, :], job16[0:3 * GH, bank, 0:S]).then_inc(bank_free, 1)

            def take_hidden(ring, i):
                m, half = divmod(i, 2)
                bank = full(ring)
                nc.vector.tensor_scalar(hid[:, m, half * HALF:(half + 1) * HALF], job_ps[:, bank, 0:HALF],
                                        bi_col[:, m:m + 1], None, ALU.add).then_inc(bank_free, 1)

            done = Tally(vec)
            done.add(nc.vector.memset(v_aug[:], 0.0))
            dve.wait_ge(vec, done.now())
            nc.vector.memset(v_aug[:, :, :, DH:DH + 1], 2.0).then_inc(bank_free, BANK_CREDIT)
            nc.vector.memset(k_stack[KQ:ROWS, :, :], 1.0).then_inc(pv_done, TILE_CREDIT)
            nc.vector.memset(o_sb[:], 1.0).then_inc(o_copied, OUT_CREDIT)
            nc.vector.memset(ctxt[:], 0.0).then_inc(exp_done, UNIT_CREDIT)
            dve.wait_ge(exp_done, UNIT_CREDIT)
            done.add(nc.vector.memset(recip[:], 1.0))
            nc.vector.memset(max_part[:], 0.0).then_inc(x_stored, 1)
            dve.wait_ge(x_stored, 1)
            dve.wait_ge(consts, 1)
            dve.wait_ge(proj_loaded, 16 * N_PROJ)
            ring = Ring(BANKS)
            copy_turned(ring, xT)
            take_cv(ring)
            square_c()
            sum_squares()
            dve.wait_ge(squares, 1)
            for m in range(MT):
                take_operand(ring, m, bq_col, DH ** -0.5)
            split_high(0, ring.count + BANK_CREDIT)
            split_low()
            unit_c(1)
            dve.wait_ge(parts_ready, 1)
            copy_turned(ring, opT_view)
            split_high(16 * 3, ring.count + BANK_CREDIT)
            split_low()
            dve.wait_ge(parts_ready, 2)
            for m in range(MT):
                take_operand(ring, m, bk_col, 1.0)
            split_high(16 * 6, ring.count + BANK_CREDIT)
            split_low()
            place_v(TILE_CREDIT)
            assert ring.count == PRO_JOBS and done.count == VEC_PRO, done.count

            with dve.Fori(0, STEPS) as n:
                ring = Ring(BANKS, job_base(n), PRO_JOBS % BANKS)
                done = Tally(vec, n * VEC_STEP + VEC_PRO)
                for kind in (COS, DOT):
                    if kind == DOT:
                        copy_turned(ring, xT)
                        dve.wait_ge(parts_ready, 3 * n + 3)
                        take_cv(ring)
                    for gh in range(SPANS):
                        span = n * STEP_SPANS + kind * SPANS + gh
                        for kt in range(T):
                            take_max(ring, max_tile_at(kind, gh, kt, 0))
                            take_max(ring, max_tile_at(kind, gh, kt, 1))
                            if kt == 0 and gh:
                                copy_out(span - 1, gh - 1)
                            take_max(ring, max_tile_at(kind, gh, kt, 2))
                            if (kind, gh, kt) in MAX_TURNED_AT:
                                take_turned_max(ring, MAX_TURNED_AT.index((kind, gh, kt)))
                            if kt == 2:
                                before_kind, before_gh = (kind, gh - 1) if gh else (1 - kind, SPANS - 1)
                                add_out(ring, before_kind, before_gh, span)
                            if kind == COS:
                                if gh == 0 and kt == 3:
                                    dve.wait_ge(ctx_ready, SPANS * n + 1)
                                    copy_turned(ring, featT)
                                if gh == 0 and kt == 4:
                                    dve.wait_ge(resid_in, n + 1)
                                    dve.wait_ge(x_stored, 16 * n + 1)
                                    take_rows(ring, 0)
                                    take_rows(ring, 1)
                                if gh == 0 and kt == 5:
                                    take_rows(ring, 2)
                                if hidden_at(gh, kt) is not None:
                                    take_hidden(ring, hidden_at(gh, kt))
                                take_max(ring, max_tile_at(kind, gh, kt, 3))
                                if gh == 1 and kt == 0:
                                    row_moments(moments1)
                                if gh == 1 and kt == 3:
                                    norm_rows(moments1, rstd1, normed1, n)
                                if gh == 1 and kt == 4:
                                    copy_turned(ring, featT, g1_col, b1_col)
                            else:
                                if gh == 0 and kt >= 3:
                                    if kt == 3:
                                        dve.wait_ge(resid_mid, n + 1)
                                        square_c()
                                    if kt == 4:
                                        sum_squares()
                                    take_rows(ring, kt - 3)
                                    if kt == 5:
                                        row_moments(moments2)
                                if gh == 1 and kt in (1, 3):
                                    if kt == 1:
                                        dve.wait_ge(squares, n + 2)
                                    take_operand(ring, kt // 2, bq_col, DH ** -0.5)
                                if gh == 1 and kt == 4:
                                    split_high(16 * 9 * (n + 1), ring.before + ring.count + BANK_CREDIT)
                                if gh == 1 and kt == 5:
                                    split_low()
                                if gh == 2 and kt == 2:
                                    unit_c(n + 2)
                                if gh == 2 and kt == 3:
                                    dve.wait_ge(parts_ready, 3 * n + 4)
                                    copy_turned(ring, opT_view)
                                if gh == 3 and kt == 0:
                                    split_high(16 * (9 * n + 12), ring.before + ring.count + BANK_CREDIT)
                                if gh == 3 and kt == 1:
                                    split_low()
                                if gh == 3 and kt == 3:
                                    norm_rows(moments2, rstd2, normed2, n)
                                if gh == 4 and kt in (1, 3):
                                    if kt == 1:
                                        dve.wait_ge(parts_ready, 3 * n + 5)
                                    take_operand(ring, kt // 2, bk_col, 1.0)
                                if gh == 4 and kt == 4:
                                    split_high(16 * (9 * n + 15), ring.before + ring.count + BANK_CREDIT)
                                if gh == 4 and kt == 5:
                                    split_low()
                            if (kind, gh, kt) in MAX_DONE_AT:
                                split_max(MAX_DONE_AT.index((kind, gh, kt)))
                    copy_out(n * STEP_SPANS + (kind + 1) * SPANS - 1, SPANS - 1)
                place_v((n + 1) * STEP_TILES + TILE_CREDIT)
                assert ring.count == STEP_JOBS and done.count == VEC_STEP, done.count

            ring = Ring(BANKS, job_base(STEPS), PRO_JOBS % BANKS)
            done = Tally(vec, STEPS * VEC_STEP + VEC_PRO)
            add_out(ring, DOT, SPANS - 1, 0)
            dve.wait_ge(ctx_ready, SPANS * STEPS + 1)
            copy_turned(ring, featT)
            dve.wait_ge(resid_in, STEPS + 1)
            dve.wait_ge(x_stored, 16 * STEPS + 1)
            for i in range(3):
                take_rows(ring, i)
            row_moments(moments1)
            norm_rows(moments1, rstd1, normed1, STEPS)
            copy_turned(ring, featT, g1_col, b1_col)
            for i in range(2 * FM):
                take_hidden(ring, i)
            dve.wait_ge(resid_mid, STEPS + 1)
            for i in range(3):
                take_rows(ring, i)
            row_moments(moments2)
            norm_rows(moments2, rstd2, normed2, STEPS)

        @block.gpsimd
        def _(gp):
            order = Tally(pool)

            def after(instruction):
                gp.wait_ge(pool, order.add(instruction))

            def input_residual(n):
                gp.wait_ge(ffn_loaded, 16 * N_FFN * (n + 1))
                nc.gpsimd.tensor_tensor(resid[:], resid[:], bo[:, None, :].broadcast_to([P, T, D]),
                                        ALU.add).then_inc(resid_in, 1)

            def root(moments, ready, n):
                gp.wait_ge(moments, n + 1)
                after(nc.gpsimd.tensor_tensor(rstd[:], mean_var[:, :, 1], eps[:], ALU.add))
                nc.gpsimd.tensor_tensor(rstd[:], rstd[:], minus_half[:, 0:T], ALU.pow).then_inc(ready, 1)

            def middle_residual(n):
                gp.wait_ge(normed1, T * (n + 1))
                gp.wait_ge(resid_in, n + 1)
                after(nc.gpsimd.tensor_tensor(resid[:], x1[:], g1[:, None, :].broadcast_to([P, T, D]), ALU.mult))
                after(nc.gpsimd.tensor_tensor(resid[:], resid[:], b1[:, None, :].broadcast_to([P, T, D]), ALU.add))
                nc.gpsimd.tensor_tensor(resid[:], resid[:], bo2[:, None, :].broadcast_to([P, T, D]),
                                        ALU.add).then_inc(resid_mid, 1)

            def c_root(n):
                gp.wait_ge(squares, n + 1)
                nc.gpsimd.tensor_tensor(c_norm[:], c_norm[:], minus_half[:], ALU.pow).then_inc(c_norm_ready, 1)

            def result(n):
                gp.wait_ge(normed2, T * (n + 1))
                after(nc.gpsimd.tensor_tensor(x1[:], x1[:], g2[:, None, :].broadcast_to([P, T, D]), ALU.mult))
                nc.gpsimd.tensor_tensor(x1[:], x1[:], b2[:, None, :].broadcast_to([P, T, D]), ALU.add).then_inc(x_out, 1)

            after(nc.gpsimd.memset(ident[:], 0.0))
            after(nc.gpsimd.memset(minus_half[:], -0.5))
            after(nc.gpsimd.memset(eps[:], BLOCK_EPS))
            after(nc.gpsimd.affine_select(out=ident[:], in_=ident[:], compare_op=ALU.not_equal, fill=1.0, base=0,
                                          pattern=[[-1, 128]], channel_multiplier=1))
            after(nc.gpsimd.tensor_copy(ident16[:], ident[:]))
            nc.gpsimd.tensor_scalar(minus_ident[:], ident[:], -1.0, None, ALU.mult).then_inc(consts, 1)
            c_root(0)
            start = order.count
            with gp.Fori(0, STEPS) as n:
                order = Tally(pool, start + 5 * n)
                input_residual(n)
                root(moments1, rstd1, n)
                middle_residual(n)
                c_root(n + 1)
                root(moments2, rstd2, n)
                result(n)
                assert order.count == 5
            order = Tally(pool, start + 5 * STEPS)
            input_residual(STEPS)
            root(moments1, rstd1, STEPS)
            middle_residual(STEPS)
            root(moments2, rstd2, STEPS)
            result(STEPS)


EC = E * R // 128
EX_JOBS = 4 + 2 + 1 + 2 + 2 * EC + 2 * EC + 3
EX_VEC = 24
EX_BANKS = 4
assert EX_JOBS % EX_BANKS == 0


def experts(nc, w, sorted_d, state_d, out):
    with ExitStack() as ctx:
        sb = lambda name, shape, dt=F32: ctx.enter_context(nc.sbuf_tensor("ex_" + name, shape, dt))
        sem = lambda name: ctx.enter_context(nc.semaphore("ex_" + name))
        h = sb("h", [P, T, D])
        attn = sb("attn", [P, T, D])
        y = sb("y", [P, T, D])
        yT = sb("yT", [DM, MT, S])
        result = sb("result", [P, T, D])
        enc_w = sb("enc_w", [DM, MT, R])
        enc_b = sb("enc_b", [R, 1])
        sw_w = sb("sw_w", [R, E])
        sw_b = sb("sw_b", [P, E])
        w1 = sb("w1", [DM, MT, E, R])
        b1 = sb("b1", [128, EC])
        w2 = sb("w2", [128, EC, D])
        b2 = sb("b2", [E, D])
        encT = sb("encT", [R, S])
        logit = sb("logit", [P, T, E])
        top = sb("top", [P, T])
        total = sb("total", [P, T])
        prob = sb("prob", [P, T, E])
        prob_max = sb("prob_max", [P, T])
        first = sb("first", [P, E])
        onehot = sb("onehot", [P, T, E])
        onehotT = sb("onehotT", [E, S])
        spread = sb("spread", [E, E * R])
        hid = sb("hid", [128, EC, S])
        ident = sb("ident", [128, 128])
        stats = sb("stats", [P, T, 6])
        mean_var = sb("mean_var", [P, T, 2])
        mean_gap = sb("mean_gap", [P, T])
        eps = sb("eps", [P, T])
        rstd = sb("rstd", [P, T])
        minus_half = sb("minus_half", [P, T])
        job_ps = ctx.enter_context(nc.psum_tensor("ex_job", [128, EX_BANKS, 512], F32))

        consts = sem("consts")
        w_loaded = sem("w_loaded")
        x_loaded = sem("x_loaded")
        bank_full = sem("bank_full")
        bank_free = sem("bank_free")
        vec = sem("vec")
        moments = sem("moments")
        rstd_ready = sem("rstd_ready")
        normed = sem("normed")
        logits_ready = sem("logits_ready")
        exp_done = sem("exp_done")
        onehot_ready = sem("onehot_ready")
        gelu_done = sem("gelu_done")
        out_stored = sem("out_stored")
        pool = sem("pool")
        block = ctx.enter_context(nc.Block())
        LOADS = 8

        @block.sync
        def _(sp):
            for dst, src in (
                    (enc_w[:], w["enc_w"].rearrange("(k p) n -> p k n", p=DM)),
                    (enc_b[:], w["enc_b"].rearrange("(r o) -> r o", o=1)),
                    (sw_w[:], w["sw_w"]),
                    (sw_b[:], w["sw_b"].partition_broadcast(P)),
                    (b1[:], w["eb1"].rearrange("(c a) r -> (a r) c", c=EC)),
                    (w2[:], w["ew2"].rearrange("(c a) r d -> (a r) c d", c=EC)),
                    (b2[:], w["eb2"])):
                sp.dma_start(dst, src, allow_slow_non_contiguous=True).then_inc(w_loaded, 16)
            for k in range(MT):
                sp.dma_start(w1[:, k, :, :], w["ew1"][:, k * DM:(k + 1) * DM, :].rearrange("e p r -> p e r")
                             ).then_inc(w_loaded, 16)
            with sp.Fori(0, B) as b:
                sp.wait_ge(bank_free, EX_JOBS * b + EX_BANKS)
                sp.dma_start(h[:], sorted_d.rearrange("(b n) d -> b n d", n=N)[bass.ds(b, 1), 0:S, :]
                             .rearrange("a (p t) d -> p (a t) d", t=T)).then_inc(x_loaded, 16)
                sp.dma_start(attn[:], state_d[bass.ds(b + STEPS - B, 1)].rearrange("a (p t) d -> p (a t) d", t=T)
                             ).then_inc(x_loaded, 16)
                sp.wait_ge(bank_free, EX_JOBS * (b + 1) + EX_BANKS)
                sp.dma_start(out[bass.ds(b, 1), 0:LAST * T, :].rearrange("a (p t) d -> p (a t) d", t=T),
                             result[0:LAST, :, :]).then_inc(out_stored, 16)
                sp.dma_start(out[bass.ds(b, 1), LAST * T:KEEP, :], result[LAST:LAST + 1, 0:FULL, :]
                             ).then_inc(out_stored, 16)
            sp.wait_ge(out_stored, 32 * B + 1)

        @block.gpsimd
        def _(gp):
            nc.gpsimd.memset(ident[:], 0.0).then_inc(pool, 1)
            nc.gpsimd.memset(spread[:], 1.0).then_inc(pool, 1)
            for e in range(E):
                nc.gpsimd.memset(first[:, e:e + 1], float(E - e)).then_inc(consts, 1)
            nc.gpsimd.memset(minus_half[:], -0.5).then_inc(consts, 1)
            nc.gpsimd.memset(eps[:], LN_EPS).then_inc(pool, 1)
            gp.wait_ge(pool, 3)
            nc.gpsimd.affine_select(out=ident[:], in_=ident[:], compare_op=ALU.not_equal, fill=1.0, base=0,
                                    pattern=[[-1, 128]], channel_multiplier=1).then_inc(consts, 1)
            nc.gpsimd.affine_select(out=spread[:], in_=spread[:], compare_op=ALU.is_ge, fill=0.0, base=0,
                                    pattern=[[1, E * R]], channel_multiplier=-R).then_inc(pool, 1)
            gp.wait_ge(pool, 4)
            nc.gpsimd.affine_select(out=spread[:], in_=spread[:], compare_op=ALU.is_ge, fill=0.0, base=R - 1,
                                    pattern=[[-1, E * R]], channel_multiplier=R).then_inc(consts, 1)
            with gp.Fori(0, B) as b:
                gp.wait_ge(moments, b + 1)
                nc.gpsimd.tensor_tensor(rstd[:], mean_var[:, :, 1], eps[:], ALU.add).then_inc(pool, 1)
                gp.wait_ge(pool, b + 5)
                nc.gpsimd.tensor_tensor(rstd[:], rstd[:], minus_half[:], ALU.pow).then_inc(rstd_ready, 1)

        @block.tensor
        def _(pe):
            def mm(out_, a, b_, start=True, stop=True):
                return nc.tensor.matmul(out_, a, b_, start=start, stop=stop)

            pe.wait_ge(w_loaded, 16 * (7 + MT))
            pe.wait_ge(consts, E + 3)
            with pe.Fori(0, B) as b:
                ring = Ring(EX_BANKS, b * EX_JOBS)

                def take():
                    bank, use = ring.take()
                    pe.wait_ge(bank_free, use)
                    return bank

                def copied():
                    pe.wait_ge(bank_free, ring.before + ring.count + EX_BANKS)

                pe.wait_ge(normed, T * (b + 1))
                for m in range(MT):
                    for half in range(2):
                        bank = take()
                        for t in range(3):
                            last = nc.tensor.transpose(job_ps[0:DM, bank, t * P:(t + 1) * P],
                                                       y[:, half * 3 + t, m * DM:(m + 1) * DM], ident[0:P, 0:P])
                        last.then_inc(bank_full, 1)
                copied()
                for half in range(2):
                    bank = take()
                    for k in range(MT):
                        last = mm(job_ps[0:R, bank, 0:HALF], enc_w[:, k, :], yT[:, k, half * HALF:(half + 1) * HALF],
                                  k == 0, k == 1)
                    last.then_inc(bank_full, 1)
                copied()
                bank = take()
                for t in range(T):
                    last = mm(job_ps[0:P, bank, t * E:(t + 1) * E], encT[:, t * P:(t + 1) * P], sw_w[:])
                last.then_inc(bank_full, 1)
                for c in range(EC):
                    for half in range(2):
                        bank = take()
                        for k in range(MT):
                            last = mm(job_ps[:, bank, 0:HALF],
                                      w1[:, k, 2 * c:2 * c + 2, :].rearrange("p a r -> p (a r)"),
                                      yT[:, k, half * HALF:(half + 1) * HALF], k == 0, k == 1)
                        last.then_inc(bank_full, 1)
                pe.wait_ge(onehot_ready, b + 1)
                for half in range(2):
                    bank = take()
                    for t in range(3):
                        last = nc.tensor.transpose(job_ps[0:E, bank, t * P:(t + 1) * P], onehot[:, half * 3 + t, :],
                                                   ident[0:P, 0:P])
                    last.then_inc(bank_full, 1)
                copied()
                for c in range(EC):
                    for half in range(2):
                        bank = take()
                        mm(job_ps[:, bank, 0:HALF], spread[:, c * 128:(c + 1) * 128],
                           onehotT[:, half * HALF:(half + 1) * HALF]).then_inc(bank_full, 1)
                copied()
                for i in range(3):
                    bank = take()
                    for t in (2 * i, 2 * i + 1):
                        to = job_ps[0:P, bank, (t % 2) * D:(t % 2 + 1) * D]
                        for c in range(EC):
                            mm(to, hid[:, c, t * P:(t + 1) * P], w2[:, c, :], c == 0, False)
                        last = mm(to, onehotT[:, t * P:(t + 1) * P], b2[:], False, True)
                    last.then_inc(bank_full, 1)
                assert ring.count == EX_JOBS

        @block.scalar
        def _(act):
            with act.Fori(0, B) as b:
                act.wait_ge(logits_ready, b + 1)
                nc.scalar.activation(prob[:], logit[:], ACT.Exp).then_inc(exp_done, 1)
                act.wait_ge(bank_free, b * EX_JOBS + 7 + 2 * EC + EX_BANKS)
                nc.scalar.activation(hid[:], hid[:], ACT.Gelu).then_inc(gelu_done, 1)

        @block.vector
        def _(dve):
            nc.vector.memset(total[:], 0.0).then_inc(bank_free, EX_BANKS)
            nc.vector.memset(top[:], 0.0).then_inc(out_stored, 1)
            dve.wait_ge(out_stored, 1)
            dve.wait_ge(bank_free, EX_BANKS)
            dve.wait_ge(w_loaded, 16 * (7 + MT))
            dve.wait_ge(consts, E + 3)
            with dve.Fori(0, B) as b:
                ring = Ring(EX_BANKS, b * EX_JOBS)
                done = Tally(vec, b * EX_VEC)

                def link(instruction):
                    dve.wait_ge(vec, done.add(instruction))

                def full():
                    bank, use = ring.take()
                    dve.wait_ge(bank_full, use)
                    return bank

                def by_expert(v):
                    return v[:, :, None].broadcast_to([P, T, E])

                dve.wait_ge(x_loaded, 32 * (b + 1))
                link(nc.vector.tensor_tensor(h[:], h[:], attn[:], ALU.add))
                for t in range(T):
                    done.add(nc.vector.bn_stats(stats[:, t, :], h[:, t, :]))
                dve.wait_ge(vec, done.now())
                combine_stats(nc, dve, done, stats, mean_var, mean_gap, D).then_inc(moments, 1)
                dve.wait_ge(moments, b + 1)
                dve.wait_ge(rstd_ready, b + 1)
                for t in range(T):
                    nc.vector.tensor_scalar(y[:, t, :], h[:, t, :], mean_var[:, t, 0:1], rstd[:, t:t + 1],
                                            ALU.subtract, ALU.mult).then_inc(normed, 1)
                for m in range(MT):
                    for half in range(2):
                        bank = full()
                        nc.vector.tensor_copy(yT[:, m, half * HALF:(half + 1) * HALF],
                                              job_ps[0:DM, bank, 0:HALF]).then_inc(bank_free, 1)
                for half in range(2):
                    bank = full()
                    nc.vector.tensor_scalar(encT[:, half * HALF:(half + 1) * HALF], job_ps[0:R, bank, 0:HALF],
                                            enc_b[:, 0:1], None, ALU.add).then_inc(bank_free, 1)
                bank = full()
                nc.vector.tensor_tensor(logit[:], job_ps[0:P, bank, 0:T * E].rearrange("p (t e) -> p t e", e=E),
                                        sw_b[:, None, :].broadcast_to([P, T, E]), ALU.add).then_inc(bank_free, 1)
                dve.wait_ge(bank_free, ring.before + ring.count + EX_BANKS)
                link(nc.vector.tensor_reduce(top[:], logit[:], AX.X, ALU.max))
                nc.vector.tensor_tensor(logit[:], logit[:], by_expert(top), ALU.subtract).then_inc(logits_ready, 1)
                for c in range(EC):
                    for half in range(2):
                        bank = full()
                        nc.vector.tensor_scalar(hid[:, c, half * HALF:(half + 1) * HALF], job_ps[:, bank, 0:HALF],
                                                b1[:, c:c + 1], None, ALU.add).then_inc(bank_free, 1)
                dve.wait_ge(exp_done, b + 1)
                link(nc.vector.tensor_reduce(total[:], prob[:], AX.X, ALU.add))
                link(nc.vector.reciprocal(total[:], total[:]))
                link(nc.vector.tensor_tensor(prob[:], prob[:], by_expert(total), ALU.mult))
                link(nc.vector.tensor_reduce(prob_max[:], prob[:], AX.X, ALU.max))
                link(nc.vector.tensor_tensor(onehot[:], prob[:], by_expert(prob_max), ALU.is_equal))
                link(nc.vector.tensor_tensor(onehot[:], onehot[:], first[:, None, :].broadcast_to([P, T, E]), ALU.mult))
                link(nc.vector.tensor_reduce(top[:], onehot[:], AX.X, ALU.max))
                nc.vector.tensor_tensor(onehot[:], onehot[:], by_expert(top), ALU.is_equal).then_inc(onehot_ready, 1)
                for half in range(2):
                    bank = full()
                    nc.vector.tensor_copy(onehotT[:, half * HALF:(half + 1) * HALF],
                                          job_ps[0:E, bank, 0:HALF]).then_inc(bank_free, 1)
                dve.wait_ge(gelu_done, b + 1)
                for c in range(EC):
                    for half in range(2):
                        bank = full()
                        part = hid[:, c, half * HALF:(half + 1) * HALF]
                        nc.vector.tensor_tensor(part, part, job_ps[:, bank, 0:HALF], ALU.mult).then_inc(bank_free, 1)
                dve.wait_ge(out_stored, 32 * b + 1)
                for i in range(3):
                    bank = full()
                    for t in (2 * i, 2 * i + 1):
                        row = nc.vector.scalar_tensor_tensor(
                            out=result[:, t, :], in0=job_ps[0:P, bank, (t % 2) * D:(t % 2 + 1) * D],
                            scalar=prob_max[:, t:t + 1], in1=h[:, t, :], op0=ALU.mult, op1=ALU.add)
                        if t % 2:
                            row.then_inc(bank_free, 1)
                        else:
                            done.add(row)
                dve.wait_ge(bank_free, ring.before + ring.count + EX_BANKS)
                assert ring.count == EX_JOBS and done.count == EX_VEC, done.count


def audio_tower(nc, w, out):
    scores_d = nc.dram_tensor("scores_scratch", (B * XT, 128), F32, kind="Internal").ap()
    sorted_d = nc.dram_tensor("sorted_scratch", (B * N, D), F32, kind="Internal").ap()
    state_d = nc.dram_tensor("state_scratch", (SLOTS, S, D), F32, kind="Internal").ap()
    parts_d = nc.dram_tensor("parts_scratch", (3, 3, D, S), BF16, kind="Internal").ap()
    sort_tokens(nc, w["x"], w["tok_w"], w["tok_b"], scores_d, sorted_d, state_d)
    layers(nc, w, parts_d, state_d)
    experts(nc, w, sorted_d, state_d, out)


_INS = {
    "x": "x", "L0_tok_w": "tok_w", "L0_tok_b": "tok_b",
    "L0_attn_Wq": "Wq", "L0_attn_bq": "bq", "L0_attn_Wk": "Wk", "L0_attn_bk": "bk", "L0_attn_Wv": "Wv",
    "L0_attn_bv": "bv", "L0_attn_Wc": "Wc", "L0_attn_bc": "bc", "L0_attn_Wo": "Wo", "L0_attn_bo": "bo",
    "L0_attn_g1": "g1", "L0_attn_b1": "b1", "L0_attn_Wi": "Wi", "L0_attn_bi": "bi", "L0_attn_Wo2": "Wo2",
    "L0_attn_bo2": "bo2", "L0_attn_g2": "g2", "L0_attn_b2": "b2",
    "L0_ffn_enc_w": "enc_w", "L0_ffn_enc_b": "enc_b", "L0_ffn_sw_w": "sw_w", "L0_ffn_sw_b": "sw_b",
    "L0_ffn_w1": "ew1", "L0_ffn_b1": "eb1", "L0_ffn_w2": "ew2", "L0_ffn_b2": "eb2",
}
_OUTS = [((B, KEEP, D), "float32")]


def kernel(**inputs):
    import numpy as _np
    import concourse.bacc as _bacc
    from concourse import mybir as _mybir
    from concourse.bass_utils import run_bass_kernel_spmd as _run

    nc = _bacc.Bacc("TRN2", target_bir_lowering=False, num_devices=1)
    arrays, args = {}, {}
    for name, short in _INS.items():
        a = _np.ascontiguousarray(inputs[name])
        arrays[f"in_{name}_dram"] = a
        args[short] = nc.dram_tensor(f"in_{name}_dram", a.shape, _mybir.dt.from_np(a.dtype), kind="ExternalInput").ap()
    shape, dtype = _OUTS[0]
    out = nc.dram_tensor("out_0_dram", shape, _mybir.dt.from_np(_np.dtype(dtype)), kind="ExternalOutput").ap()
    audio_tower(nc, args, out)
    r = _run(nc, [arrays], core_ids=[0])
    return r.results[0]["out_0_dram"]
```

```python
from contextlib import ExitStack

import concourse.bass as bass
from concourse import mybir

ALU = mybir.AluOpType
ACT = mybir.ActivationFunctionType
F32 = mybir.dt.float32
BF16 = mybir.dt.bfloat16
I32 = mybir.dt.int32
AX = mybir.AxisListType

B, N, D = 8, 1024, 192
KEEP = int(round(N * 0.7))
L, H, DH = 4, 12, 16
F = 768
R, E = 64, 8
LN_EPS, BLOCK_EPS = 1e-5, 1e-12

T = 6
P = 120
S = T * P
HALF = S // 2
MT = 2
DM = D // MT
FM = F // 128
XT = N // 128
COS, DOT = 0, 1
GROUPS, GH = 3, 4
SPANS = GROUPS * 2
STEPS = L * B
SLOTS = STEPS + B + 1
Q_PARTS = (0, 0, 0, 1, 1, 2)
K_PARTS = (0, 1, 2, 0, 1, 0)
KQ = len(Q_PARTS) * DH
ROWS = KQ + 3
MAX_TILES = H * T * 2
MLP_OUT_AT = ((0, 3), (0, 4), (1, 4), (1, 5), (2, 1), (3, 0))
HIDDEN_AT = (0, 3, 5)
LAST = (KEEP - 1) // T
FULL = KEEP - LAST * T


JUNKS = 3


def kept(t):
    return P if t < FULL else LAST


class Tally:

    def __init__(self, sem, before=0):
        self.sem, self.before, self.count = sem, before, 0

    def add(self, instruction, by=1):
        instruction.then_inc(self.sem, by)
        self.count += by
        return self.before + self.count

    def now(self):
        return self.before + self.count


def max_tile_at(kind, gh, kt, i):
    if kind == COS and gh >= 2:
        first, count = 12 + ((gh - 2) * T + kt) * 4, 4
    elif kind == COS and gh == 1 and kt >= 3:
        first, count = (kt - 3) * 4, 4
    elif kind == DOT and gh < 2:
        first, count = 12 + 4 * T * 4 + (gh * T + kt) * 3, 3
    else:
        return None
    return first + i if i < count else None


def hidden_at(gh, kt):
    return ((gh - 2) * len(HIDDEN_AT) + HIDDEN_AT.index(kt)) if gh >= 2 and kt in HIDDEN_AT else None


class Ring:

    def __init__(self, depth, before=0, bank=0):
        self.depth, self.before, self.bank, self.count = depth, before, bank, 0

    def take(self):
        k = self.count
        self.count += 1
        return (self.bank + k) % self.depth, self.before + k + 1


def combine_stats(nc, dve, done, stats, mean_var, spread, width):
    def link(instruction):
        dve.wait_ge(done.sem, done.add(instruction))

    link(nc.vector.tensor_tensor(spread[:], stats[:, :, 1], stats[:, :, 4], ALU.subtract))
    link(nc.vector.tensor_tensor(spread[:], spread[:], spread[:], ALU.mult))
    link(nc.vector.tensor_tensor(mean_var[:, :, 0], stats[:, :, 1], stats[:, :, 4], ALU.add))
    link(nc.vector.tensor_scalar(mean_var[:, :, 0], mean_var[:, :, 0], 0.5, None, ALU.mult))
    link(nc.vector.tensor_tensor(mean_var[:, :, 1], stats[:, :, 2], stats[:, :, 5], ALU.add))
    link(nc.vector.tensor_scalar(mean_var[:, :, 1], mean_var[:, :, 1], 1.0 / width, None, ALU.mult))
    return nc.vector.scalar_tensor_tensor(out=mean_var[:, :, 1], in0=spread[:], scalar=0.25,
                                          in1=mean_var[:, :, 1], op0=ALU.mult, op1=ALU.add)


def sort_tokens(nc, x, tok_w, tok_b, scores_d, sorted_d, state_d):
    with ExitStack() as ctx:
        sb = lambda name, shape, dt=F32: ctx.enter_context(nc.sbuf_tensor("so_" + name, shape, dt))
        sem = lambda name: ctx.enter_context(nc.semaphore("so_" + name))
        x_all = sb("x", [128, B * XT, D])
        prod = sb("prod", [128, B * XT, D])
        w_bc = sb("w", [128, D])
        b_bc = sb("b", [128, 1])
        score = sb("score", [128, B * XT])
        score_row = sb("score_row", [128, B * N])
        scoreT = sb("scoreT", [B * XT, 128])
        junk = sb("junk", [128, JUNKS, N])
        before = sb("before", [128, 128])
        counts = sb("counts", [128, XT, 3])
        rank = sb("rank", [128, XT])
        first_row = sb("first_row", [128, B * XT])
        place = sb("place", [128, B * XT], I32)
        ident = sb("ident", [128, 128])
        kept_x = sb("kept", [P, B, T * D])
        stats = sb("stats", [P, T, 6])
        mean_var = sb("mean_var", [P, T, 2])
        mean_gap = sb("mean_gap", [P, T])
        eps = sb("eps", [P, T])
        rstd = sb("rstd", [P, T])
        minus_half = sb("minus_half", [P, T])
        turned = ctx.enter_context(nc.psum_tensor("so_turned", [128, 128], F32))

        consts = sem("consts")
        x_loaded = [sem(f"x_loaded{i}") for i in range(2)]
        scored = sem("scored")
        turned_done = sem("turned")
        row_ready = sem("row_ready")
        row_stored = sem("row_stored")
        row_loaded = sem("row_loaded")
        vec = sem("vec")
        ranked = sem("ranked")
        scattered = [sem(f"scattered{b}") for b in range(B)]
        kept_loaded = sem("kept_loaded")
        moments = sem("moments")
        rstd_ready = sem("rstd_ready")
        pool = sem("pool")
        normed = sem("normed")
        stored = sem("stored")

        block = ctx.enter_context(nc.Block())
        RANK_OPS = 3 * XT
        NORM_OPS = T + 6
        START = 5

        @block.sync
        def _(sp):
            sp.dma_start(w_bc[:], tok_w.rearrange("d o -> (o d)").partition_broadcast(128)).then_inc(x_loaded[0], 16)
            sp.dma_start(b_bc[:], tok_b.partition_broadcast(128)).then_inc(x_loaded[0], 16)
            for b in range(B):
                sp.dma_start(x_all[:, b * XT:(b + 1) * XT, :],
                             x[b].rearrange("(t p) d -> p t d", p=128)).then_inc(x_loaded[b * 2 // B], 16)
            sp.wait_ge(row_ready, 1)
            sp.dma_start(scores_d, scoreT[:]).then_inc(row_stored, 16)
            sp.wait_ge(row_stored, 16)
            sp.dma_start(score_row[:], scores_d.rearrange("a b -> (a b)").partition_broadcast(128)).then_inc(row_loaded, 16)

            def store(b):
                sp.wait_ge(normed, T * (b + 1))
                sp.dma_start(state_d[STEPS + b].rearrange("(p t) d -> p (t d)", t=T), kept_x[:, b, :]).then_inc(stored, 16)

            for b in range(B):
                sp.wait_ge(scattered[b], 16 * XT)
                if b:
                    sp.wait_ge(kept_loaded, 16 * b)
                sp.dma_start(kept_x[:, b, :], sorted_d[b * N:b * N + S].rearrange("(p t) d -> p (t d)", t=T)
                             ).then_inc(kept_loaded, 16)
                if b >= 3:
                    store(b - 3)
            for b in range(B - 3, B):
                store(b)
            sp.wait_ge(stored, 16 * B)

        @block.gpsimd
        def _(pool_e):
            nc.gpsimd.memset(ident[:], 0.0).then_inc(pool, 1)
            nc.gpsimd.memset(before[:], 1.0).then_inc(pool, 1)
            nc.gpsimd.memset(minus_half[:], -0.5).then_inc(consts, 1)
            nc.gpsimd.memset(eps[:], LN_EPS).then_inc(pool, 1)
            for b in range(B):
                nc.gpsimd.memset(first_row[:, b * XT:(b + 1) * XT], float(b * N)).then_inc(consts, 1)
            pool_e.wait_ge(pool, 3)
            nc.gpsimd.affine_select(out=ident[:], in_=ident[:], compare_op=ALU.not_equal, fill=1.0, base=0,
                                    pattern=[[-1, 128]], channel_multiplier=1).then_inc(consts, 1)
            nc.gpsimd.affine_select(out=before[:], in_=before[:], compare_op=ALU.is_gt, fill=0.0, base=0,
                                    pattern=[[-1, 128]], channel_multiplier=1).then_inc(consts, 1)

            def root(b):
                pool_e.wait_ge(moments, b + 1)
                nc.gpsimd.tensor_tensor(rstd[:], mean_var[:, :, 1], eps[:], ALU.add).then_inc(pool, 1)
                pool_e.wait_ge(pool, 4 + b)
                nc.gpsimd.tensor_tensor(rstd[:], rstd[:], minus_half[:], ALU.pow).then_inc(rstd_ready, 1)

            for b in range(B):
                pool_e.wait_ge(ranked, b + 1)
                for t in range(XT):
                    k = b * XT + t
                    nc.gpsimd.indirect_dma_start(
                        out=sorted_d, out_offset=bass.IndirectOffsetOnAxis(ap=place[:, k:k + 1], axis=0),
                        in_=x_all[:, k, :], in_offset=None).then_inc(scattered[b], 16)
                if b >= 2:
                    root(b - 2)
            for b in range(B - 2, B):
                root(b)

        @block.tensor
        def _(pe):
            pe.wait_ge(scored, 1)
            pe.wait_ge(consts, B + 3)
            nc.tensor.transpose(turned[0:B * XT, :], score[:], ident[:]).then_inc(turned_done, 1)

        @block.vector
        def _(dve):
            nc.vector.memset(counts[:], 0.0).then_inc(vec, 1)
            for i in range(2):
                tiles = slice(i * B * XT // 2, (i + 1) * B * XT // 2)
                dve.wait_ge(x_loaded[i], 16 * (B // 2 + (2 if i == 0 else 0)))
                nc.vector.tensor_tensor(prod[:, tiles, :], x_all[:, tiles, :],
                                        w_bc[:, None, :].broadcast_to([128, B * XT // 2, D]), ALU.mult).then_inc(vec, 1)
                dve.wait_ge(vec, 2 * i + 2)
                nc.vector.tensor_reduce(score[:, tiles], prod[:, tiles, :], AX.X, ALU.add).then_inc(vec, 1)
            dve.wait_ge(vec, START)
            nc.vector.tensor_scalar(score[:], score[:], b_bc[:, 0:1], None, ALU.add).then_inc(scored, 1)
            dve.wait_ge(turned_done, 1)
            nc.vector.tensor_copy(scoreT[:], turned[0:B * XT, :]).then_inc(row_ready, 1)
            dve.wait_ge(row_loaded, 16)
            dve.wait_ge(consts, B + 3)
            dve.wait_ge(scored, 1)

            def rank_batch(b, before_ops):
                done = Tally(vec, before_ops)
                row = b * N

                def spare():
                    if done.count >= JUNKS:
                        dve.wait_ge(vec, done.now() - JUNKS + 1)
                    return junk[:, done.count % JUNKS, :]

                for t in range(XT):
                    s = score[:, bass.ds(b * XT + t, 1)]
                    if t:
                        done.add(nc.vector.tensor_scalar(spare()[:, 0:128 * t], score_row[:, bass.ds(row, 128 * t)], s, 0.0,
                                                         ALU.is_ge, ALU.add, accum_out=counts[:, t, 0:1]))
                    done.add(nc.vector.tensor_scalar(spare()[:, 0:N - 128 * t],
                                                     score_row[:, bass.ds(row + 128 * t, N - 128 * t)], s, 0.0,
                                                     ALU.is_gt, ALU.add, accum_out=counts[:, t, 1:2]))
                    done.add(nc.vector.scalar_tensor_tensor(
                        out=spare()[:, 0:128], in0=score_row[:, bass.ds(row + 128 * t, 128)], scalar=s, in1=before[:],
                        op0=ALU.is_equal, op1=ALU.mult, accum_out=counts[:, t, 2:3]))
                dve.wait_ge(vec, done.now())
                done.add(nc.vector.tensor_reduce(rank[:], counts[:], AX.X, ALU.add))
                dve.wait_ge(vec, done.now())
                nc.vector.tensor_tensor(place[:, bass.ds(b * XT, XT)], rank[:], first_row[:, bass.ds(b * XT, XT)],
                                        ALU.add).then_inc(ranked, 1)
                dve.wait_ge(ranked, b + 1)
                assert done.count == RANK_OPS

            def row_moments(b, before_ops):
                done = Tally(vec, before_ops)
                dve.wait_ge(kept_loaded, 16 * (b + 1))
                for t in range(T):
                    done.add(nc.vector.bn_stats(stats[:, t, :], rows_of(b, t)))
                dve.wait_ge(vec, done.now())
                combine_stats(nc, dve, done, stats, mean_var, mean_gap, D).then_inc(moments, 1)
                dve.wait_ge(moments, b + 1)
                assert done.count == NORM_OPS

            def norm_rows(b):
                dve.wait_ge(rstd_ready, b + 1)
                for t in range(T):
                    nc.vector.tensor_scalar(rows_of(b, t), rows_of(b, t), mean_var[:, t, 0:1], rstd[:, t:t + 1],
                                            ALU.subtract, ALU.mult).then_inc(normed, 1)
                dve.wait_ge(normed, T * (b + 1))

            def rows_of(b, t):
                return kept_x[:, bass.ds(b, 1), t * D:(t + 1) * D].rearrange("p a d -> p (a d)")

            with dve.Fori(0, 3) as b:
                rank_batch(b, b * RANK_OPS + START)
            row_moments(0, 3 * RANK_OPS + START)
            with dve.Fori(3, B) as b:
                rank_batch(b, b * (RANK_OPS + NORM_OPS) + START - 2 * NORM_OPS)
                norm_rows(b - 3)
                row_moments(b - 2, b * (RANK_OPS + NORM_OPS) + START - 2 * NORM_OPS + RANK_OPS)
            norm_rows(B - 3)
            for b in range(B - 2, B):
                row_moments(b, B * RANK_OPS + b * NORM_OPS + START)
                norm_rows(b)


SPAN_UNITS = T * 2
STEP_UNITS = 2 * SPANS * SPAN_UNITS
STEP_TILES = 2 * SPANS * T
STEP_SPANS = 2 * SPANS
PRO_JOBS = 4 + T + 4 + 4 + 4
TAIL_JOBS = 4 + 3 + 4 + FM * 2 + T
STEP_JOBS = PRO_JOBS + TAIL_JOBS + STEP_SPANS + MAX_TILES + GROUPS
MAX_DONE_AT = ((COS, 3, 4), (DOT, 0, 0), (DOT, 1, 5))
MAX_TURNED_AT = ((COS, 4, 0), (DOT, 0, 2), (DOT, 2, 1))
assert sum(max_tile_at(k, g, t, i) is not None
           for k in (COS, DOT) for g in range(SPANS) for t in range(T) for i in range(4)) == MAX_TILES


def jobs_at(kind, gh, kt):
    n = sum(max_tile_at(kind, gh, kt, i) is not None for i in range(4)) + (kt == 2) + ((kind, gh, kt) in MAX_TURNED_AT)
    if kind == COS:
        n += {(0, 3): 4, (0, 4): 2, (0, 5): 1, (1, 4): 4}.get((gh, kt), 0) + (hidden_at(gh, kt) is not None)
    else:
        n += {(1, 1): 2, (1, 3): 2, (2, 3): 4, (4, 3): 2, (4, 5): 2}.get((gh, kt), 0) + ((gh, kt) in MLP_OUT_AT)
    return n


def jobs_through(kind, gh, kt):
    order = [(s, g, t) for s in (COS, DOT) for g in range(SPANS) for t in range(T)]
    n = sum(jobs_at(*at) for at in order[:order.index((kind, gh, kt)) + 1])
    return n + (4 + T if kind == DOT else 0)


UNIT_CREDIT, TILE_CREDIT, OUT_CREDIT = 2, 3, 1
BANKS = BANK_CREDIT = 3
VEC_PRO, VEC_STEP = 18, 67
N_PROJ, N_FFN = 9, 13
assert STEP_JOBS % BANKS == 0 and jobs_through(DOT, SPANS - 1, T - 1) == STEP_JOBS


def layers(nc, w, parts_d, state_d):
    with ExitStack() as ctx:
        sb = lambda name, shape, dt=F32: ctx.enter_context(nc.sbuf_tensor("la_" + name, shape, dt))
        sem = lambda name: ctx.enter_context(nc.semaphore("la_" + name))
        q_stack = sb("q_stack", [ROWS, H, S], BF16)
        k_stack = sb("k_stack", [ROWS, H, S], BF16)
        c_stack = sb("c_stack", [KQ, H, S], BF16)
        d_stack = sb("d_stack", [KQ, H, S], BF16)
        prob = sb("prob", [P, 3, GH, HALF])
        x_in = sb("x_in", [P, T, D])
        resid = sb("resid", [P, T, D])
        x1 = sb("x1", [P, T, D])
        xT = sb("xT", [DM, MT, S])
        featT = sb("featT", [DM, MT, S])
        ctxt = sb("ctx", [P, T, D])
        partial = sb("partial", [P, 3, GH * DH])
        hid = sb("hid", [128, FM, S])
        c_tok = sb("c_tok", [P, T, D])
        v_next = sb("v_next", [P, T, D])
        v_aug = sb("v_aug", [P, T, H, 32])
        o_sb = sb("o_sb", [128, HALF])
        opT = sb("opT", [128, MT * S])
        part = [sb(f"part{i}", [DM, MT, S], BF16) for i in range(3)]
        wq, wk, wo = (sb(n, [DM, MT, D]) for n in ("wq", "wk", "wo"))
        wcv = sb("wcv", [DM, MT, 2 * D])
        wi = sb("wi", [DM, MT, F])
        wo2 = sb("wo2", [128, FM, D])
        bcv = sb("bcv", [P, 2 * D])
        bq_col, bk_col, g1_col, b1_col = (sb(n, [DM, MT]) for n in ("bq_col", "bk_col", "g1_col", "b1_col"))
        bi_col = sb("bi_col", [128, FM])
        bo, g1, b1, bo2, g2, b2 = (sb(n, [P, D]) for n in ("bo", "g1", "b1", "bo2", "g2", "b2"))
        ident = sb("ident", [128, 128])
        ident16 = sb("ident16", [128, 128], BF16)
        minus_ident = sb("minus_ident", [128, 128], BF16)
        minus_half = sb("minus_half", [P, T * H])
        neg_max = sb("neg_max", [P, GROUPS, 2, T * GH])
        max_part = sb("max_part", [P, 2 * T - 1, 3, GH], BF16)
        maxT = sb("maxT", [3 * GH, GROUPS, S], BF16)
        recip = sb("recip", [P, 3, GH])
        stats = sb("stats", [P, T, 6])
        mean_var = sb("mean_var", [P, T, 2])
        mean_gap = sb("mean_gap", [P, T])
        eps = sb("eps", [P, T])
        rstd = sb("rstd", [P, T])
        c_norm = sb("c_norm", [P, T * H])

        score_ps = ctx.enter_context(nc.psum_tensor("la_score", [128, GH, 512], F32))
        out_ps = ctx.enter_context(nc.psum_tensor("la_out", [128, 512], F32))
        job_ps = ctx.enter_context(nc.psum_tensor("la_job", [128, BANKS, 512], F32))
        job16 = job_ps[:, :, :].bitcast(BF16)

        consts = sem("consts")
        proj_loaded = sem("proj_loaded")
        ffn_loaded = sem("ffn_loaded")
        qk_loaded = sem("qk_loaded")
        c_loaded = sem("c_loaded")
        m_loaded = [sem(f"m_loaded{g}") for g in range(GROUPS)]
        parts_stored = sem("parts_stored")
        x_stored = sem("x_stored")
        scores_ready = sem("scores_ready")
        exp_done = sem("exp_done")
        pv_done = sem("pv_done")
        o_copied = sem("o_copied")
        bank_full = sem("bank_full")
        bank_free = sem("bank_free")
        vec = sem("vec")
        v_ready = sem("v_ready")
        parts_ready = sem("parts_ready")
        max_ready = sem("max_ready")
        moments1 = sem("moments1")
        moments2 = sem("moments2")
        rstd1 = sem("rstd1")
        rstd2 = sem("rstd2")
        normed1 = sem("normed1")
        normed2 = sem("normed2")
        resid_in = sem("resid_in")
        resid_mid = sem("resid_mid")
        x_out = sem("x_out")
        ctx_ready = sem("ctx_ready")
        squares = sem("squares")
        c_norm_ready = sem("c_norm_ready")
        c_unit = sem("c_unit")
        gelu_done = sem("gelu_done")
        pool = sem("pool")

        block = ctx.enter_context(nc.Block())

        def slot_of_input(n):
            return (n + STEPS) % (STEPS + B)

        def slot_of_output(n):
            return (n + SLOTS - 1) % SLOTS

        def job_base(n):
            return n * STEP_JOBS + PRO_JOBS

        @block.sync
        def _(sp):
            def load_projection(layer, slot):
                y = layer
                for dst, src in (
                        (wq[:], w["Wq"][y].rearrange("a (k p) n -> p (a k) n", p=DM)),
                        (wk[:], w["Wk"][y].rearrange("a (k p) n -> p (a k) n", p=DM)),
                        (wcv[:, :, 0:D], w["Wc"][y].rearrange("a (k p) n -> p (a k) n", p=DM)),
                        (wcv[:, :, D:2 * D], w["Wv"][y].rearrange("a (k p) n -> p (a k) n", p=DM)),
                        (bcv[:, 0:D], w["bc"][y].rearrange("a d -> (a d)").partition_broadcast(P)),
                        (bcv[:, D:2 * D], w["bv"][y].rearrange("a d -> (a d)").partition_broadcast(P)),
                        (bq_col[:], w["bq"][y].rearrange("a (k p) -> p (a k)", p=DM)),
                        (bk_col[:], w["bk"][y].rearrange("a (k p) -> p (a k)", p=DM)),
                        (x_in[:], state_d[slot].rearrange("a (p t) d -> p (a t) d", t=T))):
                    sp.dma_start(dst, src, allow_slow_non_contiguous=True).then_inc(proj_loaded, 16)

            def load_mlp(layer, slot):
                y = layer
                for dst, src in (
                        (wo[:], w["Wo"][y].rearrange("a (k p) n -> p (a k) n", p=DM)),
                        (wi[:], w["Wi"][y].rearrange("a (k p) n -> p (a k) n", p=DM)),
                        (wo2[:], w["Wo2"][y].rearrange("a (k p) n -> p (a k) n", p=128)),
                        *((tile[:], w[name][y].rearrange("a d -> (a d)").partition_broadcast(P))
                          for tile, name in ((bo, "bo"), (g1, "g1"), (b1, "b1"), (bo2, "bo2"))),
                        (g1_col[:], w["g1"][y].rearrange("a (k p) -> p (a k)", p=DM)),
                        (b1_col[:], w["b1"][y].rearrange("a (k p) -> p (a k)", p=DM)),
                        (bi_col[:], w["bi"][y].rearrange("a (k p) -> p (a k)", p=128)),
                        (resid[:], state_d[slot].rearrange("a (p t) d -> p (a t) d", t=T))):
                    sp.dma_start(dst, src, allow_slow_non_contiguous=True).then_inc(ffn_loaded, 16)

            def load_last_norm(layer):
                for tile, name in ((g2, "g2"), (b2, "b2")):
                    sp.dma_start(tile[:], w[name][layer].rearrange("a d -> (a d)").partition_broadcast(P)
                                 ).then_inc(ffn_loaded, 16)

            def store_parts(operand, count):
                sp.wait_ge(parts_ready, count)
                for i in range(3):
                    sp.dma_start(parts_d[operand, i].rearrange("(m p) s -> p m s", p=DM),
                                 part[i][:]).then_inc(parts_stored, 16)

            def load_stack(stack, operand, order, loaded):
                for i, p in enumerate(order):
                    sp.dma_start(stack[i * DH:(i + 1) * DH, :, :],
                                 parts_d[operand, p].rearrange("(h d) s -> d h s", d=DH)).then_inc(loaded, 16)

            def load_max(n, g):
                sp.wait_ge(bank_free, job_base(n) + jobs_through(*MAX_TURNED_AT[g]) + BANK_CREDIT)
                for i in range(3):
                    sp.dma_start(q_stack[KQ + i:KQ + i + 1, g * GH:(g + 1) * GH, :],
                                 maxT[i * GH:(i + 1) * GH, g, :]).then_inc(m_loaded[g], 16)

            load_projection(bass.ds(0, 1), bass.ds(STEPS, 1))
            load_mlp(bass.ds(0, 1), bass.ds(STEPS, 1))
            load_last_norm(bass.ds(0, 1))
            store_parts(0, 1)
            store_parts(1, 2)
            sp.wait_ge(parts_stored, 16 * 6)
            load_stack(c_stack, 1, Q_PARTS, c_loaded)
            load_stack(d_stack, 1, K_PARTS, c_loaded)
            store_parts(2, 3)
            with sp.Fori(0, STEPS) as n:
                sp.wait_ge(pv_done, n * STEP_TILES + TILE_CREDIT)
                load_stack(q_stack, 0, Q_PARTS, qk_loaded)
                sp.wait_ge(parts_stored, 16 * 9 * (n + 1))
                load_stack(k_stack, 2, K_PARTS, qk_loaded)
                sp.wait_ge(x_stored, 16 * n + 1)
                sp.wait_ge(bank_free, job_base(n) + BANK_CREDIT)
                load_projection(bass.ds(((n + 1) // B) % L, 1), bass.ds(slot_of_input(n + 1), 1))
                load_max(n, 0)
                load_max(n, 1)
                store_parts(0, 3 * n + 4)
                load_max(n, 2)
                store_parts(1, 3 * n + 5)
                sp.wait_ge(scores_ready, n * STEP_UNITS + STEP_UNITS // 2)
                sp.wait_ge(parts_stored, 16 * (9 * n + 15))
                load_stack(c_stack, 1, Q_PARTS, c_loaded)
                load_stack(d_stack, 1, K_PARTS, c_loaded)
                sp.wait_ge(bank_free, job_base(n) + jobs_through(DOT, *MLP_OUT_AT[-1]) + BANK_CREDIT)
                load_mlp(bass.ds(n // B, 1), bass.ds(slot_of_input(n), 1))
                sp.wait_ge(x_out, n + 1)
                load_last_norm(bass.ds(n // B, 1))
                sp.dma_start(state_d[bass.ds(slot_of_output(n), 1)].rearrange("a (p t) d -> p (a t) d", t=T),
                             x1[:]).then_inc(x_stored, 16)
                store_parts(2, 3 * n + 6)
            sp.wait_ge(x_out, STEPS + 1)
            sp.dma_start(state_d[STEPS - 1].rearrange("(p t) d -> p t d", t=T), x1[:]).then_inc(x_stored, 16)
            sp.wait_ge(x_stored, 16 * (STEPS + 1) + 1)
            sp.wait_ge(parts_stored, 16 * 9 * (STEPS + 1))
            sp.wait_ge(c_loaded, 16 * 12 * (STEPS + 1))
            sp.wait_ge(proj_loaded, 16 * N_PROJ * (STEPS + 1))

        @block.tensor
        def _(pe):
            def mm(out, a, b, start=True, stop=True):
                return nc.tensor.matmul(out, a, b, start=start, stop=stop)

            def take(ring):
                bank, use = ring.take()
                pe.wait_ge(bank_free, use)
                return bank

            def turn_features(ring, src):
                for m in range(MT):
                    for half in range(2):
                        bank = take(ring)
                        for t in range(3):
                            last = nc.tensor.transpose(job_ps[0:DM, bank, t * P:(t + 1) * P],
                                                       src[:, half * 3 + t, m * DM:(m + 1) * DM], ident[0:P, 0:P])
                        last.then_inc(bank_full, 1)

            def project_cv(ring):
                for t in range(T):
                    bank = take(ring)
                    if t == 0:
                        pe.wait_ge(bank_free, ring.before + ring.count - 1 + BANK_CREDIT)
                    for k in range(MT):
                        last = mm(job_ps[0:P, bank, 0:2 * D], xT[:, k, t * P:(t + 1) * P], wcv[:, k, :], k == 0, k == 1)
                    last.then_inc(bank_full, 1)

            def project_t(ring, weights, m):
                for half in range(2):
                    bank = take(ring)
                    for k in range(MT):
                        last = mm(job_ps[0:DM, bank, 0:HALF], weights[:, k, m * DM:(m + 1) * DM],
                                  xT[:, k, half * HALF:(half + 1) * HALF], k == 0, k == 1)
                    last.then_inc(bank_full, 1)

            def scores(kind, tile, unit, gh, kt, pair):
                g, half = divmod(gh, 2)
                pe.wait_ge(exp_done, unit - 1 + UNIT_CREDIT)
                ks, qs, rows = (d_stack, c_stack, KQ) if kind == COS else (k_stack, q_stack, ROWS)
                for j in (2 * pair, 2 * pair + 1):
                    h = g * GH + j
                    diagonal = kind == COS and kt // 3 == half
                    last = mm(score_ps[0:P, j, 0:HALF], ks[0:rows, h, kt * P:(kt + 1) * P],
                              qs[0:rows, h, half * HALF:(half + 1) * HALF], True, not diagonal)
                    if diagonal:
                        at = (kt % 3) * P
                        last = mm(score_ps[0:P, j, at:at + P], ident16[0:P, 0:P], minus_ident[0:P, 0:P], False, True)
                last.then_inc(scores_ready, 1)

            def values(tile, span, gh, kt, v_parts=None):
                g = gh // 2
                if v_parts is not None:
                    pe.wait_ge(v_ready, v_parts)
                pe.wait_ge(exp_done, 2 * tile + 2 + UNIT_CREDIT)
                if kt == 0:
                    pe.wait_ge(o_copied, span + OUT_CREDIT)
                rows = kept(kt)
                for j in range(GH):
                    last = mm(out_ps[32 * j:32 * j + 32, 0:HALF], v_aug[0:rows, kt, g * GH + j, :],
                              prob[0:rows, kt % 3, j, :], kt == 0, kt == T - 1)
                last.then_inc(pv_done, 1)

            def turn_out(ring, copies):
                bank = take(ring)
                pe.wait_ge(o_copied, copies)
                for t in range(3):
                    last = nc.tensor.transpose(job_ps[0:P, bank, t * 128:(t + 1) * 128], o_sb[:, t * P:(t + 1) * P], ident[:])
                last.then_inc(bank_full, 1)

            def max_tile(ring, i):
                if i is None:
                    return
                h, qt, half = i // (2 * T), (i // 2) % T, i % 2
                bank = take(ring)
                if half == 0:
                    out, keys = job_ps[0:P, bank, 0:HALF], k_stack[0:KQ, h, 0:HALF]
                else:
                    out = job_ps[0:P, bank, 0:3 * LAST]
                    keys = k_stack[0:KQ, h, HALF:S].rearrange("p (t k) -> p t k", t=3)[:, :, 0:LAST]
                mm(out, q_stack[0:KQ, h, qt * P:(qt + 1) * P], keys).then_inc(bank_full, 1)

            def turn_max(ring, count):
                bank = take(ring)
                pe.wait_ge(max_ready, count)
                for t in range(T):
                    last = nc.tensor.transpose(job16[0:3 * GH * T, bank, t * P:(t + 1) * P],
                                               max_part[:, t:t + T, :, :].rearrange("p t a h -> p (t a h)"),
                                               ident16[0:P, 0:P])
                last.then_inc(bank_full, 1)

            def output_projection(ring, i):
                bank = take(ring)
                if i == 0:
                    pe.wait_ge(bank_free, ring.before + ring.count - 1 + BANK_CREDIT)
                for t in (2 * i, 2 * i + 1):
                    for k in range(MT):
                        last = mm(job_ps[0:P, bank, (t % 2) * D:(t % 2 + 1) * D], featT[:, k, t * P:(t + 1) * P],
                                  wo[:, k, :], k == 0, k == 1)
                last.then_inc(bank_full, 1)

            def mlp_in(ring, i, turned):
                m, half = divmod(i, 2)
                bank = take(ring)
                if i == 0:
                    pe.wait_ge(bank_free, ring.before + turned + BANK_CREDIT)
                for k in range(MT):
                    last = mm(job_ps[:, bank, 0:HALF], wi[:, k, m * 128:(m + 1) * 128],
                              featT[:, k, half * HALF:(half + 1) * HALF], k == 0, k == 1)
                last.then_inc(bank_full, 1)

            def mlp_out(ring, t, n):
                pe.wait_ge(gelu_done, n + 1)
                bank = take(ring)
                for k in range(FM):
                    last = mm(job_ps[0:P, bank, 0:D], hid[:, k, t * P:(t + 1) * P], wo2[:, k, :], k == 0, k == FM - 1)
                last.then_inc(bank_full, 1)

            ring = Ring(BANKS)
            pe.wait_ge(consts, 1)
            pe.wait_ge(proj_loaded, 16 * N_PROJ)
            turn_features(ring, x_in)
            project_cv(ring)
            for m in range(MT):
                project_t(ring, wq, m)
            pe.wait_ge(c_unit, 1)
            turn_features(ring, c_tok)
            for m in range(MT):
                project_t(ring, wk, m)
            assert ring.count == PRO_JOBS
            pe.wait_ge(c_loaded, 16 * 12)
            for pair in range(2):
                scores(COS, 0, pair, 0, 0, pair)

            with pe.Fori(0, STEPS) as n:
                ring = Ring(BANKS, job_base(n), PRO_JOBS % BANKS)
                for kind in (COS, DOT):
                    if kind == DOT:
                        pe.wait_ge(m_loaded[0], 16 * 3 * (n + 1))
                        for pair in range(2):
                            scores(DOT, 0, n * STEP_UNITS + STEP_UNITS // 2 + pair, 0, 0, pair)
                        pe.wait_ge(proj_loaded, 16 * N_PROJ * (n + 2))
                        turn_features(ring, x_in)
                        project_cv(ring)
                    for gh in range(SPANS):
                        span = n * STEP_SPANS + kind * SPANS + gh
                        for kt in range(T):
                            tile = n * STEP_TILES + (kind * SPANS + gh) * T + kt
                            unit = n * STEP_UNITS + ((kind * SPANS + gh) * T + kt) * 2
                            if kind == DOT and gh in (2, 4) and kt == 0:
                                pe.wait_ge(m_loaded[gh // 2], 16 * 3 * (n + 1))
                            if (kind, gh, kt) == (COS, 1, 3):
                                pe.wait_ge(qk_loaded, 16 * 12 * (n + 1))
                            first = gh == 0 and kt == 0
                            if not first:
                                scores(kind, tile, unit, gh, kt, 0)
                            max_tile(ring, max_tile_at(kind, gh, kt, 0))
                            if not first:
                                scores(kind, tile, unit + 1, gh, kt, 1)
                            max_tile(ring, max_tile_at(kind, gh, kt, 1))
                            if kt:
                                v_parts = 2 * n + kt if kind == COS and gh == 0 and kt <= 2 else None
                                values(tile - 1, span, gh, kt - 1, v_parts)
                            elif gh:
                                values(tile - 1, span - 1, gh - 1, T - 1)
                            max_tile(ring, max_tile_at(kind, gh, kt, 2))
                            if (kind, gh, kt) in MAX_TURNED_AT:
                                turn_max(ring, GROUPS * n + MAX_TURNED_AT.index((kind, gh, kt)) + 1)
                            if kt == 2:
                                turn_out(ring, span + OUT_CREDIT)
                            if kind == COS:
                                if gh == 0 and kt == 3:
                                    pe.wait_ge(ctx_ready, SPANS * n + 1)
                                    turn_features(ring, ctxt)
                                if gh == 0 and kt == 4:
                                    pe.wait_ge(ffn_loaded, 16 * N_FFN * (n + 1))
                                    output_projection(ring, 0)
                                    output_projection(ring, 1)
                                if gh == 0 and kt == 5:
                                    output_projection(ring, 2)
                                if hidden_at(gh, kt) is not None:
                                    mlp_in(ring, hidden_at(gh, kt), jobs_through(COS, 1, 4))
                                max_tile(ring, max_tile_at(kind, gh, kt, 3))
                                if gh == 1 and kt == 4:
                                    pe.wait_ge(normed1, T * (n + 1))
                                    turn_features(ring, x1)
                            else:
                                if (gh, kt) in MLP_OUT_AT:
                                    mlp_out(ring, MLP_OUT_AT.index((gh, kt)), n)
                                if gh == 1 and kt in (1, 3):
                                    project_t(ring, wq, kt // 2)
                                if gh == 2 and kt == 3:
                                    pe.wait_ge(c_unit, n + 2)
                                    turn_features(ring, c_tok)
                                if gh == 4 and kt in (3, 5):
                                    project_t(ring, wk, kt // 4)
                            assert ring.count == jobs_through(kind, gh, kt), (kind, gh, kt, ring.count)
                    if kind == DOT:
                        pe.wait_ge(c_loaded, 16 * 12 * (n + 2))
                        for pair in range(2):
                            scores(COS, 0, (n + 1) * STEP_UNITS + pair, 0, 0, pair)
                    last_tile = n * STEP_TILES + (kind + 1) * SPANS * T - 1
                    values(last_tile, n * STEP_SPANS + (kind + 1) * SPANS - 1, SPANS - 1, T - 1)
                assert ring.count == STEP_JOBS

            ring = Ring(BANKS, job_base(STEPS), PRO_JOBS % BANKS)
            turn_out(ring, STEP_SPANS * STEPS + OUT_CREDIT)
            pe.wait_ge(ctx_ready, SPANS * STEPS + 1)
            turn_features(ring, ctxt)
            pe.wait_ge(ffn_loaded, 16 * N_FFN * (STEPS + 1))
            for i in range(3):
                output_projection(ring, i)
            pe.wait_ge(normed1, T * (STEPS + 1))
            turn_features(ring, x1)
            turned = ring.count
            for i in range(2 * FM):
                mlp_in(ring, i, turned)
            for t in range(T):
                mlp_out(ring, t, STEPS)

        @block.scalar
        def _(act):
            with act.Fori(0, STEPS) as n:
                for kind in (COS, DOT):
                    if kind == DOT:
                        act.wait_ge(bank_free, job_base(n) + jobs_through(COS, SPANS - 1, T - 1) + BANK_CREDIT)
                        nc.scalar.activation(hid[:], hid[:], ACT.Gelu).then_inc(gelu_done, 1)
                    for gh in range(SPANS):
                        for kt in range(T):
                            tile = n * STEP_TILES + (kind * SPANS + gh) * T + kt
                            unit = n * STEP_UNITS + ((kind * SPANS + gh) * T + kt) * 2
                            for pair in range(2):
                                act.wait_ge(scores_ready, unit + pair + 1)
                                if pair == 0:
                                    act.wait_ge(pv_done, tile - 2 + TILE_CREDIT)
                                nc.scalar.activation(prob[:, kt % 3, 2 * pair:2 * pair + 2, :],
                                                     score_ps[0:P, 2 * pair:2 * pair + 2, 0:HALF], ACT.Exp,
                                                     scale=-1.0 if kind == COS else 1.0).then_inc(exp_done, 1)
            act.wait_ge(bank_free, job_base(STEPS) + 1 + 4 + 3 + 4 + 2 * FM + BANK_CREDIT)
            nc.scalar.activation(hid[:], hid[:], ACT.Gelu).then_inc(gelu_done, 1)

        @block.vector
        def _(dve):
            def full(ring):
                bank, use = ring.take()
                dve.wait_ge(bank_full, use)
                return bank

            def copy_turned(ring, dst, scale=None, bias=None):
                for m in range(MT):
                    for half in range(2):
                        bank = full(ring)
                        out, src = dst[0:DM, m, half * HALF:(half + 1) * HALF], job_ps[0:DM, bank, 0:HALF]
                        if scale is None:
                            nc.vector.tensor_copy(out, src).then_inc(bank_free, 1)
                        else:
                            nc.vector.tensor_scalar(out, src, scale[:, m:m + 1], bias[:, m:m + 1],
                                                    ALU.mult, ALU.add).then_inc(bank_free, 1)

            opT_view = opT[0:DM, :].rearrange("p (m s) -> p m s", m=MT)
            squares_view = opT[0:P, 0:T * D]

            def take_cv(ring):
                for t in range(T):
                    bank = full(ring)
                    done.add(nc.vector.tensor_tensor(c_tok[:, t, :], job_ps[0:P, bank, 0:D], bcv[:, 0:D], ALU.add))
                    nc.vector.tensor_tensor(v_next[:, t, :], job_ps[0:P, bank, D:2 * D], bcv[:, D:2 * D],
                                            ALU.add).then_inc(bank_free, 1)

            def square_c():
                dve.wait_ge(vec, done.now())
                c_flat = c_tok[:, :, :].rearrange("p t d -> p (t d)")
                done.add(nc.vector.tensor_tensor(squares_view, c_flat, c_flat, ALU.mult))

            def sum_squares():
                dve.wait_ge(vec, done.now())
                nc.vector.tensor_reduce(c_norm[:], squares_view.rearrange("p (h d) -> p h d", d=DH), AX.X,
                                        ALU.add).then_inc(squares, 1)

            def take_operand(ring, m, bias, factor):
                for half in range(2):
                    bank = full(ring)
                    nc.vector.tensor_scalar(opT_view[:, m, half * HALF:(half + 1) * HALF], job_ps[0:DM, bank, 0:HALF],
                                            bias[:, m:m + 1], factor, ALU.add, ALU.mult).then_inc(bank_free, 1)

            def split_high(free_before, copied):
                dve.wait_ge(bank_free, copied)
                dve.wait_ge(parts_stored, free_before)
                done.add(nc.vector.tensor_copy(part[0][:, :, :], opT_view))

            def split_off_high():
                dve.wait_ge(vec, done.now())
                done.add(nc.vector.tensor_tensor(opT_view, opT_view, part[0][:, :, :], ALU.subtract))

            def split_mid():
                dve.wait_ge(vec, done.now())
                done.add(nc.vector.tensor_copy(part[1][:, :, :], opT_view))

            def split_low():
                dve.wait_ge(vec, done.now())
                nc.vector.tensor_tensor(part[2][:, :, :], opT_view, part[1][:, :, :], ALU.subtract).then_inc(parts_ready, 1)

            def unit_c(count):
                dve.wait_ge(c_norm_ready, count)
                view = c_tok[:, :, :].rearrange("p t (h d) -> p (t h) d", d=DH)
                nc.vector.tensor_tensor(view, view, c_norm[:, :, None].broadcast_to([P, T * H, DH]),
                                        ALU.mult).then_inc(c_unit, 1)

            def place_v(count):
                dve.wait_ge(pv_done, count)
                for tiles in (slice(0, 1), slice(1, T)):
                    nc.vector.tensor_copy(v_aug[:, tiles, :, 0:DH].rearrange("p t h d -> p (t h) d"),
                                          v_next[:, tiles, :].rearrange("p t (h d) -> p (t h) d", d=DH)
                                          ).then_inc(v_ready, 1)

            def copy_out(span, gh):
                dve.wait_ge(pv_done, (span + 1) * T + TILE_CREDIT)
                nc.vector.tensor_copy(o_sb[:], out_ps[:, 0:HALF]).then_inc(o_copied, 1)

            def add_out(ring, kind, gh):
                g, half = divmod(gh, 2)
                bank = full(ring)
                sums = job_ps[0:P, bank, 0:3 * 128].rearrange("p (t j c) -> p t j c", t=3, j=GH)
                done.add(nc.vector.reciprocal(recip[:], sums[:, :, :, DH]))
                dve.wait_ge(vec, done.now())
                target = ctxt[:, half * 3:half * 3 + 3, g * GH * DH:(g + 1) * GH * DH]
                out = (target if kind == COS else partial[:, :, :]).rearrange("p t (j d) -> p t j d", d=DH)
                nc.vector.tensor_tensor(out, sums[:, :, :, 0:DH], recip[:, :, :, None].broadcast_to([P, 3, GH, DH]),
                                        ALU.mult).then_inc(bank_free, 1)
                dve.wait_ge(bank_free, ring.before + ring.count + BANK_CREDIT)
                if kind == DOT:
                    nc.vector.tensor_tensor(target, target, partial[:, :, :], ALU.add).then_inc(ctx_ready, 1)

            def take_rows(ring, tiles):
                bank = full(ring)
                rows = slice(tiles[0], tiles[-1] + 1)
                nc.vector.tensor_tensor(x1[:, rows, :],
                                        job_ps[0:P, bank, 0:len(tiles) * D].rearrange("p (t d) -> p t d", d=D),
                                        resid[:, rows, :], ALU.add).then_inc(bank_free, 1)
                dve.wait_ge(bank_free, ring.before + ring.count + BANK_CREDIT)
                for t in tiles:
                    done.add(nc.vector.bn_stats(stats[:, t, :], x1[:, t, :]))

            def row_moments(moments):
                dve.wait_ge(vec, done.now())
                combine_stats(nc, dve, done, stats, mean_var, mean_gap, D).then_inc(moments, 1)

            def norm_rows(moments, rstd_ready, normed, n):
                dve.wait_ge(moments, n + 1)
                dve.wait_ge(rstd_ready, n + 1)
                for t in range(T):
                    nc.vector.tensor_scalar(x1[:, t, :], x1[:, t, :], mean_var[:, t, 0:1], rstd[:, t:t + 1],
                                            ALU.subtract, ALU.mult).then_inc(normed, 1)

            def take_max(ring, i):
                if i is None:
                    return
                h, qt, half = i // (2 * T), (i // 2) % T, i % 2
                bank = full(ring)
                g, at = h // GH, qt * GH + h % GH
                nc.vector.tensor_reduce(neg_max[:, g, half, at:at + 1], job_ps[0:P, bank, 0:HALF if half == 0 else 3 * LAST],
                                        AX.X, ALU.max, negate=True).then_inc(bank_free, 1)

            def split_max(g):
                view = lambda i: neg_max[:, g, i, :].rearrange("p (t h) -> p t h", h=GH)
                dve.wait_ge(bank_free, ring.before + ring.count + BANK_CREDIT)
                done.add(nc.vector.tensor_tensor(view(0), view(0), view(1), ALU.min))
                for i in range(2):
                    dve.wait_ge(vec, done.now())
                    done.add(nc.vector.tensor_copy(max_part[:, 0:T, i, :], view(0)))
                    dve.wait_ge(vec, done.now())
                    done.add(nc.vector.tensor_tensor(view(0), view(0), max_part[:, 0:T, i, :], ALU.subtract))
                dve.wait_ge(vec, done.now())
                nc.vector.tensor_copy(max_part[:, 0:T, 2, :], view(0)).then_inc(max_ready, 1)

            def take_turned_max(ring, g):
                bank = full(ring)
                nc.vector.tensor_copy(maxT[:, g, :], job16[0:3 * GH, bank, 0:S]).then_inc(bank_free, 1)

            def take_hidden(ring, i):
                m, half = divmod(i, 2)
                bank = full(ring)
                nc.vector.tensor_scalar(hid[:, m, half * HALF:(half + 1) * HALF], job_ps[:, bank, 0:HALF],
                                        bi_col[:, m:m + 1], None, ALU.add).then_inc(bank_free, 1)

            done = Tally(vec)
            done.add(nc.vector.memset(v_aug[:], 0.0))
            dve.wait_ge(vec, done.now())
            nc.vector.memset(v_aug[:, :, :, DH:DH + 1], 2.0).then_inc(bank_free, BANK_CREDIT)
            nc.vector.memset(k_stack[KQ:ROWS, :, :], 1.0).then_inc(pv_done, TILE_CREDIT)
            nc.vector.memset(o_sb[:], 1.0).then_inc(o_copied, OUT_CREDIT)
            nc.vector.memset(ctxt[:], 0.0).then_inc(exp_done, UNIT_CREDIT)
            dve.wait_ge(exp_done, UNIT_CREDIT)
            done.add(nc.vector.memset(recip[:], 1.0))
            nc.vector.memset(max_part[:], 0.0).then_inc(x_stored, 1)
            dve.wait_ge(x_stored, 1)
            dve.wait_ge(consts, 1)
            dve.wait_ge(proj_loaded, 16 * N_PROJ)
            ring = Ring(BANKS)
            copy_turned(ring, xT)
            take_cv(ring)
            square_c()
            sum_squares()
            dve.wait_ge(squares, 1)
            for m in range(MT):
                take_operand(ring, m, bq_col, DH ** -0.5)
            split_high(0, ring.count + BANK_CREDIT)
            split_off_high()
            split_mid()
            split_low()
            unit_c(1)
            dve.wait_ge(parts_ready, 1)
            copy_turned(ring, opT_view)
            split_high(16 * 3, ring.count + BANK_CREDIT)
            split_off_high()
            split_mid()
            split_low()
            dve.wait_ge(parts_ready, 2)
            for m in range(MT):
                take_operand(ring, m, bk_col, 1.0)
            split_high(16 * 6, ring.count + BANK_CREDIT)
            split_off_high()
            split_mid()
            split_low()
            place_v(TILE_CREDIT)
            assert ring.count == PRO_JOBS and done.count == VEC_PRO, done.count

            with dve.Fori(0, STEPS) as n:
                ring = Ring(BANKS, job_base(n), PRO_JOBS % BANKS)
                done = Tally(vec, n * VEC_STEP + VEC_PRO)
                for kind in (COS, DOT):
                    if kind == DOT:
                        copy_turned(ring, xT)
                        dve.wait_ge(parts_ready, 3 * n + 3)
                        take_cv(ring)
                    for gh in range(SPANS):
                        span = n * STEP_SPANS + kind * SPANS + gh
                        for kt in range(T):
                            take_max(ring, max_tile_at(kind, gh, kt, 0))
                            take_max(ring, max_tile_at(kind, gh, kt, 1))
                            if kt == 0 and gh:
                                copy_out(span - 1, gh - 1)
                            take_max(ring, max_tile_at(kind, gh, kt, 2))
                            if (kind, gh, kt) in MAX_TURNED_AT:
                                take_turned_max(ring, MAX_TURNED_AT.index((kind, gh, kt)))
                            if kt == 2:
                                before_kind, before_gh = (kind, gh - 1) if gh else (1 - kind, SPANS - 1)
                                add_out(ring, before_kind, before_gh)
                            if kind == COS:
                                if gh == 0 and kt == 3:
                                    dve.wait_ge(ctx_ready, SPANS * n + 1)
                                    copy_turned(ring, featT)
                                if gh == 0 and kt == 4:
                                    dve.wait_ge(resid_in, n + 1)
                                    dve.wait_ge(x_stored, 16 * n + 1)
                                    take_rows(ring, (0, 1))
                                    take_rows(ring, (2, 3))
                                if gh == 0 and kt == 5:
                                    take_rows(ring, (4, 5))
                                if hidden_at(gh, kt) is not None:
                                    take_hidden(ring, hidden_at(gh, kt))
                                take_max(ring, max_tile_at(kind, gh, kt, 3))
                                if gh == 1 and kt == 0:
                                    row_moments(moments1)
                                if gh == 1 and kt == 2:
                                    norm_rows(moments1, rstd1, normed1, n)
                                if gh == 1 and kt == 4:
                                    copy_turned(ring, featT, g1_col, b1_col)
                            else:
                                if gh == 0 and kt == 3:
                                    dve.wait_ge(resid_mid, n + 1)
                                    square_c()
                                if gh == 0 and kt == 4:
                                    sum_squares()
                                if (gh, kt) in MLP_OUT_AT:
                                    take_rows(ring, (MLP_OUT_AT.index((gh, kt)),))
                                if gh == 1 and kt in (1, 3):
                                    if kt == 1:
                                        dve.wait_ge(squares, n + 2)
                                    take_operand(ring, kt // 2, bq_col, DH ** -0.5)
                                if gh == 1 and kt == 3:
                                    split_high(16 * 9 * (n + 1), ring.before + ring.count + BANK_CREDIT)
                                if gh == 1 and kt == 4:
                                    split_off_high()
                                if gh == 1 and kt == 5:
                                    split_mid()
                                if gh == 2 and kt == 0:
                                    split_low()
                                if gh == 2 and kt == 1:
                                    unit_c(n + 2)
                                if gh == 2 and kt == 3:
                                    dve.wait_ge(parts_ready, 3 * n + 4)
                                    copy_turned(ring, opT_view)
                                if gh == 2 and kt == 5:
                                    split_high(16 * (9 * n + 12), ring.before + ring.count + BANK_CREDIT)
                                    split_off_high()
                                if gh == 3 and kt == 1:
                                    split_mid()
                                    split_low()
                                if gh == 3 and kt == 5:
                                    row_moments(moments2)
                                if gh == 4 and kt == 2:
                                    norm_rows(moments2, rstd2, normed2, n)
                                if gh == 4 and kt in (3, 5):
                                    if kt == 3:
                                        dve.wait_ge(parts_ready, 3 * n + 5)
                                    take_operand(ring, kt // 4, bk_col, 1.0)
                                if gh == 5 and kt == 1:
                                    split_high(16 * (9 * n + 15), ring.before + ring.count + BANK_CREDIT)
                                    split_off_high()
                                if gh == 5 and kt == 3:
                                    split_mid()
                                    split_low()
                            if (kind, gh, kt) in MAX_DONE_AT:
                                split_max(MAX_DONE_AT.index((kind, gh, kt)))
                    copy_out(n * STEP_SPANS + (kind + 1) * SPANS - 1, SPANS - 1)
                place_v((n + 1) * STEP_TILES + TILE_CREDIT)
                assert ring.count == STEP_JOBS and done.count == VEC_STEP, done.count

            ring = Ring(BANKS, job_base(STEPS), PRO_JOBS % BANKS)
            done = Tally(vec, STEPS * VEC_STEP + VEC_PRO)
            add_out(ring, DOT, SPANS - 1)
            dve.wait_ge(ctx_ready, SPANS * STEPS + 1)
            copy_turned(ring, featT)
            dve.wait_ge(resid_in, STEPS + 1)
            dve.wait_ge(x_stored, 16 * STEPS + 1)
            for t in range(0, T, 2):
                take_rows(ring, (t, t + 1))
            row_moments(moments1)
            norm_rows(moments1, rstd1, normed1, STEPS)
            copy_turned(ring, featT, g1_col, b1_col)
            for i in range(2 * FM):
                take_hidden(ring, i)
            dve.wait_ge(resid_mid, STEPS + 1)
            for t in range(T):
                take_rows(ring, (t,))
            row_moments(moments2)
            norm_rows(moments2, rstd2, normed2, STEPS)

        @block.gpsimd
        def _(gp):
            order = Tally(pool)

            def after(instruction):
                gp.wait_ge(pool, order.add(instruction))

            def input_residual(n):
                gp.wait_ge(ffn_loaded, 16 * N_FFN * (n + 1))
                nc.gpsimd.tensor_tensor(resid[:], resid[:], bo[:, None, :].broadcast_to([P, T, D]),
                                        ALU.add).then_inc(resid_in, 1)

            def root(moments, ready, n):
                gp.wait_ge(moments, n + 1)
                after(nc.gpsimd.tensor_tensor(rstd[:], mean_var[:, :, 1], eps[:], ALU.add))
                nc.gpsimd.tensor_tensor(rstd[:], rstd[:], minus_half[:, 0:T], ALU.pow).then_inc(ready, 1)

            def middle_residual(n):
                gp.wait_ge(normed1, T * (n + 1))
                gp.wait_ge(resid_in, n + 1)
                after(nc.gpsimd.tensor_tensor(resid[:], x1[:], g1[:, None, :].broadcast_to([P, T, D]), ALU.mult))
                after(nc.gpsimd.tensor_tensor(resid[:], resid[:], b1[:, None, :].broadcast_to([P, T, D]), ALU.add))
                nc.gpsimd.tensor_tensor(resid[:], resid[:], bo2[:, None, :].broadcast_to([P, T, D]),
                                        ALU.add).then_inc(resid_mid, 1)

            def c_root(n):
                gp.wait_ge(squares, n + 1)
                nc.gpsimd.tensor_tensor(c_norm[:], c_norm[:], minus_half[:], ALU.pow).then_inc(c_norm_ready, 1)

            def result(n):
                gp.wait_ge(normed2, T * (n + 1))
                after(nc.gpsimd.tensor_tensor(x1[:], x1[:], g2[:, None, :].broadcast_to([P, T, D]), ALU.mult))
                nc.gpsimd.tensor_tensor(x1[:], x1[:], b2[:, None, :].broadcast_to([P, T, D]), ALU.add).then_inc(x_out, 1)

            after(nc.gpsimd.memset(ident[:], 0.0))
            after(nc.gpsimd.memset(minus_half[:], -0.5))
            after(nc.gpsimd.memset(eps[:], BLOCK_EPS))
            after(nc.gpsimd.affine_select(out=ident[:], in_=ident[:], compare_op=ALU.not_equal, fill=1.0, base=0,
                                          pattern=[[-1, 128]], channel_multiplier=1))
            after(nc.gpsimd.tensor_copy(ident16[:], ident[:]))
            nc.gpsimd.tensor_scalar(minus_ident[:], ident[:], -1.0, None, ALU.mult).then_inc(consts, 1)
            c_root(0)
            start = order.count
            with gp.Fori(0, STEPS) as n:
                order = Tally(pool, start + 5 * n)
                input_residual(n)
                root(moments1, rstd1, n)
                middle_residual(n)
                c_root(n + 1)
                root(moments2, rstd2, n)
                result(n)
                assert order.count == 5
            order = Tally(pool, start + 5 * STEPS)
            input_residual(STEPS)
            root(moments1, rstd1, STEPS)
            middle_residual(STEPS)
            root(moments2, rstd2, STEPS)
            result(STEPS)


EC = E * R // 128
TURN_JOBS = 4
EX_JOBS = 2 + 1 + 2 * EC + 2 + TURN_JOBS + 2 * EC + 3
EX_VEC_NORM, EX_VEC = 12, 23
EX_BANKS = 7
assert EX_JOBS % EX_BANKS == 0


def experts(nc, w, sorted_d, state_d, out):
    with ExitStack() as ctx:
        sb = lambda name, shape, dt=F32: ctx.enter_context(nc.sbuf_tensor("ex_" + name, shape, dt))
        sem = lambda name: ctx.enter_context(nc.semaphore("ex_" + name))
        h = sb("h", [P, 2 * T, D])
        attn = sb("attn", [P, T, D])
        y = sb("y", [P, T, D])
        yT = sb("yT", [DM, MT, S])
        result = sb("result", [P, T, D])
        enc_w = sb("enc_w", [DM, MT, R])
        enc_b = sb("enc_b", [R, 1])
        sw_w = sb("sw_w", [R, E])
        sw_b = sb("sw_b", [P, E])
        w1 = sb("w1", [DM, MT, E, R])
        b1 = sb("b1", [128, EC])
        w2 = sb("w2", [128, EC, D])
        b2 = sb("b2", [E, D])
        encT = sb("encT", [R, S])
        logit = sb("logit", [P, T, E])
        top = sb("top", [P, T])
        total = sb("total", [P, T])
        prob = sb("prob", [P, T, E])
        prob_max = sb("prob_max", [P, T])
        first = sb("first", [P, E])
        onehot = sb("onehot", [P, T, E])
        onehotT = sb("onehotT", [E, S])
        spread = sb("spread", [E, E * R])
        hid = sb("hid", [128, EC, S])
        ident = sb("ident", [128, 128])
        stats = sb("stats", [P, T, 6])
        mean_var = sb("mean_var", [P, T, 2])
        mean_gap = sb("mean_gap", [P, T])
        eps = sb("eps", [P, T])
        rstd = sb("rstd", [P, T])
        minus_half = sb("minus_half", [P, T])
        job_ps = ctx.enter_context(nc.psum_tensor("ex_job", [128, EX_BANKS, 512], F32))

        consts = sem("consts")
        w_loaded = sem("w_loaded")
        x_loaded = sem("x_loaded")
        added = sem("added")
        bank_full = sem("bank_full")
        bank_free = sem("bank_free")
        vec = sem("vec")
        moments = sem("moments")
        rstd_ready = sem("rstd_ready")
        normed = sem("normed")
        logits_ready = sem("logits_ready")
        exp_done = sem("exp_done")
        onehot_ready = sem("onehot_ready")
        gelu_done = sem("gelu_done")
        out_stored = sem("out_stored")
        pool = sem("pool")
        block = ctx.enter_context(nc.Block())

        def rows(b):
            return bass.ds((b % 2) * T, T)

        def row(b, t):
            return bass.ds((b % 2) * T + t, 1)

        @block.sync
        def _(sp):
            def load(b, tiles):
                sp.dma_start(h[:, tiles, :], sorted_d.rearrange("(b n) d -> b n d", n=N)[bass.ds(b, 1), 0:S, :]
                             .rearrange("a (p t) d -> p (a t) d", t=T)).then_inc(x_loaded, 16)
                sp.dma_start(attn[:], state_d[bass.ds(b + STEPS - B, 1)].rearrange("a (p t) d -> p (a t) d", t=T)
                             ).then_inc(x_loaded, 16)

            load(0, slice(0, T))
            for dst, src in (
                    (enc_w[:], w["enc_w"].rearrange("(k p) n -> p k n", p=DM)),
                    (enc_b[:], w["enc_b"].rearrange("(r o) -> r o", o=1)),
                    (sw_w[:], w["sw_w"]),
                    (sw_b[:], w["sw_b"].partition_broadcast(P)),
                    (b1[:], w["eb1"].rearrange("(c a) r -> (a r) c", c=EC)),
                    (w2[:], w["ew2"].rearrange("(c a) r d -> (a r) c d", c=EC)),
                    (b2[:], w["eb2"])):
                sp.dma_start(dst, src, allow_slow_non_contiguous=True).then_inc(w_loaded, 16)
            for k in range(MT):
                sp.dma_start(w1[:, k, :, :], w["ew1"][:, k * DM:(k + 1) * DM, :].rearrange("e p r -> p e r")
                             ).then_inc(w_loaded, 16)
            with sp.Fori(0, B) as b:
                sp.wait_ge(added, b + 1)
                sp.wait_ge(bank_free, EX_JOBS * b + EX_BANKS)
                load((b + 1) % B, rows(b + 1))
                sp.wait_ge(bank_free, EX_JOBS * (b + 1) + EX_BANKS)
                sp.dma_start(out[bass.ds(b, 1), 0:LAST * T, :].rearrange("a (p t) d -> p (a t) d", t=T),
                             result[0:LAST, :, :]).then_inc(out_stored, 16)
                sp.dma_start(out[bass.ds(b, 1), LAST * T:KEEP, :], result[LAST:LAST + 1, 0:FULL, :]
                             ).then_inc(out_stored, 16)
            sp.wait_ge(out_stored, 32 * B + 1)

        @block.gpsimd
        def _(gp):
            nc.gpsimd.memset(ident[:], 0.0).then_inc(pool, 1)
            nc.gpsimd.memset(spread[:], 1.0).then_inc(pool, 1)
            for e in range(E):
                nc.gpsimd.memset(first[:, e:e + 1], float(E - e)).then_inc(consts, 1)
            nc.gpsimd.memset(minus_half[:], -0.5).then_inc(consts, 1)
            nc.gpsimd.memset(eps[:], LN_EPS).then_inc(pool, 1)
            gp.wait_ge(pool, 3)
            nc.gpsimd.affine_select(out=ident[:], in_=ident[:], compare_op=ALU.not_equal, fill=1.0, base=0,
                                    pattern=[[-1, 128]], channel_multiplier=1).then_inc(consts, 1)
            nc.gpsimd.affine_select(out=spread[:], in_=spread[:], compare_op=ALU.is_ge, fill=0.0, base=0,
                                    pattern=[[1, E * R]], channel_multiplier=-R).then_inc(pool, 1)
            gp.wait_ge(pool, 4)
            nc.gpsimd.affine_select(out=spread[:], in_=spread[:], compare_op=ALU.is_ge, fill=0.0, base=R - 1,
                                    pattern=[[-1, E * R]], channel_multiplier=R).then_inc(consts, 1)
            with gp.Fori(0, B + 1) as b:
                gp.wait_ge(moments, b + 1)
                nc.gpsimd.tensor_tensor(rstd[:], mean_var[:, :, 1], eps[:], ALU.add).then_inc(pool, 1)
                gp.wait_ge(pool, b + 5)
                nc.gpsimd.tensor_tensor(rstd[:], rstd[:], minus_half[:], ALU.pow).then_inc(rstd_ready, 1)

        @block.tensor
        def _(pe):
            def mm(out_, a, b_, start=True, stop=True):
                return nc.tensor.matmul(out_, a, b_, start=start, stop=stop)

            def take(ring):
                bank, use = ring.take()
                pe.wait_ge(bank_free, use)
                return bank

            def copied(ring):
                pe.wait_ge(bank_free, ring.before + ring.count + EX_BANKS)

            def turn_normed(ring, b):
                pe.wait_ge(normed, T * (b + 1))
                for m in range(MT):
                    for half in range(2):
                        bank = take(ring)
                        for t in range(3):
                            last = nc.tensor.transpose(job_ps[0:DM, bank, t * P:(t + 1) * P],
                                                       y[:, half * 3 + t, m * DM:(m + 1) * DM], ident[0:P, 0:P])
                        last.then_inc(bank_full, 1)

            pe.wait_ge(consts, E + 3)
            ring = Ring(EX_BANKS)
            turn_normed(ring, 0)
            pe.wait_ge(w_loaded, 16 * (7 + MT))
            with pe.Fori(0, B) as b:
                ring = Ring(EX_BANKS, b * EX_JOBS + TURN_JOBS, TURN_JOBS)
                copied(ring)
                for half in range(2):
                    bank = take(ring)
                    for k in range(MT):
                        last = mm(job_ps[0:R, bank, 0:HALF], enc_w[:, k, :], yT[:, k, half * HALF:(half + 1) * HALF],
                                  k == 0, k == 1)
                    last.then_inc(bank_full, 1)
                copied(ring)
                bank = take(ring)
                for t in range(T):
                    last = mm(job_ps[0:P, bank, t * E:(t + 1) * E], encT[:, t * P:(t + 1) * P], sw_w[:])
                last.then_inc(bank_full, 1)
                for c in range(EC):
                    for half in range(2):
                        bank = take(ring)
                        for k in range(MT):
                            last = mm(job_ps[:, bank, 0:HALF],
                                      w1[:, k, 2 * c:2 * c + 2, :].rearrange("p a r -> p (a r)"),
                                      yT[:, k, half * HALF:(half + 1) * HALF], k == 0, k == 1)
                        last.then_inc(bank_full, 1)
                pe.wait_ge(onehot_ready, b + 1)
                for half in range(2):
                    bank = take(ring)
                    for t in range(3):
                        last = nc.tensor.transpose(job_ps[0:E, bank, t * P:(t + 1) * P], onehot[:, half * 3 + t, :],
                                                   ident[0:P, 0:P])
                    last.then_inc(bank_full, 1)
                copied(ring)
                for c in range(EC):
                    for half in range(2):
                        bank = take(ring)
                        mm(job_ps[:, bank, 0:HALF], spread[:, c * 128:(c + 1) * 128],
                           onehotT[:, half * HALF:(half + 1) * HALF]).then_inc(bank_full, 1)
                copied(ring)
                for i in range(3):
                    bank = take(ring)
                    for t in (2 * i, 2 * i + 1):
                        to = job_ps[0:P, bank, (t % 2) * D:(t % 2 + 1) * D]
                        for c in range(EC):
                            mm(to, hid[:, c, t * P:(t + 1) * P], w2[:, c, :], c == 0, False)
                        last = mm(to, onehotT[:, t * P:(t + 1) * P], b2[:], False, True)
                    last.then_inc(bank_full, 1)
                turn_normed(ring, b + 1)
                assert ring.count == EX_JOBS

        @block.scalar
        def _(act):
            with act.Fori(0, B) as b:
                act.wait_ge(logits_ready, b + 1)
                nc.scalar.activation(prob[:], logit[:], ACT.Exp).then_inc(exp_done, 1)
                for i in range(2):
                    act.wait_ge(bank_free, b * EX_JOBS + TURN_JOBS + 2 + 1 + (i + 1) * EC + EX_BANKS)
                    part = hid[:, i * EC // 2:(i + 1) * EC // 2, :]
                    nc.scalar.activation(part, part, ACT.Gelu).then_inc(gelu_done, 1)

        @block.vector
        def _(dve):
            nc.vector.memset(total[:], 0.0).then_inc(bank_free, EX_BANKS)
            nc.vector.memset(top[:], 0.0).then_inc(out_stored, 1)
            dve.wait_ge(out_stored, 1)
            dve.wait_ge(bank_free, EX_BANKS)
            def link(instruction):
                dve.wait_ge(vec, done.add(instruction))

            def full(ring):
                bank, use = ring.take()
                dve.wait_ge(bank_full, use)
                return bank

            def by_expert(v):
                return v[:, :, None].broadcast_to([P, T, E])

            def add_rows(b, tiles):
                dve.wait_ge(x_loaded, 32 * (b + 1))
                nc.vector.tensor_tensor(h[:, tiles, :], h[:, tiles, :], attn[:], ALU.add).then_inc(added, 1)
                dve.wait_ge(added, b + 1)

            def row_stats(tile):
                for t in range(T):
                    done.add(nc.vector.bn_stats(stats[:, t, :], h[:, tile(t), :].rearrange("p a d -> p (a d)")))

            def row_moments():
                dve.wait_ge(vec, done.now())
                combine_stats(nc, dve, done, stats, mean_var, mean_gap, D).then_inc(moments, 1)

            def norm_rows(b, tile):
                dve.wait_ge(moments, b + 1)
                dve.wait_ge(rstd_ready, b + 1)
                for t in range(T):
                    nc.vector.tensor_scalar(y[:, t, :], h[:, tile(t), :].rearrange("p a d -> p (a d)"),
                                            mean_var[:, t, 0:1], rstd[:, t:t + 1],
                                            ALU.subtract, ALU.mult).then_inc(normed, 1)

            def copy_turned(ring):
                for m in range(MT):
                    for half in range(2):
                        bank = full(ring)
                        nc.vector.tensor_copy(yT[:, m, half * HALF:(half + 1) * HALF],
                                              job_ps[0:DM, bank, 0:HALF]).then_inc(bank_free, 1)

            done = Tally(vec)
            add_rows(0, slice(0, T))
            row_stats(lambda t: slice(t, t + 1))
            row_moments()
            norm_rows(0, lambda t: slice(t, t + 1))
            ring = Ring(EX_BANKS)
            dve.wait_ge(consts, E + 3)
            copy_turned(ring)
            assert ring.count == TURN_JOBS and done.count == EX_VEC_NORM, done.count
            dve.wait_ge(w_loaded, 16 * (7 + MT))
            with dve.Fori(0, B) as b:
                ring = Ring(EX_BANKS, b * EX_JOBS + TURN_JOBS, TURN_JOBS)
                done = Tally(vec, b * EX_VEC + EX_VEC_NORM)
                for half in range(2):
                    bank = full(ring)
                    nc.vector.tensor_scalar(encT[:, half * HALF:(half + 1) * HALF], job_ps[0:R, bank, 0:HALF],
                                            enc_b[:, 0:1], None, ALU.add).then_inc(bank_free, 1)
                bank = full(ring)
                nc.vector.tensor_tensor(logit[:], job_ps[0:P, bank, 0:T * E].rearrange("p (t e) -> p t e", e=E),
                                        sw_b[:, None, :].broadcast_to([P, T, E]), ALU.add).then_inc(bank_free, 1)
                dve.wait_ge(bank_free, ring.before + ring.count + EX_BANKS)
                link(nc.vector.tensor_reduce(top[:], logit[:], AX.X, ALU.max))
                nc.vector.tensor_tensor(logit[:], logit[:], by_expert(top), ALU.subtract).then_inc(logits_ready, 1)
                for i in range(2 * EC):
                    c, half = divmod(i, 2)
                    bank = full(ring)
                    nc.vector.tensor_scalar(hid[:, c, half * HALF:(half + 1) * HALF], job_ps[:, bank, 0:HALF],
                                            b1[:, c:c + 1], None, ALU.add).then_inc(bank_free, 1)
                    if i == 1:
                        dve.wait_ge(exp_done, b + 1)
                        link(nc.vector.tensor_reduce(total[:], prob[:], AX.X, ALU.add))
                        link(nc.vector.reciprocal(total[:], total[:]))
                        link(nc.vector.tensor_tensor(prob[:], prob[:], by_expert(total), ALU.mult))
                        link(nc.vector.tensor_reduce(prob_max[:], prob[:], AX.X, ALU.max))
                    if i == 2:
                        link(nc.vector.tensor_tensor(onehot[:], prob[:], by_expert(prob_max), ALU.is_equal))
                        link(nc.vector.tensor_tensor(onehot[:], onehot[:], first[:, None, :].broadcast_to([P, T, E]),
                                                     ALU.mult))
                        link(nc.vector.tensor_reduce(top[:], onehot[:], AX.X, ALU.max))
                        nc.vector.tensor_tensor(onehot[:], onehot[:], by_expert(top), ALU.is_equal).then_inc(onehot_ready, 1)
                for half in range(2):
                    bank = full(ring)
                    nc.vector.tensor_copy(onehotT[:, half * HALF:(half + 1) * HALF],
                                          job_ps[0:E, bank, 0:HALF]).then_inc(bank_free, 1)
                for c in range(EC):
                    if c % (EC // 2) == 0:
                        dve.wait_ge(gelu_done, 2 * b + 1 + c // (EC // 2))
                    for half in range(2):
                        bank = full(ring)
                        part = hid[:, c, half * HALF:(half + 1) * HALF]
                        nc.vector.tensor_tensor(part, part, job_ps[:, bank, 0:HALF], ALU.mult).then_inc(bank_free, 1)
                add_rows(b + 1, rows(b + 1))
                dve.wait_ge(out_stored, 32 * b + 1)
                for i in range(3):
                    bank = full(ring)
                    for t in (2 * i, 2 * i + 1):
                        summed = nc.vector.scalar_tensor_tensor(
                            out=result[:, t, :], in0=job_ps[0:P, bank, (t % 2) * D:(t % 2 + 1) * D],
                            scalar=prob_max[:, t:t + 1], in1=h[:, row(b, t), :].rearrange("p a d -> p (a d)"),
                            op0=ALU.mult, op1=ALU.add)
                        if t % 2:
                            summed.then_inc(bank_free, 1)
                        else:
                            done.add(summed)
                    if i == 0:
                        row_stats(lambda t: row(b + 1, t))
                        row_moments()
                    if i == 1:
                        norm_rows(b + 1, lambda t: row(b + 1, t))
                copy_turned(ring)
                dve.wait_ge(bank_free, ring.before + ring.count + EX_BANKS)
                assert ring.count == EX_JOBS and done.count == EX_VEC, done.count


def audio_tower(nc, w, out):
    scores_d = nc.dram_tensor("scores_scratch", (B * XT, 128), F32, kind="Internal").ap()
    sorted_d = nc.dram_tensor("sorted_scratch", (B * N, D), F32, kind="Internal").ap()
    state_d = nc.dram_tensor("state_scratch", (SLOTS, S, D), F32, kind="Internal").ap()
    parts_d = nc.dram_tensor("parts_scratch", (3, 3, D, S), BF16, kind="Internal").ap()
    sort_tokens(nc, w["x"], w["tok_w"], w["tok_b"], scores_d, sorted_d, state_d)
    layers(nc, w, parts_d, state_d)
    experts(nc, w, sorted_d, state_d, out)


_INS = {
    "x": "x", "L0_tok_w": "tok_w", "L0_tok_b": "tok_b",
    "L0_attn_Wq": "Wq", "L0_attn_bq": "bq", "L0_attn_Wk": "Wk", "L0_attn_bk": "bk", "L0_attn_Wv": "Wv",
    "L0_attn_bv": "bv", "L0_attn_Wc": "Wc", "L0_attn_bc": "bc", "L0_attn_Wo": "Wo", "L0_attn_bo": "bo",
    "L0_attn_g1": "g1", "L0_attn_b1": "b1", "L0_attn_Wi": "Wi", "L0_attn_bi": "bi", "L0_attn_Wo2": "Wo2",
    "L0_attn_bo2": "bo2", "L0_attn_g2": "g2", "L0_attn_b2": "b2",
    "L0_ffn_enc_w": "enc_w", "L0_ffn_enc_b": "enc_b", "L0_ffn_sw_w": "sw_w", "L0_ffn_sw_b": "sw_b",
    "L0_ffn_w1": "ew1", "L0_ffn_b1": "eb1", "L0_ffn_w2": "ew2", "L0_ffn_b2": "eb2",
}
_OUTS = [((B, KEEP, D), "float32")]


def kernel(**inputs):
    import numpy as _np
    import concourse.bacc as _bacc
    from concourse import mybir as _mybir
    from concourse.bass_utils import run_bass_kernel_spmd as _run

    nc = _bacc.Bacc("TRN2", target_bir_lowering=False, num_devices=1)
    arrays, args = {}, {}
    for name, short in _INS.items():
        a = _np.ascontiguousarray(inputs[name])
        arrays[f"in_{name}_dram"] = a
        args[short] = nc.dram_tensor(f"in_{name}_dram", a.shape, _mybir.dt.from_np(a.dtype), kind="ExternalInput").ap()
    shape, dtype = _OUTS[0]
    out = nc.dram_tensor("out_0_dram", shape, _mybir.dt.from_np(_np.dtype(dtype)), kind="ExternalOutput").ap()
    audio_tower(nc, args, out)
    r = _run(nc, [arrays], core_ids=[0])
    return r.results[0]["out_0_dram"]
```
